# Optimizing a Trainium2 kernel written in Bass

```python
import numpy as np
import jax
import jax.numpy as jnp

def _softmax(x, axis=-1):
    return jax.nn.softmax(x, axis=axis)

def _gelu(x):
    return jax.nn.gelu(x, approximate=True)

def _silu(x):
    return jax.nn.silu(x)

def _sigmoid(x):
    return jax.nn.sigmoid(x)

def _layernorm(x, axis=-1, eps=1e-05):
    m = jnp.mean(x, axis=axis, keepdims=True)
    v = jnp.var(x, axis=axis, keepdims=True)
    return (x - m) / jnp.sqrt(v + eps)

def _scatter_add(tgt, idx, src, axis=0):
    return tgt.at[idx].add(src)

def _segment_sum(src, seg, n):
    return jax.ops.segment_sum(src, seg, n)
kernel_name = 'mk_decoder_preln_d1_seqx_r2_2489bd'

def setup_inputs(seed: int=0):
    np.random.seed(seed)
    _w = jnp.asarray

    def _rec_inputs():
        import jax
        import jax.numpy as jnp
        _rk = jax.random.key(seed)
        x = 0.002226 + 0.9996 * jax.random.normal(jax.random.fold_in(_rk, 1), (8, 100, 512), jnp.float32)
        _lenS = 100 - jax.random.randint(jax.random.fold_in(_rk, 7), (8,), 0, max(1, 100 // 4) + 1, jnp.int32)
        _lenS2 = 722 - jax.random.randint(jax.random.fold_in(_rk, 8), (8,), 0, max(1, 722 // 4) + 1, jnp.int32)
        _ctx_1024P = jax.random.normal(jax.random.fold_in(_rk, 11), (8, 16, 512), jnp.float32)
        _ctx_1024c = jax.random.dirichlet(jax.random.fold_in(_rk, 511), 0.3 * jnp.ones((16,), jnp.float32), (8, 722))
        _ctx_1024t = jnp.einsum('bsk,bkd->bsd', _ctx_1024c, _ctx_1024P)
        _ctx_1024t = _ctx_1024t * jax.lax.rsqrt(jnp.mean(jnp.square(_ctx_1024t)) + 1e-12) * 0.953939
        ctx_1024 = -0.000125008 + 0.999885 * (_ctx_1024t + 0.3 * jax.random.normal(jax.random.fold_in(_rk, 611), (8, 722, 512), jnp.float32))
        return (x, ctx_1024)
    x, ctx_1024 = _rec_inputs()

    def _L0_attn_setup():
        import jax, jax.numpy as jnp
        import numpy as np
        B, T, D = (8, 2048, 512)

        def _rg_lru(x, Wi, bi, Wg, bg, Wo, bo):
            u = jnp.einsum('btd,ed->bte', x, Wi) + bi
            g = jax.nn.sigmoid(jnp.einsum('btd,ed->bte', x, Wg) + bg)

            def step(h, gu):
                g_t, u_t = gu
                h = g_t * h + (1.0 - g_t) * u_t
                return (h, h)
            h0 = jnp.zeros((x.shape[0], x.shape[2]), dtype=u.dtype)
            _, h = jax.lax.scan(step, h0, (jnp.swapaxes(g, 0, 1), jnp.swapaxes(u, 0, 1)))
            h = jnp.swapaxes(h, 0, 1)
            return jnp.einsum('btd,ed->bte', h, Wo) + bo
        key = jax.random.key(seed)
        ks = jax.random.split(key, 7)
        s = 1.0 / np.sqrt(D)
        return {'x': jax.random.normal(ks[0], (B, T, D), dtype=jnp.float32), 'Wi': jax.random.uniform(ks[1], (D, D), jnp.float32, -s, s), 'bi': jax.random.uniform(ks[2], (D,), jnp.float32, -s, s), 'Wg': jax.random.uniform(ks[3], (D, D), jnp.float32, -s, s), 'bg': jax.random.uniform(ks[4], (D,), jnp.float32, -s, s), 'Wo': jax.random.uniform(ks[5], (D, D), jnp.float32, -s, s), 'bo': jax.random.uniform(ks[6], (D,), jnp.float32, -s, s)}
    _L0_attn_all = _L0_attn_setup()
    _L0_attn_in = {k: v for k, v in _L0_attn_all.items() if k in ('Wi', 'bi', 'Wg', 'bg', 'Wo', 'bo')}
    del _L0_attn_all

    def _L0_xattn_setup():
        import jax, jax.numpy as jnp
        import numpy as np
        B, M, N, DIM, DH, H = (8, 2048, 64, 512, 128, 8)
        INNER = DH * H
        EPS = 1e-05

        def _layernorm(x, g, b):
            mu = jnp.mean(x, axis=-1, keepdims=True)
            var = jnp.var(x, axis=-1, keepdims=True)
            return (x - mu) * jax.lax.rsqrt(var + EPS) * g + b
        key = jax.random.key(seed)
        ks = jax.random.split(key, 8)
        sd = 0.02
        return {'x': jax.random.normal(ks[0], (B, M, DIM), jnp.float32), 'latents': jax.random.normal(ks[1], (B, N, DIM), jnp.float32), 'gamma_media': jnp.ones((DIM,), jnp.float32), 'beta_media': jnp.zeros((DIM,), jnp.float32), 'gamma_lat': jnp.ones((DIM,), jnp.float32), 'beta_lat': jnp.zeros((DIM,), jnp.float32), 'Wq': jax.random.normal(ks[2], (DIM, INNER), jnp.float32) * sd, 'bq': jnp.zeros((INNER,), jnp.float32), 'Wkv': jax.random.normal(ks[3], (DIM, 2 * INNER), jnp.float32) * sd, 'bkv': jnp.zeros((2 * INNER,), jnp.float32), 'Wo': jax.random.normal(ks[4], (INNER, DIM), jnp.float32) * sd, 'bo': jnp.zeros((DIM,), jnp.float32)}
    _L0_xattn_all = _L0_xattn_setup()
    _L0_xattn_in = {k: v for k, v in _L0_xattn_all.items() if k in ('gamma_media', 'beta_media', 'gamma_lat', 'beta_lat', 'Wq', 'bq', 'Wkv', 'bkv', 'Wo', 'bo')}
    del _L0_xattn_all

    def _L0_ffn_setup():
        import jax, jax.numpy as jnp
        import numpy as np
        B, S, H, FFN, E = (2, 1024, 512, 2048, 8)
        key = jax.random.key(seed)
        k0, k1, k2, k3 = jax.random.split(key, 4)
        return {'hidden_states': jax.random.normal(k0, (B, S, H), dtype=jnp.float32), 'Wr': jax.random.normal(k1, (H, E), dtype=jnp.float32) * 0.02, 'br': jnp.zeros((E,), dtype=jnp.float32), 'W1': jax.random.normal(k2, (E, H, FFN), dtype=jnp.float32) * 0.02, 'W2': jax.random.normal(k3, (E, FFN, H), dtype=jnp.float32) * 0.02}
    _L0_ffn_all = _L0_ffn_setup()
    _L0_ffn_in = {k: v for k, v in _L0_ffn_all.items() if k in ('Wr', 'br', 'W1', 'W2')}
    del _L0_ffn_all
    return {'x': x, 'ctx_1024': ctx_1024, 'L0_attn_Wi': _L0_attn_in['Wi'], 'L0_attn_bi': _L0_attn_in['bi'], 'L0_attn_Wg': _L0_attn_in['Wg'], 'L0_attn_bg': _L0_attn_in['bg'], 'L0_attn_Wo': _L0_attn_in['Wo'], 'L0_attn_bo': _L0_attn_in['bo'], 'L0_xattn_gamma_media': _L0_xattn_in['gamma_media'], 'L0_xattn_beta_media': _L0_xattn_in['beta_media'], 'L0_xattn_gamma_lat': _L0_xattn_in['gamma_lat'], 'L0_xattn_beta_lat': _L0_xattn_in['beta_lat'], 'L0_xattn_Wq': _L0_xattn_in['Wq'], 'L0_xattn_bq': _L0_xattn_in['bq'], 'L0_xattn_Wkv': _L0_xattn_in['Wkv'], 'L0_xattn_bkv': _L0_xattn_in['bkv'], 'L0_xattn_Wo': _L0_xattn_in['Wo'], 'L0_xattn_bo': _L0_xattn_in['bo'], 'L0_ffn_Wr': _L0_ffn_in['Wr'], 'L0_ffn_br': _L0_ffn_in['br'], 'L0_ffn_W1': _L0_ffn_in['W1'], 'L0_ffn_W2': _L0_ffn_in['W2']}

def reference(x, ctx_1024, L0_attn_Wi, L0_attn_bi, L0_attn_Wg, L0_attn_bg, L0_attn_Wo, L0_attn_bo, L0_xattn_gamma_media, L0_xattn_beta_media, L0_xattn_gamma_lat, L0_xattn_beta_lat, L0_xattn_Wq, L0_xattn_bq, L0_xattn_Wkv, L0_xattn_bkv, L0_xattn_Wo, L0_xattn_bo, L0_ffn_Wr, L0_ffn_br, L0_ffn_W1, L0_ffn_W2):
    import jax
    import jax.numpy as jnp

    def _L0_attn_ref(x, Wi, bi, Wg, bg, Wo, bo):
        import jax, jax.numpy as jnp
        import numpy as np
        B, T, D = (8, 2048, 512)

        def _rg_lru(x, Wi, bi, Wg, bg, Wo, bo):
            u = jnp.einsum('btd,ed->bte', x, Wi) + bi
            g = jax.nn.sigmoid(jnp.einsum('btd,ed->bte', x, Wg) + bg)

            def step(h, gu):
                g_t, u_t = gu
                h = g_t * h + (1.0 - g_t) * u_t
                return (h, h)
            h0 = jnp.zeros((x.shape[0], x.shape[2]), dtype=u.dtype)
            _, h = jax.lax.scan(step, h0, (jnp.swapaxes(g, 0, 1), jnp.swapaxes(u, 0, 1)))
            h = jnp.swapaxes(h, 0, 1)
            return jnp.einsum('btd,ed->bte', h, Wo) + bo
        return _rg_lru(x, Wi, bi, Wg, bg, Wo, bo)

    def _L0_xattn_ref(x, latents, gamma_media, beta_media, gamma_lat, beta_lat, Wq, bq, Wkv, bkv, Wo, bo):
        import jax, jax.numpy as jnp
        import numpy as np
        B, M, N, DIM, DH, H = (8, 2048, 64, 512, 128, 8)
        INNER = DH * H
        EPS = 1e-05

        def _layernorm(x, g, b):
            mu = jnp.mean(x, axis=-1, keepdims=True)
            var = jnp.var(x, axis=-1, keepdims=True)
            return (x - mu) * jax.lax.rsqrt(var + EPS) * g + b
        b = x.shape[0]
        xn = _layernorm(x, gamma_media, beta_media)
        ln = _layernorm(latents, gamma_lat, beta_lat)
        q = ln @ Wq + bq
        kv_input = jnp.concatenate([xn, ln], axis=1)
        kv = kv_input @ Wkv + bkv
        k, v = jnp.split(kv, 2, axis=-1)

        def to_heads(t):
            return t.reshape(b, t.shape[1], H, DH).transpose(0, 2, 1, 3)
        q, k, v = (to_heads(q), to_heads(k), to_heads(v))
        q = q * DH ** (-0.5)
        sim = jnp.einsum('bhid,bhjd->bhij', q, k)
        attn = jax.nn.softmax(sim, axis=-1)
        out = jnp.einsum('bhij,bhjd->bhid', attn, v)
        out = out.transpose(0, 2, 1, 3).reshape(b, -1, INNER)
        return out @ Wo + bo

    def _L0_ffn_ref(hidden_states, Wr, br, W1, W2):
        import jax, jax.numpy as jnp
        import numpy as np
        B, S, H, FFN, E = (2, 1024, 512, 2048, 8)
        b, s, h = hidden_states.shape
        x = hidden_states.reshape(-1, h)
        route = jax.nn.sigmoid(x @ Wr + br)
        max_prob = jnp.max(route, axis=1, keepdims=True)
        max_ind = jnp.argmax(route, axis=1)
        out = jnp.zeros_like(x)
        n_experts = Wr.shape[1]
        for e in range(n_experts):
            mask = (max_ind == e)[:, None].astype(x.dtype)
            y = jax.nn.gelu(x @ W1[e], approximate=False) @ W2[e]
            out = out + mask * y
        out = out * max_prob
        return out.reshape(b, s, h)
    x = x + _L0_attn_ref(_layernorm(x, axis=-1), L0_attn_Wi, L0_attn_bi, L0_attn_Wg, L0_attn_bg, L0_attn_Wo, L0_attn_bo)
    x = x + _L0_xattn_ref(ctx_1024, _layernorm(x, axis=-1), L0_xattn_gamma_media, L0_xattn_beta_media, L0_xattn_gamma_lat, L0_xattn_beta_lat, L0_xattn_Wq, L0_xattn_bq, L0_xattn_Wkv, L0_xattn_bkv, L0_xattn_Wo, L0_xattn_bo)
    x = x + _L0_ffn_ref(_layernorm(x, axis=-1), L0_ffn_Wr, L0_ffn_br, L0_ffn_W1, L0_ffn_W2)
    return x

_drawn_inputs = setup_inputs


def setup_inputs(seed=0):
    import zlib

    import numpy as np

    out = dict(_drawn_inputs(seed))
    spreads = {'L0_xattn_gamma_media': (1.0, 0.2),
     'L0_xattn_beta_media': (0.0, 0.1),
     'L0_xattn_gamma_lat': (1.0, 0.6),
     'L0_xattn_beta_lat': (0.0, 0.523),
     'L0_xattn_bq': (0.0, 0.8),
     'L0_xattn_bkv': (0.0, 0.1),
     'L0_xattn_bo': (0.0, 0.1),
     'L0_ffn_br': (0.0, 0.1)}
    factors = {'L0_attn_bg': 7.497, 'L0_xattn_Wq': 2.812, 'L0_attn_bi': 3.016}
    for name, (base, spread) in spreads.items():
        noise = np.random.default_rng([zlib.crc32(name.encode()), seed]).standard_normal(out[name].shape)
        drawn = base * np.exp(spread * noise) if base else spread * noise
        out[name] = jnp.asarray(drawn.astype(out[name].dtype))
    for name, factor in factors.items():
        out[name] = (out[name] * factor).astype(out[name].dtype)
    return out
```

```python
from contextlib import ExitStack

import numpy as np

import concourse.bass as bass
from concourse import mybir
from concourse.alu_op_type import AluOpType as ALU

F32 = mybir.dt.float32
F32R = mybir.dt.float32r
I32 = mybir.dt.int32
ACT = mybir.ActivationFunctionType
AX = mybir.AxisListType.X

B, T, D = 8, 100, 512
MEDIA = 722
HEADS, DH = 8, 128
INNER = HEADS * DH
FFN, E = 2048, 8
P = 128
ND = D // P
NTOK = B * T
EPS = 1e-5

HALF = 4
HT = HALF * T

MC = -(-MEDIA // P)
KC = MC + 1
MLAST = MEDIA - (MC - 1) * P
KEYS = MEDIA + T
KPAD = KC * P
SH = [412, KEYS - 412]
ROWS = HEADS * T
RT = -(-ROWS // P)
RLAST = ROWS - (RT - 1) * P
GROUPS = [[0, 1], [2, 3], [4, 5, 6]]
GW = 2 * P + RLAST

TILE = 128
NOV = NTOK // TILE
NSLOT = E + NOV + 1
N_CA, N_WB, N_CC = 14, 6, 7
POOL_B, DVE_B = 4 + 2 * MC, 56
FC = 512
NF = FFN // FC
NREC = 2 + E


def rows_of(tile):
    return RLAST if tile == RT - 1 else P


def segments(group):
    lo = group[0] * P
    hi = min(ROWS, (group[-1] + 1) * P)
    out = []
    while lo < hi:
        end = min(hi, (lo // T + 1) * T)
        out.append((lo // T, lo, end))
        lo = end
    return out


class Chain:

    def __init__(self, eng, sem):
        self.eng, self.sem, self.n, self.turn, self.per = eng, sem, 0, None, 0

    def add(self, ins):
        ins.then_inc(self.sem, 1)
        self.n += 1
        return ins

    def join(self):
        v = self.n if self.turn is None else self.turn * self.per + self.n
        self.eng.wait_ge(self.sem, v)

    def enter(self, turn, per):
        self.turn, self.per, self.start = turn, per, self.n

    def leave(self, turns):
        assert self.n - self.start == self.per, (self.n - self.start, self.per)
        self.n = self.start + turns * self.per
        self.turn = None


class Ring:

    def __init__(self, banks, read, begin):
        self.banks, self.read, self.begin, self.n, self.turn, self.per = banks, read, begin, 0, 0, 0

    def at(self, turn, per, first):
        assert per % 2 == 0
        self.turn, self.per, self.n = turn, per, first

    def take(self):
        k = self.n % 2
        self.n += 1
        return self.banks[k], self.read[k], self.turn * self.per + self.n

    def free(self, eng):
        v = self.turn * (self.per // 2) + self.n // 2 + self.begin
        if not isinstance(v, int) or v > 0:
            eng.wait_ge(self.read[self.n % 2], v)

    def all_read(self, eng):
        for k in range(2):
            eng.wait_ge(self.read[k], self.turn * (self.per // 2) + (self.n + 1 - k) // 2 + self.begin)


class Memory:

    def __init__(self, nc):
        self.nc = nc
        self.at = -(-nc.sbuf_base // 64) * 64
        self.end = nc.sbuf_usable_end

    def __call__(self, name, shape, dtype=F32):
        size = int(np.prod(shape[1:])) * 4
        t = self.nc.alloc_sbuf_tensor_at(name, shape, dtype, offset=self.at)
        self.at += -(-size // 64) * 64
        assert self.at <= self.end, (name, self.at, self.end)
        return t


def build(nc, a, out):
    mem = Memory(nc)
    ctx = ExitStack()

    def sem(name):
        return ctx.enter_context(nc.semaphore(name))

    bank = [ctx.enter_context(nc.psum_tensor(f"bank{k}", [P, 512], F32)) for k in range(8)]

    def dram(name, shape, dtype=F32):
        return nc.dram_tensor(name, shape, dtype, kind="Internal").ap()
    d_ln = dram("scr_latents", (B, T, D))
    d_x1 = dram("scr_x1", (B, T, D))
    d_q = dram("scr_q", (B, P, ROWS))
    d_c = dram("scr_c", (B, ROWS))
    d_tok = dram("scr_tokens", (NTOK + 1, D))

    ident = mem("ident", [P, P])
    phalf = mem("phalf", [P, 16])
    gm = mem("gm", [P, D])
    bm = mem("bm", [P, D])
    bv = mem("bv", [P, HEADS])
    bk = mem("bk", [P, HEADS])
    wr = mem("wr", [P, ND, E])
    raw = mem("raw", [P, KC, D])
    mvr = mem("mvr", [P, MC, 2])
    rsr = mem("rsr", [P, MC])
    brb = mem("brb", [P, E])
    rec = mem("rec", [P, B + 1, NREC])
    str_ = mem("str_", [P, MC, 6])
    base = mem.at

    wk = mem("wk", [P, HEADS, D])
    wv = mem("wv", [P, ND, INNER])
    wo = mem("wo", [P, HEADS, D])
    base_b = mem.at
    xn_h = mem("xn_h", [P, KC, D], F32R)
    xn_l = mem("xn_l", [P, KC, D], F32R)
    xt_h = mem("xt_h", [P, ND, KEYS + 2], F32R)
    xt_l = mem("xt_l", [P, ND, KEYS + 2], F32R)
    qt_h = mem("qt_h", [P, ND, RT * P], F32R)
    qt_l = mem("qt_l", [P, ND, RT * P], F32R)
    pr = [mem(f"pr{k}", [P, KPAD]) for k in range(3)]
    pt_h = mem("pt_h", [P, KC, GW], F32R)
    pt_l = mem("pt_l", [P, KC, GW], F32R)
    zt = mem("zt", [P, ND, GW])
    qb = mem("qb", [P, ROWS])
    ot = mem("ot", [P, ROWS])
    x1b = mem("x1b", [P, D])
    x2b = mem("x2b", [P, D])
    x3b = mem("x3b", [P, D])
    x3t = mem("x3t", [P, ND, T])
    cqn = mem("cqn", [P, RT])
    cq = mem("cq", [P, RT])
    stx = mem("stx", [P, 6])
    rbuf = mem("rbuf", [P, NREC])
    mvx = mem("mvx", [P, 2])
    rsx = mem("rsx", [P, 2])
    smx = mem("smx", [P, 6])
    rsm = mem("rsm", [P, 8])

    mem.at = base_b
    w3 = [mem(f"w3_{k}", [P, ND, D]) for k in range(3)]
    wq = mem("wq", [P, ND, INNER])
    xin = mem("xin", [P, B, D])
    xh = mem("xh", [P, B, D])
    xt = mem("xt", [P, ND, NTOK])
    qa = mem("qa", [P, HEADS, HALF, T])
    mem.at -= HEADS * HALF * T * 4
    ug = [mem(f"ug{k}", [P, NTOK]) for k in range(2)]
    gg = [mem(f"gg{k}", [P, NTOK]) for k in range(2)]
    og = mem("og", [P, NTOK])
    hs = mem("hs", [P, ND, NTOK])
    mem.at -= ND * NTOK * 4
    crow = mem("crow", [P, HEADS, HALF, T])
    ab = mem("ab", [P, 2, ND])
    bq = mem("bq", [P, HEADS])
    gl = mem("gl", [P, D])
    bl = mem("bl", [P, D])
    boa = mem("boa", [P, D])
    box = mem("box", [P, D])
    sta = mem("sta", [P, B, 6])
    mva = mem("mva", [P, B, 2])
    rsa = mem("rsa", [P, B])

    mem.at = base
    stage = [mem(f"stage{k}", [P, 4, FC]) for k in range(4)]
    wsh = [mem(f"wsh{k}", [P, 4, FC], F32R) for k in range(4)]
    wsl = [mem(f"wsl{k}", [P, 4, FC], F32R) for k in range(4)]
    gat = mem("gat", [P, D])
    x3g = mem("x3g", [P, D])
    x2g = mem("x2g", [P, D])
    cur = mem("cur", [P, 4])
    pg = mem("pg", [P, 1])
    xg_h = mem("xg_h", [P, ND, TILE], F32R)
    xg_l = mem("xg_l", [P, ND, TILE], F32R)
    hid = [mem(f"hid{k}", [P, FC]) for k in range(2)]
    ht_h = [mem(f"ht_h{k}", [P, 4, TILE], F32R) for k in range(2)]
    ht_l = [mem(f"ht_l{k}", [P, 4, TILE], F32R) for k in range(2)]
    yo = mem("yo", [P, D])
    idx = mem("idx", [P, NSLOT], I32)
    sm = mem("sm", [P, NSLOT, 4])
    idc = mem("idc", [P, 2], I32)
    ctl = mem("ctl", [P, 8], I32)
    lmx = mem("lmx", [P, B])
    eq = mem("eq", [P, B, E])
    desc = mem("desc", [P, B, E])
    kmx = mem("kmx", [P, B])
    oh = mem("oh", [P, B, E])
    tmp = mem("tmp", [P, B, E])
    rank = mem("rank", [P, B])
    pin = mem("pin", [P, B])
    jt = mem("jt", [P, B])
    pa = mem("pa", [P, B])
    pb = mem("pb", [P, B])
    eid = mem("eid", [P, B, E])
    cnt = mem("cnt", [P, E])
    cmr = mem("cmr", [P, NOV, B])
    cmp_ = mem("cmp_", [P, NOV, E])
    ovc = mem("ovc", [P, E])
    ove = mem("ove", [P, E])
    ovb = mem("ovb", [P, E])
    ones8 = mem("ones8", [P, E])
    ek = mem("ek", [P, 8])
    vals = mem("vals", [P, B, 4])
    tokv = mem("tokv", [P, B])
    iota = mem("iota", [P, P])
    ohp = mem("ohp", [P, B, P])
    ohs = mem("ohs", [P, B, NSLOT])
    ohv = mem("ohv", [P, B, 4, NSLOT])
    upper = mem("upper", [P, P])
    ones = mem("ones", [P, P])

    s_x = [sem(f"s_xin{b}") for b in range(B)]
    s_ca, s_wq, s_wb, s_cc, s_zero, s_zout = (
        sem("s_ca"), sem("s_wq"), sem("s_wb"), sem("s_cc"), sem("s_zero"), sem("s_zout"))
    s_dve, s_act, s_pool = sem("s_dve"), sem("s_act"), sem("s_pool")
    s_mva, s_rsa, s_xha, s_tpa, s_tea = sem("s_mva"), sem("s_rsa"), sem("s_xha"), sem("s_tpa"), sem("s_tea")
    s_ugp, s_ugs, s_hsc, s_xr = sem("s_ugp"), sem("s_ugs"), sem("s_hsc"), sem("s_xr")
    s_op, s_x1, s_lnh, s_lnr, s_x1r = sem("s_op"), sem("s_x1"), sem("s_lnh"), sem("s_lnr"), sem("s_x1r")
    s_tpl, s_tel, s_qp, s_qe, s_out_a = sem("s_tpl"), sem("s_tel"), sem("s_qp"), sem("s_qe"), sem("s_out_a")
    s_qout = [sem("s_qout0"), sem("s_qout1")]
    s_apart = sem("s_apart")
    s_padb, s_rawz, s_lat = sem("s_padb"), sem("s_rawz"), sem("s_lat")
    s_cp, s_ce, s_cout = sem("s_cp"), sem("s_ce"), sem("s_cout")
    s_raw, s_rawfree, s_mvr, s_rsr, s_apr, s_ln = (sem(n) for n in (
        "s_raw", "s_rawfree", "s_mvr", "s_rsr", "s_apr", "s_ln"))
    s_qb, s_qbfree, s_x1l, s_x1free, s_x2, s_x2out, s_cq, s_cqfree = (sem(n) for n in (
        "s_qb", "s_qbfree", "s_x1l", "s_x1free", "s_x2", "s_x2out", "s_cq", "s_cqfree"))
    s_tb, s_zb = sem("s_tb"), sem("s_zb")
    s_tread, s_zread = [sem("s_tread0"), sem("s_tread1")], [sem("s_zread0"), sem("s_zread1")]
    s_hi, s_xnh, s_xnl, s_s, s_nb, s_exp, s_p, s_qp2, s_qread = (sem(n) for n in (
        "s_hi", "s_xnh", "s_xnl", "s_s", "s_nb", "s_exp", "s_p", "s_qp2", "s_qread"))
    s_mvx, s_rsx, s_x3, s_x3t, s_lp = (sem(n) for n in ("s_mvx", "s_rsx", "s_x3", "s_x3t", "s_lp"))
    s_lm, s_gate, s_oh, s_rk, s_ohv, s_tp, s_idx, s_ctl = (sem(n) for n in (
        "s_lm", "s_gate", "s_oh", "s_rk", "s_ohv", "s_tp", "s_idx", "s_ctl"))
    s_w = [sem(f"s_w{k}") for k in range(4)]
    s_wh, s_wl = sem("s_wh"), sem("s_wl")
    s_gat, s_gfree, s_x3g, s_xtp, s_xth, s_xtl = (sem(n) for n in (
        "s_gat", "s_gfree", "s_x3g", "s_xtp", "s_xth", "s_xtl"))
    s_hp, s_gelu, s_htp, s_hth, s_htl, s_yp, s_yo, s_out, s_yofree = (sem(n) for n in (
        "s_hp", "s_gelu", "s_htp", "s_hth", "s_htl", "s_yp", "s_yo", "s_out", "s_yofree"))

    def bc(vec, n, parts=P):
        return vec.rearrange("(o n) -> o n", o=1).broadcast_to([parts, n])

    plan = [("PT", 0), ("PT", 1), ("S", 2), ("R", 0), ("Z", (0, 0)), ("Z", (0, 1)), ("N", 2), ("L+", 0), ("S", 3),
            ("Z", (0, 2)), ("N", 3), ("Z", (0, 3)), ("PT", 2), ("V", 0), ("PT", 3), ("S", 4), ("R", 1),
            ("Z", (1, 0)), ("Z", (1, 1)), ("N", 4), ("L+", 1), ("S", 5), ("R", 2), ("Z", (1, 2)), ("R", 3), ("N", 5),
            ("S", 6), ("Z", (1, 3)), ("N", 6), ("PT", 4), ("V", 1), ("PT", 5), ("T+", 0), ("PT", 6), ("T+", 1),
            ("Z", (2, 0)), ("T+", 2), ("T+", 3), ("Q+", 0), ("Z", (2, 1)), ("Q+", 1), ("T+", 4), ("T+", 5), ("Q+", 2),
            ("Z", (2, 2)), ("Q+", 3), ("T+", 6), ("Q+", 4), ("Q+", 5), ("Z", (2, 3)), ("Q+", 6), ("Q+", 7),
            ("V", 2), ("S+", 0), ("X+", 0), ("X+", 1), ("N+", 0), ("S+", 1), ("X+", 2), ("X+", 3), ("N+", 1), ("Y", 0),
            ("X+", 4), ("X+", 5), ("X+", 6)]
    first = [(what[:-1], k) for what, k in plan if what[-1] == "+" and what != "L+"]
    TB0, HI0 = KC, KC + 2 * ND
    TB_USES = KC + 2 * RT + 1
    ZB_USES = 3 * (ND + 1) + 1
    HI_USES = KC + 2 * ND + 2 * RT
    qbank = [bank[2], bank[3], bank[0], bank[1]]
    s_pair = [(bank[0], bank[1]), (bank[2], bank[3])]
    tbank, zbank = (bank[4], bank[5]), (bank[6], bank[7])

    def rings():
        return Ring(tbank, s_tread, 0), Ring(zbank, s_zread, 1)

    def batches(eng, body, chain=None, per=0):
        with eng.Fori(0, B - 1) as b:
            if chain:
                chain.enter(b, per)
            body(b, plan)
            if chain:
                chain.leave(B - 1)
        body(B - 1, [e for e in plan if e[0][-1] != "+"])

    def steps(run, b, events):
        for what, k in events:
            if what[-1] == "+":
                run(b + 1, [(what[:-1], k)])
            else:
                run(b, [(what, k)])

    def tcols(c):
        return (c * P, min(P, MEDIA - c * P)) if c < MC else (MEDIA, T)

    slot_plan = [("M", 0), ("W", 0), ("M", 1), ("H", 0), ("W", 1), ("M", 2), ("H", 1), ("W", 2), ("O", 0), ("W", 3),
                 ("M", 3), ("H", 2), ("W", 4), ("O", 1), ("H", 3), ("W", 5), ("O", 2), ("G", 1), ("X", 1), ("W", 6),
                 ("O", 3), ("R", 0), ("K", 1), ("W", 7)]
    pieces = [(1, 0), (1, 1), (1, 2), (2, 0), (1, 3), (2, 1), (2, 2), (2, 3)]
    piece_of = {p: n for n, p in enumerate(pieces)}
    NW = len(pieces)

    def slots(eng, body, chain=None, per=0):
        with eng.Fori(0, E - 1) as n:
            if chain:
                chain.enter(n, per)
            body(n, None)
            if chain:
                chain.leave(E - 1)
        eng.wait_ge(s_ctl, 1)
        n_ov = eng.value_load(ctl[0:1, 7:8], min_val=0, max_val=NOV)
        body(E - 1, 0 < n_ov)
        with eng.Fori(0, NOV) as k:
            with eng.If(k < n_ov):
                if chain:
                    chain.enter(k, per)
                body(k + E, k + 1 < n_ov)
                if chain:
                    chain.leave(NOV)
        return n_ov

    def only_if(eng, cond):
        return ExitStack() if cond is None else eng.If(cond)

    def w_src(which, e, f):
        if which == 1:
            return a["W1"][e].rearrange("(k p) f -> p k f", p=P)[:, :, f * FC:(f + 1) * FC]
        return a["W2"][e, f * FC:(f + 1) * FC, :].rearrange("(k p) n -> p k n", p=P)

    def split_products(pe, dest, pairs, start, stop):
        n = len(pairs)
        for k, ((lh, ll), (rh, rl)) in enumerate(pairs):
            pe.matmul(dest, lh, rh, start=start and k == 0, stop=False)
            pe.matmul(dest, lh, rl, start=False, stop=False)
            last = pe.matmul(dest, ll, rh, start=False, stop=stop and k == n - 1)
        return last

    with ctx:
        block = ctx.enter_context(nc.Block())

        @block.sync
        def _(sp):
            for b in range(B):
                sp.dma_start(xin[0:T, b, :], a["x"][b]).then_inc(s_x[b], 16)
                if b == 1:
                    loads_a = [(ident[:], a["ident"]), (phalf[:], a["phalf"]), (boa[:], bc(a["bo_a"], D)),
                               (ab[:], a["ab"]),
                               (w3[0][:], a["WiT"].rearrange("(c p) n -> p c n", p=P)),
                               (w3[1][:], a["WgT"].rearrange("(c p) n -> p c n", p=P)),
                               (w3[2][:], a["WoT"].rearrange("(c p) n -> p c n", p=P)),
                               (bq[:], a["bq"]),
                               (gl[:], bc(a["gl"], D)), (bl[:], bc(a["bl"], D)), (box[:], bc(a["bo_x"], D)),
                               (gm[:], bc(a["gm"], D)), (bm[:], bc(a["bm"], D)), (bk[:], a["bk"])]
                    for dst, src in loads_a:
                        sp.dma_start(dst, src).then_inc(s_ca, 16)
                    assert len(loads_a) == N_CA
            sp.dma_start(wq[:], a["Wq"].rearrange("(c p) n -> p c n", p=P)).then_inc(s_wq, 16)
            loads_b = [(wk[:], a["WkT"].rearrange("(h p) d -> p h d", p=P)),
                       (wv[:], a["Wv"].rearrange("(c p) n -> p c n", p=P)),
                       (wo[:], a["Wo_x"].rearrange("(h p) n -> p h n", p=P)),
                       (bv[:], a["bv"]), (wr[:], a["Wr"].rearrange("(c p) e -> p c e", p=P))]
            for dst, src in loads_b:
                sp.dma_start(dst, src).then_inc(s_wb, 16)
            assert len(loads_b) + 1 == N_WB

            def load_context(b, turn):
                sp.dma_start(raw[:, 0:MC - 1, :], a["ctx"][b, 0:(MC - 1) * P, :].rearrange("(c p) d -> p c d", p=P)
                             ).then_inc(s_raw, 16)
                sp.dma_start(raw[0:MLAST, MC - 1, :], a["ctx"][b, (MC - 1) * P:MEDIA, :]).then_inc(s_raw, 16)

            sp.wait_ge(s_rawz, 1)
            load_context(0, 0)
            for half in range(2):
                for bb in range(HALF):
                    b = half * HALF + bb
                    sp.wait_ge(s_x1r, b + 1)
                    sp.dma_start(d_x1[b], xin[0:T, b, :]).then_inc(s_out_a, 16)
                    sp.wait_ge(s_lnr, b + 1)
                    sp.dma_start(d_ln[b], xh[0:T, b, :]).then_inc(s_out_a, 16)
                sp.wait_ge(s_qe, HEADS * (half + 1))
                for bb in range(HALF):
                    sp.dma_start(d_q[half * HALF + bb].rearrange("p (h t) -> p h t", h=HEADS), qa[:, :, bb, :]
                                 ).then_inc(s_qout[half], 16)
                sp.wait_ge(s_ce, HEADS * (half + 1))
                for bb in range(HALF):
                    b = half * HALF + bb
                    sp.dma_start(d_c[b:b + 1, :].rearrange("o (h t) -> o h t", h=HEADS), crow[0:1, :, bb, :]
                                 ).then_inc(s_cout, 16)
            sp.wait_ge(s_out_a, 16 * 2 * B)
            sp.wait_ge(s_qout[0], 16 * HALF)
            sp.wait_ge(s_qout[1], 16 * HALF)

            sp.wait_ge(s_cout, 16 * B)
            sp.dma_start(brb[:], bc(a["br"], E)).then_inc(s_wb, 16)
            sp.wait_ge(s_zero, 1)
            sp.dma_start(d_tok[NTOK:NTOK + 1, :], x2b[0:1, :]).then_inc(s_zout, 16)
            sp.wait_ge(s_padb, 1)

            def load_queries(b):
                sp.dma_start(qb[:], d_q[b]).then_inc(s_qb, 16)

            def load_bias_rows(b):
                m = (RT - 1) * P
                sp.dma_start(cqn[:, 0:RT - 1], d_c[b, 0:m].rearrange("(i p) -> p i", p=P),
                             allow_slow_non_contiguous=True).then_inc(s_cq, 16)
                sp.dma_start(cqn[0:RLAST, RT - 1:RT], d_c[b, m:ROWS].rearrange("(p o) -> p o", o=1)).then_inc(s_cq, 16)

            sp.dma_start(raw[0:T, MC, :], d_ln[0]).then_inc(s_lat, 16)
            load_queries(0)
            load_bias_rows(0)
            sp.dma_start(x1b[0:T, :], d_x1[0]).then_inc(s_x1l, 16)
            sp.wait_ge(s_zout, 16)
            sp.sem_inc(s_x2out, 16)

            def batch(b, events):
                more = ("T+", 0) in events
                if more:
                    sp.wait_ge(s_rawfree, b + 1)
                    load_context(b + 1, b + 1)
                    sp.dma_start(raw[0:T, MC, :], d_ln[b + 1]).then_inc(s_lat, 16)
                    sp.wait_ge(s_qbfree, b + 1)
                    load_queries(b + 1)
                    sp.wait_ge(s_cqfree, b + 1)
                    load_bias_rows(b + 1)
                sp.wait_ge(s_x2, b + 1)
                sp.dma_start(d_tok[bass.ds(b * T, T), :], x2b[0:T, :]).then_inc(s_x2out, 16)
                if more:
                    sp.dma_start(x1b[0:T, :], d_x1[b + 1]).then_inc(s_x1l, 16)

            batches(sp, batch)

            loads_c = [(desc[:], a["desc"]), (eid[:], a["eid"]), (tokv[0:T, :], a["tokv"]),
                       (upper[:], a["upper"]), (ones[:], a["ones"]), (ones8[:], a["ones"][:, 0:E]),
                       (iota[:], a["iota"])]
            sp.wait_ge(s_x2out, 16 * (B + 1))
            for dst, src in loads_c:
                sp.dma_start(dst, src).then_inc(s_cc, 16)
            assert len(loads_c) == N_CC

            def load_weights(e, turn, chunks):
                for j in chunks:
                    which, f = pieces[j]
                    if j >= 4 or not isinstance(turn, int) or turn > 0:
                        sp.wait_ge(s_wl, turn * NW + j - 3)
                    sp.dma_start(stage[j % 4][:], w_src(which, e, f)).then_inc(s_w[j % 4], 16)

            load_weights(0, 0, range(4))
            with sp.Fori(0, E - 1) as n:
                load_weights(n, n, range(4, NW))
                load_weights(n + 1, n + 1, range(4))
            load_weights(E - 1, E - 1, range(4, NW))
            sp.wait_ge(s_ctl, 1)
            n_ov = sp.value_load(ctl[0:1, 7:8], min_val=0, max_val=NOV)
            with sp.Fori(0, NOV) as k:
                with sp.If(k < n_ov):
                    e = sp.value_load(ctl[0:1, bass.ds(k, 1)], min_val=0, max_val=E - 1)
                    load_weights(e, k + E, range(NW))

        @block.gpsimd
        def _(pool):
            ch = Chain(pool, s_pool)
            pool.memset(raw[:], 0.0).then_inc(s_rawz, 1)

            def inv_std(dst, var, n, parts, made, at, done):
                pool.wait_ge(made, at)
                apart()
                ch.add(pool.tensor_scalar(dst, var, EPS, 0.0, ALU.add, ALU.add))
                ch.join()
                ch.add(pool.tensor_tensor(dst, dst, phalf[0:parts, 0:n], ALU.pow))
                ch.join()
                pool.sem_inc(done, 1)

            def apart():
                pool.sem_inc(s_apart, 1)

            def norm_rows(turn):
                inv_std(rsr[:], mvr[:, :, 1], MC, P, s_mvr, turn + 1, s_rsr)
                for c in range(MC):
                    r = MLAST if c == MC - 1 else P
                    pool.wait_ge(s_apr, turn * MC + c + 1)
                    ch.add(pool.tensor_tensor(raw[0:r, c, :], raw[0:r, c, :], gm[0:r, :], ALU.mult))
                    ch.join()
                    ch.add(pool.tensor_tensor(raw[0:r, c, :], raw[0:r, c, :], bm[0:r, :], ALU.add))
                ch.join()
                pool.sem_inc(s_ln, 1)

            pool.wait_ge(s_ca, 16 * N_CA)
            inv_std(rsa[0:T, :], mva[0:T, :, 1], B, T, s_mva, 1, s_rsa)
            for b in range(B):
                pool.wait_ge(s_xha, b + 1)
                pool.tensor_tensor(xin[0:T, b, :], xin[0:T, b, :], boa[0:T, :], ALU.add).then_inc(s_xr, 1)
            norm_rows(0)
            for half in range(2):
                hb = slice(half * HALF, (half + 1) * HALF)
                for k in range(2):
                    inv_std(rsa[0:T, hb], mva[0:T, hb, 1], HALF, T, s_mva, 2 + 2 * half + k, s_rsa)
                for bb in range(HALF):
                    b = half * HALF + bb
                    pool.tensor_tensor(xin[0:T, b, :], xin[0:T, b, :], box[0:T, :], ALU.add).then_inc(s_x1r, 1)
                    pool.wait_ge(s_lnh, b + 1)
                    ch.add(pool.tensor_tensor(xh[0:T, b, :], xh[0:T, b, :], gl[0:T, :], ALU.mult))
                    ch.join()
                    pool.tensor_tensor(xh[0:T, b, :], xh[0:T, b, :], bl[0:T, :], ALU.add).then_inc(s_lnr, 1)

            def router_std(turn):
                pool.wait_ge(s_mvx, turn + 1)
                apart()
                ch.add(pool.tensor_scalar(rsx[0:T, 1:2], rsx[0:T, 0:1], EPS, 0.0, ALU.add, ALU.add))
                ch.join()
                ch.add(pool.tensor_tensor(rbuf[0:T, 1:2], rsx[0:T, 1:2], phalf[0:T, 0:1], ALU.pow))
                ch.join()
                pool.sem_inc(s_rsx, 1)

            def run(b, events):
                for what, k in events:
                    if what == "R" and k == 0:
                        router_std(b)
                    elif what == "X":
                        pool.wait_ge(s_xnh, b * KC + k + 1)
                        pool.tensor_tensor(xn_l[:, k, :], raw[:, k, :], xn_h[:, k, :].bitcast(F32), ALU.subtract
                                           ).then_inc(s_xnl, 1)
                        if k == KC - 1:
                            pool.wait_ge(s_xnl, b * KC + KC)
                            pool.sem_inc(s_rawfree, 1)
                    elif what == "L" and k == 0:
                        norm_rows(b)

            run(0, first)
            batches(pool, lambda b, events: steps(run, b, events), ch, POOL_B)
            router_std(B)

            pool.wait_ge(s_idx, 1)
            pool.wait_ge(s_x2out, 16 * (B + 1))
            pool.sem_inc(s_yofree, 1)

            def gather(n):
                if not isinstance(n, int) or n > 0:
                    pool.wait_ge(s_gfree, n)
                ch.add(pool.tensor_copy(idc[:, 0:1], idx[:, bass.ds(n, 1)]))
                ch.join()
                apart()
                pool.indirect_dma_start(
                    out=gat[:], out_offset=None, in_=d_tok,
                    in_offset=bass.IndirectOffsetOnAxis(ap=idc[:, 0:1], axis=0)).then_inc(s_gat, 16)

            def slot(n, more):
                gather(n + 1)
                ch.add(pool.tensor_copy(idc[:, 1:2], idx[:, bass.ds(n, 1)]))
                ch.join()
                pool.wait_ge(s_yo, n + 2)
                apart()
                pool.indirect_dma_start(
                    out=out, out_offset=bass.IndirectOffsetOnAxis(ap=idc[:, 1:2], axis=0),
                    in_=yo[:], in_offset=None, bounds_check=NTOK - 1, oob_is_err=False).then_inc(s_out, 16)
                pool.wait_ge(s_out, n * 16 + 16)
                pool.sem_inc(s_yofree, 1)

            gather(0)
            n_ov = slots(pool, slot, ch, 2)
            pool.wait_ge(s_gat, n_ov * 16 + 16 * (E + 1))

        @block.tensor
        def _(pe):
            pe.wait_ge(s_ca, 16 * N_CA)
            for b in range(B):
                pe.wait_ge(s_xha, b + 1)
                if b >= 2:
                    pe.wait_ge(s_tea, b - 1)
                for c in range(ND):
                    last = pe.transpose(tbank[b % 2][:, c * T:(c + 1) * T], xh[0:T, b, c * P:(c + 1) * P],
                                        ident[0:T, 0:T])
                last.then_inc(s_tpa, 1)
            pe.wait_ge(s_tea, B)
            n = 0
            for e in range(ND):
                for w in range(2):
                    for half in range(2):
                        k = [0, 1, 2, 3][n % 4]
                        if n >= 4:
                            pe.wait_ge(s_ugs, n - 3)
                        for c in range(ND):
                            last = pe.matmul(bank[k][:, 0:HT], w3[w][:, c, e * P:(e + 1) * P],
                                             xt[:, c, half * HT:(half + 1) * HT], start=c == 0, stop=c == ND - 1)
                        last.then_inc(s_ugp, 1)
                        n += 1
            pe.wait_ge(s_wq, 16)
            pe.wait_ge(s_hsc, ND)
            for half in range(2):
                for bb in range(HALF):
                    b = half * HALF + bb
                    if b >= 2:
                        pe.wait_ge(s_x1, b - 1)
                    for c in range(ND):
                        last = pe.matmul(zbank[b % 2][0:T, :], hs[:, c, b * T:(b + 1) * T], w3[2][:, c, :],
                                         start=c == 0, stop=c == ND - 1)
                    last.then_inc(s_op, 1)
            for half in range(2):
                if half:
                    pe.wait_ge(s_ce, HEADS)
                for bb in range(HALF):
                    b = half * HALF + bb
                    pe.wait_ge(s_lnr, b + 1)
                    if b >= 2:
                        pe.wait_ge(s_tel, b - 1)
                    for c in range(ND):
                        last = pe.transpose(tbank[b % 2][:, c * T:(c + 1) * T], xh[0:T, b, c * P:(c + 1) * P],
                                            ident[0:T, 0:T])
                    last.then_inc(s_tpl, 1)
                pe.wait_ge(s_tel, HALF * (half + 1))
                for h in range(HEADS):
                    n = half * HEADS + h
                    if n >= 4:
                        pe.wait_ge(s_qe, n - 3)
                    for c in range(ND):
                        last = pe.matmul(bank[n % 4][:, 0:HT], wq[:, c, h * P:(h + 1) * P],
                                         xt[:, c, half * HT:(half + 1) * HT], start=c == 0, stop=c == ND - 1)
                    last.then_inc(s_qp, 1)
                for h in range(HEADS):
                    n = half * HEADS + h
                    pe.wait_ge(s_qe, n + 1)
                    if n >= 4:
                        pe.wait_ge(s_ce, n - 3)
                    pe.matmul(bank[4 + n % 4][0:1, 0:HT], bk[:, h:h + 1], qa[:, h, :, :].rearrange("p b t -> p (b t)"),
                              start=True, stop=True).then_inc(s_cp, 1)
            pe.wait_ge(s_ce, 2 * HEADS)

            pe.wait_ge(s_wb, 16 * N_WB)

            tb, zb = rings()
            for s in s_zread:
                pe.sem_inc(s, 1)

            def run(b, events):
                for what, k in events:
                    if what == "T":
                        if k == 0:
                            pe.wait_ge(s_ln, b + 1)
                            pe.wait_ge(s_lat, b * 16 + 16)
                        tb.free(pe)
                        t, _, _ = tb.take()
                        for c in range(ND):
                            last = pe.transpose(t[:, c * P:(c + 1) * P], raw[:, k, c * P:(c + 1) * P], ident[:])
                        last.then_inc(s_tb, 1)
                    elif what == "Q":
                        dc, hg = k // 2, k % 2
                        if k == 0:
                            pe.wait_ge(s_qb, b * 16 + 16)
                        if k >= 4:
                            pe.wait_ge(s_qread, b * 2 * ND + k - 3)
                        elif not isinstance(b, int) or b > 0:
                            pe.wait_ge(s_exp, b * RT - (k < 2))
                        for hh in range(4):
                            h = hg * 4 + hh
                            last = pe.matmul(qbank[k % 4][:, hh * T:(hh + 1) * T], wk[:, h, dc * P:(dc + 1) * P],
                                             qb[:, h * T:(h + 1) * T], start=True, stop=True)
                        last.then_inc(s_qp2, 1)
                    elif what == "S":
                        if k == 0:
                            tb.all_read(pe)
                            pe.wait_ge(s_qread, (b + 1) * 2 * ND)
                        elif k >= 2:
                            pe.wait_ge(s_exp, b * RT + k - 1)
                        at = 0
                        for half in range(2):
                            last = split_products(
                                pe, s_pair[k % 2][half][:, 0:SH[half]],
                                [((qt_h[:, c, k * P:(k + 1) * P], qt_l[:, c, k * P:(k + 1) * P]),
                                  (xt_h[:, c, at:at + SH[half]], xt_l[:, c, at:at + SH[half]])) for c in range(ND)],
                                True, True)
                            at += SH[half]
                        last.then_inc(s_s, 1)
                    elif what == "PT":
                        pe.wait_ge(s_p, b * RT + k + 1)
                        for chunks in (range(0, 4), range(4, KC)):
                            tb.free(pe)
                            t, _, _ = tb.take()
                            for n, c in enumerate(chunks):
                                last = pe.transpose(t[:, n * P:(n + 1) * P], pr[k % 3][:, c * P:(c + 1) * P],
                                                    ident[:])
                            last.then_inc(s_tb, 1)
                    elif what == "Z":
                        g, dc = k
                        if k == (0, 0):
                            pe.wait_ge(s_xnl, b * KC + KC)
                        if dc == 0:
                            tb.all_read(pe)
                        w = sum(rows_of(i) for i in GROUPS[g])
                        zb.free(pe)
                        z, _, _ = zb.take()
                        split_products(
                            pe, z[:, 0:w],
                            [((xn_h[:, c, dc * P:(dc + 1) * P], xn_l[:, c, dc * P:(dc + 1) * P]),
                              (pt_h[:, c, 0:w], pt_l[:, c, 0:w])) for c in range(KC)],
                            True, True).then_inc(s_zb, 1)
                    elif what == "V":
                        lo = GROUPS[k][0] * P
                        zb.all_read(pe)
                        z, _, _ = zb.take()
                        for h, c0, c1 in segments(GROUPS[k]):
                            for dc in range(ND):
                                last = pe.matmul(z[:, c0 - lo:c1 - lo], wv[:, dc, h * P:(h + 1) * P],
                                                 zt[:, dc, c0 - lo:c1 - lo], start=dc == 0, stop=dc == ND - 1)
                        last.then_inc(s_zb, 1)
                    elif what == "Y":
                        zb.all_read(pe)
                        z, _, _ = zb.take()
                        for h in range(HEADS):
                            last = pe.matmul(z[0:T, :], ot[:, h * T:(h + 1) * T], wo[:, h, :],
                                             start=h == 0, stop=h == HEADS - 1)
                        last.then_inc(s_zb, 1)
                    elif what == "R" and k == 2:
                        pe.wait_ge(s_x3, b + 1)
                        tb.free(pe)
                        t, _, _ = tb.take()
                        for c in range(ND):
                            last = pe.transpose(t[:, c * T:(c + 1) * T], x3b[0:T, c * P:(c + 1) * P],
                                                ident[0:T, 0:T])
                        last.then_inc(s_tb, 1)
                    elif what == "R" and k == 3:
                        pe.wait_ge(s_x3t, b + 1)
                        t = tb.banks[(tb.n - 1) % 2]
                        for c in range(ND):
                            last = pe.matmul(t[0:T, ND * T:ND * T + E], x3t[:, c, :], wr[:, c, :],
                                             start=c == 0, stop=c == ND - 1)
                        last.then_inc(s_lp, 1)

            def batch(b, events):
                tb.at(b, TB_USES, TB0)
                zb.at(b, ZB_USES, 0)
                steps(run, b, events)

            run(0, first)
            batches(pe, batch)
            run(B, [("R", 2), ("R", 3)])

            pe.wait_ge(s_cc, 16 * N_CC)
            pe.wait_ge(s_oh, 1)
            ohf = oh[0:T, :, :].rearrange("p b e -> p (b e)")
            pe.matmul(bank[0][0:T, 0:B * E], upper[0:T, 0:T], ohf, start=True, stop=False, skip_group_check=True)
            for k in range(1, B):
                last = pe.matmul(bank[0][0:T, k * E:B * E], ones[0:T, 0:T], ohf[:, 0:(B - k) * E],
                                 start=False, stop=k == B - 1, skip_group_check=True)
            for b in range(B):
                last = pe.matmul(bank[1][:, 0:E], ones[0:T, :], ohf[:, b * E:(b + 1) * E],
                                 start=b == 0, stop=b == B - 1)
            last.then_inc(s_rk, 1)
            pe.wait_ge(s_ohv, 1)
            for b in range(B):
                last = pe.matmul(bank[2][:, 0:4 * NSLOT], ohp[0:T, b, :], ohv[0:T, b, :, :].rearrange("p v s -> p (v s)"),
                                 start=b == 0, stop=b == B - 1)
            last.then_inc(s_tp, 1)

            def tokens(n):
                pe.wait_ge(s_x3g, n + 1)
                for c in range(ND):
                    last = pe.transpose(bank[4][:, c * P:(c + 1) * P], x3g[:, c * P:(c + 1) * P], ident[:])
                last.then_inc(s_xtp, 1)

            def slot(n, more):
                for what, k in slot_plan:
                    if what == "X":
                        tokens(n + 1)
                    elif what == "M":
                        q = piece_of[(1, k)]
                        if k == 0:
                            pe.wait_ge(s_xtl, n + 1)
                        pe.wait_ge(s_wl, n * NW + q + 1)
                        if k >= 2:
                            pe.wait_ge(s_gelu, n * NF + k - 1)
                        split_products(
                            pe, bank[k % 2][:],
                            [((xg_h[:, c, :], xg_l[:, c, :]), (wsh[q % 4][:, c, :], wsl[q % 4][:, c, :]))
                             for c in range(ND)], True, True).then_inc(s_hp, 1)
                    elif what == "H":
                        pe.wait_ge(s_gelu, n * NF + k + 1)
                        for c in range(4):
                            last = pe.transpose(bank[2 + k % 2][:, c * P:(c + 1) * P],
                                                hid[k % 2][:, c * P:(c + 1) * P], ident[:])
                        last.then_inc(s_htp, 1)
                    elif what == "O":
                        q = piece_of[(2, k)]
                        pe.wait_ge(s_htl, n * NF + k + 1)
                        pe.wait_ge(s_wl, n * NW + q + 1)
                        if k == 0:
                            pe.wait_ge(s_yo, n + 1)
                        last = split_products(
                            pe, bank[6][:],
                            [((ht_h[k % 2][:, c, :], ht_l[k % 2][:, c, :]),
                              (wsh[q % 4][:, c, :], wsl[q % 4][:, c, :])) for c in range(4)], k == 0, k == NF - 1)
                        last.then_inc(s_yp, 1)

            tokens(0)
            slots(pe, slot)

        @block.scalar
        def _(act):
            for b in range(B):
                act.wait_ge(s_tpa, b + 1)
                act.activation(xt[:, :, b * T:(b + 1) * T],
                               tbank[b % 2][:, 0:ND * T].rearrange("p (c t) -> p c t", c=ND), ACT.Copy
                               ).then_inc(s_tea, 1)
            act.wait_ge(s_ca, 16 * N_CA)
            n = 0
            for e in range(ND):
                if e >= 2:
                    act.wait_ge(s_hsc, e - 1)
                for w, dst in enumerate((ug, gg)):
                    for half in range(2):
                        act.wait_ge(s_ugp, n + 1)
                        act.activation(dst[e % 2][:, half * HT:(half + 1) * HT], bank[n % 4][:, 0:HT],
                                       (ACT.Identity, ACT.Sigmoid)[w], bias=ab[:, w, e:e + 1]).then_inc(s_ugs, 1)
                        n += 1
            for half in range(2):
                for b in range(half * HALF, (half + 1) * HALF):
                    act.wait_ge(s_tpl, b + 1)
                    act.activation(xt[:, :, b * T:(b + 1) * T],
                                   tbank[b % 2][:, 0:ND * T].rearrange("p (c t) -> p c t", c=ND), ACT.Copy
                                   ).then_inc(s_tel, 1)
                for h in range(HEADS):
                    n = half * HEADS + h
                    act.wait_ge(s_cp, n + 1)
                    if half and not h:
                        act.wait_ge(s_cout, 16 * HALF)
                    act.copy(crow[0:1, h, :, :].rearrange("p b t -> p (b t)"), bank[4 + n % 4][0:1, 0:HT]
                             ).then_inc(s_ce, 1)

            act.wait_ge(s_padb, 1)
            act.wait_ge(s_qout[0], 16 * HALF)
            act.wait_ge(s_qout[1], 16 * HALF)
            act.wait_ge(s_out_a, 32 * B)
            tb, zb = rings()

            def run(b, events):
                for what, k in events:
                    if what == "T":
                        t, _, n = tb.take()
                        act.wait_ge(s_tb, n)
                        c0, w = tcols(k)
                        act.copy(xt_h[:, :, c0:c0 + w], t[:].rearrange("p (c n) -> p c n", c=ND)[:, :, 0:w]
                                 ).then_inc(s_hi, 1)
                    elif what == "X":
                        act.copy(xn_h[:, k, :], raw[:, k, :]).then_inc(s_xnh, 1)
                    elif what == "Q":
                        dc, hg = k // 2, k % 2
                        act.wait_ge(s_qp2, b * 2 * ND + k + 1)
                        act.copy(qt_h[:, dc, hg * 4 * T:(hg + 1) * 4 * T], qbank[k % 4][:, 0:4 * T]).then_inc(s_hi, 1)
                    elif what == "S":
                        act.wait_ge(s_nb, b * RT + k + 1)
                        p, (s0, s1) = pr[k % 3], s_pair[k % 2]
                        nb = smx[:, 4 + k % 2:5 + k % 2]
                        cut = MEDIA - SH[0]
                        r = rsm[:, 4 * (k % 2):4 * (k % 2) + 3]
                        act.activation(p[:, 0:SH[0]], s0[:, 0:SH[0]], ACT.Exp, bias=nb, accum_out=r[:, 0:1])
                        act.activation(p[:, SH[0]:MEDIA], s1[:, 0:cut], ACT.Exp, bias=nb, accum_out=r[:, 1:2])
                        act.activation(p[:, MC * P:MC * P + T], s1[:, cut:SH[1]], ACT.Exp, bias=nb,
                                       accum_out=r[:, 2:3]).then_inc(s_exp, 1)
                    elif what == "PT":
                        r = rows_of(k)
                        g = [g for g in GROUPS if k in g][0]
                        col = (k - g[0]) * P
                        for chunks in (range(0, 4), range(4, KC)):
                            t, _, u = tb.take()
                            act.wait_ge(s_tb, u)
                            n = len(chunks)
                            act.copy(pt_h[:, chunks[0]:chunks[0] + n, col:col + r],
                                     t[:, 0:n * P].rearrange("p (c q) -> p c q", c=n)[:, :, 0:r]).then_inc(s_hi, 1)
                    elif what == "Z":
                        g, dc = k
                        w = sum(rows_of(i) for i in GROUPS[g])
                        z, read, n = zb.take()
                        act.wait_ge(s_zb, n)
                        act.copy(zt[:, dc, 0:w], z[:, 0:w]).then_inc(read, 1)
                    elif what in ("V", "Y"):
                        zb.take()
                    elif what == "R" and k == 2:
                        t, _, n = tb.take()
                        act.wait_ge(s_tb, n)
                        act.copy(x3t[:], t[:, 0:ND * T].rearrange("p (c t) -> p c t", c=ND)).then_inc(s_x3t, 1)

            def batch(b, events):
                tb.at(b, TB_USES, TB0)
                zb.at(b, ZB_USES, 0)
                steps(run, b, events)

            run(0, first)
            batches(act, batch)
            run(B, [("R", 2)])

            act.wait_ge(s_lm, 1)
            act.activation(vals[0:T, :, 3], lmx[0:T, :], ACT.Sigmoid).then_inc(s_gate, 1)

            def high_weights(n, q):
                act.wait_ge(s_w[q % 4], n * 32 + 16 * (q // 4) + 16)
                act.copy(wsh[q % 4][:], stage[q % 4][:]).then_inc(s_wh, 1)

            def tokens(n):
                act.wait_ge(s_xtp, n + 1)
                act.copy(xg_h[:], bank[4][:].rearrange("p (c t) -> p c t", c=ND)).then_inc(s_xth, 1)

            def slot(n, more):
                for what, k in slot_plan:
                    if what == "W":
                        with only_if(act, more if k >= 4 else None):
                            which, f = pieces[k]
                            act.wait_ge((s_hp, s_yp)[which - 1], n * NF + f + 1)
                            high_weights(n, k + 4)
                    elif what == "X":
                        tokens(n + 1)
                    elif what == "M":
                        act.wait_ge(s_hp, n * NF + k + 1)
                        act.activation(hid[k % 2][:], bank[k % 2][:], ACT.Gelu).then_inc(s_gelu, 1)
                    elif what == "H":
                        act.wait_ge(s_htp, n * NF + k + 1)
                        act.copy(ht_h[k % 2][:], bank[2 + k % 2][:].rearrange("p (c t) -> p c t", c=4)
                                 ).then_inc(s_hth, 1)

            for q in range(4):
                high_weights(0, q)
            tokens(0)
            slots(act, slot)

        @block.vector
        def _(dve):
            ch = Chain(dve, s_dve)

            def stats(st, mv, src):
                ch.add(dve.bn_stats(st, src))
                ch.join()
                return ch.add(dve.bn_aggr(mv, st))

            def tally(s):
                ch.join()
                dve.sem_inc(s, 1)

            def rows_stats(turn):
                dve.wait_ge(s_raw, turn * 32 + 32)
                for c in range(MC):
                    r = MLAST if c == MC - 1 else P
                    ch.add(dve.bn_stats(str_[0:r, c, :], raw[0:r, c, :]))
                ch.join()
                dve.sem_inc(s_apart, 1)
                for c in range(MC):
                    r = MLAST if c == MC - 1 else P
                    ch.add(dve.bn_aggr(mvr[0:r, c, :], str_[0:r, c, :]))
                tally(s_mvr)

            def rows_norm(turn):
                dve.wait_ge(s_rsr, turn + 1)
                for c in range(MC):
                    r = MLAST if c == MC - 1 else P
                    dve.tensor_scalar(raw[0:r, c, :], raw[0:r, c, :], mvr[0:r, c, 0:1], rsr[0:r, c:c + 1],
                                      ALU.subtract, ALU.mult).then_inc(s_apr, 1)

            ch.add(dve.memset(mvr[:], 0.0))
            ch.join()
            for b in range(B):
                dve.wait_ge(s_x[b], 16)
                ch.add(dve.bn_stats(sta[0:T, b, :], xin[0:T, b, :]))
            ch.join()
            for b in range(B):
                ch.add(dve.bn_aggr(mva[0:T, b, :], sta[0:T, b, :]))
            tally(s_mva)
            dve.wait_ge(s_rsa, 1)
            for b in range(B):
                dve.tensor_scalar(xh[0:T, b, :], xin[0:T, b, :], mva[0:T, b, 0:1], rsa[0:T, b:b + 1],
                                  ALU.subtract, ALU.mult).then_inc(s_xha, 1)
            for e in range(ND):
                g, u = gg[e % 2], ug[e % 2]
                dve.wait_ge(s_ugs, 4 * e + 4)
                ch.add(dve.tensor_scalar(og[:], g[:], -1.0, 1.0, ALU.mult, ALU.add))
                ch.join()
                ch.add(dve.tensor_tensor(u[:], u[:], og[:], ALU.mult))
                ch.add(dve.memset(g[:].rearrange("p (b t) -> p b t", b=B)[:, :, 0:1], 0.0))
                ch.join()
                dve.tensor_tensor_scan(hs[:, e, :], g[:], u[:], 0.0, ALU.mult, ALU.add).then_inc(s_hsc, 1)
                if e < 2:
                    (rows_stats, rows_norm)[e](0)
            for half in range(2):
                bs = range(half * HALF, (half + 1) * HALF)
                for b in bs:
                    dve.wait_ge(s_op, b + 1)
                    dve.wait_ge(s_xr, b + 1)
                    ch.add(dve.tensor_tensor(xin[0:T, b, :], zbank[b % 2][0:T, :], xin[0:T, b, :], ALU.add))
                    ch.join()
                    dve.sem_inc(s_x1, 1)
                    ch.add(dve.bn_stats(sta[0:T, b, :], xin[0:T, b, :]))
                ch.join()
                for b in bs:
                    ch.add(dve.bn_aggr(mva[0:T, b, :], sta[0:T, b, :]))
                tally(s_mva)
                dve.wait_ge(s_rsa, 2 + 2 * half)
                for b in bs:
                    ch.add(dve.tensor_scalar(xh[0:T, b, :], xin[0:T, b, :], mva[0:T, b, 0:1], rsa[0:T, b:b + 1],
                                             ALU.subtract, ALU.mult))
                ch.join()
                for b in bs:
                    ch.add(dve.bn_stats(sta[0:T, b, :], xh[0:T, b, :]))
                ch.join()
                for b in bs:
                    ch.add(dve.bn_aggr(mva[0:T, b, :], sta[0:T, b, :]))
                tally(s_mva)
                dve.wait_ge(s_rsa, 3 + 2 * half)
                for b in bs:
                    dve.tensor_scalar(xh[0:T, b, :], xh[0:T, b, :], mva[0:T, b, 0:1], rsa[0:T, b:b + 1],
                                      ALU.subtract, ALU.mult).then_inc(s_lnh, 1)
            for half in range(2):
                for h in range(HEADS):
                    n = half * HEADS + h
                    dve.wait_ge(s_qp, n + 1)
                    if half and not h:
                        dve.wait_ge(s_qout[0], 16 * HALF)
                    dve.tensor_scalar(qa[:, h, :, :].rearrange("p b t -> p (b t)"), bank[n % 4][:, 0:HT],
                                      bq[:, h:h + 1], float(DH) ** -0.5, ALU.add, ALU.mult).then_inc(s_qe, 1)

            dve.wait_ge(s_out_a, 32 * B)
            dve.wait_ge(s_qout[1], 16 * HALF)
            dve.wait_ge(s_cout, 16 * B)
            ch.add(dve.memset(x2b[:], 0.0))
            tally(s_zero)
            for k in range(3):
                ch.add(dve.memset(pr[k][:], 0.0))
            ch.add(dve.memset(cqn[:], 0.0))
            ch.add(dve.memset(qt_h[:, :, ROWS:RT * P].bitcast(F32), 0.0))
            ch.add(dve.memset(qt_l[:, :, ROWS:RT * P].bitcast(F32), 0.0))
            tally(s_padb)

            dve.wait_ge(s_wb, 16 * N_WB)

            def low(dst, src, high):
                return dve.tensor_tensor(dst, src, high.bitcast(F32), ALU.subtract)

            tb, zb = rings()
            hi = [0, 0]

            def high_part():
                hi[0] += 1
                dve.wait_ge(s_hi, hi[1] * HI_USES + hi[0])

            def run(b, events):
                for what, k in events:
                    if what == "T":
                        t, read, _ = tb.take()
                        high_part()
                        c0, w = tcols(k)
                        low(xt_l[:, :, c0:c0 + w], t[:].rearrange("p (c n) -> p c n", c=ND)[:, :, 0:w],
                            xt_h[:, :, c0:c0 + w]).then_inc(read, 1)
                    elif what == "Q":
                        dc, hg = k // 2, k % 2
                        high_part()
                        cols = slice(hg * 4 * T, (hg + 1) * 4 * T)
                        low(qt_l[:, dc, cols], qbank[k % 4][:, 0:4 * T], qt_h[:, dc, cols]).then_inc(s_qread, 1)
                        if k == 2 * ND - 1:
                            dve.sem_inc(s_qbfree, 1)
                            dve.wait_ge(s_cq, b * 32 + 32)
                            ch.add(dve.tensor_copy(cq[:], cqn[:]))
                            tally(s_cqfree)
                    elif what == "S":
                        dve.wait_ge(s_s, b * RT + k + 1)
                        s0, s1 = s_pair[k % 2]
                        ch.add(dve.reduce_max(smx[:, 0:1], s0[:, 0:SH[0]], AX))
                        ch.add(dve.reduce_max(smx[:, 1:2], s1[:, 0:SH[1]], AX))
                        ch.join()
                        c = cq[:, k:k + 1]
                        ch.add(dve.scalar_tensor_tensor(smx[:, 2:3], smx[:, 0:1], smx[:, 1:2], c, ALU.max, ALU.add))
                        ch.join()
                        dve.tensor_tensor(smx[:, 4 + k % 2:5 + k % 2], c, smx[:, 2:3], ALU.subtract
                                          ).then_inc(s_nb, 1)
                    elif what == "N":
                        dve.wait_ge(s_exp, b * RT + k + 1)
                        o = 4 * (k % 2)
                        ch.add(dve.reduce_sum(rsm[:, o + 3:o + 4], rsm[:, o:o + 3], AX))
                        ch.join()
                        ch.add(dve.reciprocal(rsm[:, o + 3:o + 4], rsm[:, o + 3:o + 4]))
                        ch.join()
                        dve.tensor_scalar(pr[k % 3][:], pr[k % 3][:], rsm[:, o + 3:o + 4], None, ALU.mult
                                          ).then_inc(s_p, 1)
                    elif what == "PT":
                        r = rows_of(k)
                        g = [g for g in GROUPS if k in g][0]
                        col = (k - g[0]) * P
                        for chunks in (range(0, 4), range(4, KC)):
                            t, read, _ = tb.take()
                            high_part()
                            n = len(chunks)
                            part = (slice(None), slice(chunks[0], chunks[0] + n), slice(col, col + r))
                            low(pt_l[part], t[:, 0:n * P].rearrange("p (c q) -> p c q", c=n)[:, :, 0:r],
                                pt_h[part]).then_inc(read, 1)
                    elif what == "Z":
                        zb.take()
                    elif what == "V":
                        lo = GROUPS[k][0] * P
                        z, read, n = zb.take()
                        dve.wait_ge(s_zb, n)
                        for h, c0, c1 in segments(GROUPS[k]):
                            last = dve.tensor_scalar(ot[:, c0:c1], z[:, c0 - lo:c1 - lo],
                                                     bv[:, h:h + 1], None, ALU.add)
                        last.then_inc(read, 1)
                    elif what == "Y":
                        z, read, n = zb.take()
                        dve.wait_ge(s_zb, n)
                        dve.wait_ge(s_x1l, b * 16 + 16)
                        dve.wait_ge(s_x2out, b * 16 + 16)
                        ch.add(dve.tensor_tensor(x2b[0:T, :], z[0:T, :], x1b[0:T, :], ALU.add))
                        ch.join()
                        dve.sem_inc(read, 1)
                        dve.sem_inc(s_x2, 1)
                    elif what == "L":
                        (rows_stats, rows_norm)[k](b)
                    elif what == "R" and k == 0:
                        ch.add(dve.bn_stats(stx[0:T, :], x2b[0:T, :]))
                        ch.join()
                        dve.sem_inc(s_apart, 1)
                        ch.add(dve.bn_aggr(mvx[0:T, :], stx[0:T, :]))
                        ch.join()
                        ch.add(dve.tensor_copy(rbuf[0:T, 0:1], mvx[0:T, 0:1]))
                        ch.add(dve.tensor_copy(rsx[0:T, 0:1], mvx[0:T, 1:2]))
                        tally(s_mvx)
                    elif what == "R" and k == 1:
                        dve.wait_ge(s_rsx, b + 1)
                        ch.add(dve.tensor_scalar(x3b[0:T, :], x2b[0:T, :], rbuf[0:T, 0:1], rbuf[0:T, 1:2],
                                                 ALU.subtract, ALU.mult))
                        tally(s_x3)
                    elif what == "R" and k == 2:
                        router_bank[0] = tb.take()
                    elif what == "R" and k == 3:
                        t, read, _ = router_bank[0]
                        dve.wait_ge(s_lp, b + 1)
                        ch.add(dve.tensor_tensor(rbuf[0:T, 2:NREC], t[0:T, ND * T:ND * T + E], brb[0:T, :], ALU.add))
                        ch.join()
                        dve.sem_inc(read, 1)
                        ch.add(dve.tensor_copy(rec[0:T, bass.ds(b, 1), :], rbuf[0:T, :].unsqueeze(1)))

            router_bank = [None]

            def batch(b, events):
                tb.at(b, TB_USES, TB0)
                zb.at(b, ZB_USES, 0)
                hi[0], hi[1] = HI0, b
                steps(run, b, events)

            run(0, first)
            batches(dve, batch, ch, DVE_B)
            run(B, [("R", k) for k in range(4)])
            ch.join()

            dve.wait_ge(s_cc, 16 * N_CC)
            dve.wait_ge(s_x2out, 16 * (B + 1))
            t = slice(0, T)
            be = "p b e -> p (b e)"
            lg = rec[t, 1:B + 1, 2:NREC]
            ch.add(dve.reduce_max(lmx[t, :], lg, AX))
            tally(s_lm)
            for b in range(B):
                ch.add(dve.tensor_scalar(eq[t, b, :], lg[:, b, :], lmx[t, b:b + 1], None, ALU.is_ge))
            ch.join()
            ch.add(dve.tensor_tensor(eq[t].rearrange(be), eq[t].rearrange(be), desc[t].rearrange(be), ALU.mult))
            ch.join()
            ch.add(dve.reduce_max(kmx[t, :], eq[t], AX))
            ch.join()
            for b in range(B):
                ch.add(dve.tensor_scalar(oh[t, b, :], desc[t, b, :], kmx[t, b:b + 1], None, ALU.is_equal))
            tally(s_oh)
            dve.wait_ge(s_rk, 1)
            ch.add(dve.tensor_tensor(tmp[t].rearrange(be), bank[0][t, 0:B * E], oh[t].rearrange(be), ALU.mult))
            ch.add(dve.tensor_copy(cnt[:], bank[1][:, 0:E]))
            ch.join()
            ch.add(dve.reduce_sum(rank[t, :], tmp[t], AX))
            for j in range(NOV):
                ch.add(dve.tensor_scalar(cmp_[:, j, :], cnt[:], float(TILE * (j + 1)), None, ALU.is_gt))
            ch.join()
            ch.add(dve.reduce_sum(ovc[:], cmp_[:].rearrange("p j e -> p e j"), AX))
            ch.add(dve.tensor_tensor(tmp[t].rearrange(be), eid[t].rearrange(be), oh[t].rearrange(be), ALU.mult))
            for j in range(NOV):
                ch.add(dve.tensor_scalar(cmr[t, j, :], rank[t, :], float(TILE * (j + 1)), None, ALU.is_ge))
            ch.join()
            ch.add(dve.reduce_sum(jt[t, :], cmr[t].rearrange("p j b -> p b j"), AX))
            ch.add(dve.reduce_sum(pa[t, :], tmp[t], AX))
            ch.add(dve.tensor_tensor_scan(ove[:], ones8[:], ovc[:], 0.0, ALU.mult, ALU.add))
            ch.join()
            ch.add(dve.tensor_tensor(ovb[:], ove[:], ovc[:], ALU.subtract))
            ch.add(dve.scalar_tensor_tensor(pin[t, :], jt[t, :], -float(TILE), rank[t, :], ALU.mult, ALU.add))
            ch.join()
            for b in range(B):
                ch.add(dve.tensor_tensor(tmp[t, b, :], oh[t, b, :], ovb[t, :], ALU.mult))
                ch.add(dve.tensor_scalar(ohp[t, b, :], iota[t, :], pin[t, b:b + 1], None, ALU.is_equal))
            ch.join()
            ch.add(dve.reduce_sum(pb[t, :], tmp[t], AX))
            ch.join()
            ch.add(dve.scalar_tensor_tensor(pb[t, :], pb[t, :], float(E - 1), jt[t, :], ALU.add, ALU.add))
            ch.join()
            ch.add(dve.tensor_tensor(pb[t, :], pb[t, :], pa[t, :], ALU.subtract))
            ch.join()
            ch.add(dve.tensor_tensor(pb[t, :], pb[t, :], cmr[t, 0, :], ALU.mult))
            ch.join()
            ch.add(dve.tensor_tensor(pb[t, :], pb[t, :], pa[t, :], ALU.add))
            ch.add(dve.tensor_copy(vals[t, :, 0], tokv[t, :]))
            ch.add(dve.tensor_copy(vals[t, :, 1:3], rec[t, 1:B + 1, 0:2]))
            ch.join()
            for b in range(B):
                ch.add(dve.tensor_scalar(ohs[t, b, :], iota[t, 0:NSLOT], pb[t, b:b + 1], None, ALU.is_equal))
            ch.join()
            dve.wait_ge(s_gate, 1)
            ch.add(dve.tensor_tensor(ohv[t], ohs[t].unsqueeze(2).broadcast_to([T, B, 4, NSLOT]),
                                     vals[t].unsqueeze(3).broadcast_to([T, B, 4, NSLOT]), ALU.mult))
            tally(s_ohv)
            for k in range(NOV):
                ch.add(dve.tensor_scalar(cmp_[:, k, :], ove[:], float(k), None, ALU.is_le))
            ch.join()
            ch.add(dve.reduce_sum(ek[:, 0:NOV], cmp_[:], AX))
            ch.join()
            ch.add(dve.tensor_scalar(ek[:, 0:NOV], ek[:, 0:NOV], float(E - 1), None, ALU.min))
            ch.add(dve.tensor_copy(ek[:, 7:8], ove[:, E - 1:E]))
            ch.add(dve.memset(ek[:, 6:7], 0.0))
            ch.join()
            ch.add(dve.tensor_copy(ctl[:], ek[:]))
            tally(s_ctl)
            dve.wait_ge(s_tp, 1)
            ch.add(dve.tensor_scalar(idx[:], bank[2][:, 0:NSLOT], float(NTOK), None, ALU.add))
            tally(s_idx)
            ch.add(dve.tensor_copy(sm[:].rearrange("p s v -> p v s"),
                                   bank[2][:, 0:4 * NSLOT].rearrange("p (v s) -> p v s", v=4)))
            ch.join()

            dve.sem_inc(s_yo, 1)

            def norm_tokens(n):
                ch.add(dve.tensor_copy(cur[:], sm[:, bass.ds(n, 1), :].rearrange("p o v -> p (o v)")))
                ch.join()
                dve.wait_ge(s_gat, n * 16 + 16)
                ch.add(dve.tensor_scalar(x3g[:], gat[:], cur[:, 1:2], cur[:, 2:3], ALU.subtract, ALU.mult))
                tally(s_x3g)

            def keep_tokens(n):
                ch.add(dve.tensor_copy(x2g[:], gat[:]))
                ch.add(dve.tensor_copy(pg[:], cur[:, 3:4]))
                tally(s_gfree)

            def split_tokens(n):
                dve.wait_ge(s_xth, n + 1)
                low(xg_l[:], bank[4][:].rearrange("p (c t) -> p c t", c=ND), xg_h[:]).then_inc(s_xtl, 1)

            def low_weights(n, q):
                dve.wait_ge(s_wh, n * NW + q + 1)
                low(wsl[q % 4][:], stage[q % 4][:], wsh[q % 4][:]).then_inc(s_wl, 1)

            def slot(n, more):
                for what, k in slot_plan:
                    if what == "G":
                        dve.wait_ge(s_xtp, n + 1)
                        norm_tokens(n + 1)
                    elif what == "K":
                        dve.wait_ge(s_yo, n + 2)
                        keep_tokens(n + 1)
                    elif what == "W":
                        with only_if(dve, more if k >= 4 else None):
                            low_weights(n, k + 4)
                    elif what == "X":
                        split_tokens(n + 1)
                    elif what == "H":
                        dve.wait_ge(s_hth, n * NF + k + 1)
                        low(ht_l[k % 2][:], bank[2 + k % 2][:].rearrange("p (c t) -> p c t", c=4), ht_h[k % 2][:]
                            ).then_inc(s_htl, 1)
                    elif what == "R":
                        dve.wait_ge(s_yp, n * NF + NF)
                        dve.wait_ge(s_yofree, n + 1)
                        dve.scalar_tensor_tensor(yo[:], bank[6][:], pg[:], x2g[:], ALU.mult, ALU.add
                                                 ).then_inc(s_yo, 1)

            norm_tokens(0)
            keep_tokens(0)
            for q in range(4):
                low_weights(0, q)
            split_tokens(0)
            slots(dve, slot, ch, 4)


def kernel(**inputs):
    from concourse import bacc
    from concourse.bass_utils import run_bass_kernel_spmd

    src = {k: np.ascontiguousarray(v) for k, v in inputs.items()}
    t = np.ascontiguousarray
    arrays = {
        "x": src["x"], "ctx": src["ctx_1024"],
        "WiT": t(src["L0_attn_Wi"].T), "WgT": t(src["L0_attn_Wg"].T), "WoT": t(src["L0_attn_Wo"].T),
        "ab": t(np.stack([src["L0_attn_bi"], src["L0_attn_bg"]]).reshape(2, ND, P).transpose(2, 0, 1)),
        "bo_a": src["L0_attn_bo"],
        "gm": src["L0_xattn_gamma_media"], "bm": src["L0_xattn_beta_media"],
        "gl": src["L0_xattn_gamma_lat"], "bl": src["L0_xattn_beta_lat"],
        "Wq": src["L0_xattn_Wq"], "bq": t(src["L0_xattn_bq"].reshape(HEADS, P).T),
        "WkT": t(src["L0_xattn_Wkv"][:, :INNER].T), "Wv": t(src["L0_xattn_Wkv"][:, INNER:]),
        "bk": t(src["L0_xattn_bkv"][:INNER].reshape(HEADS, P).T),
        "bv": t(src["L0_xattn_bkv"][INNER:].reshape(HEADS, P).T), "Wo_x": src["L0_xattn_Wo"], "bo_x": src["L0_xattn_bo"],
        "Wr": src["L0_ffn_Wr"], "br": src["L0_ffn_br"], "W1": src["L0_ffn_W1"], "W2": src["L0_ffn_W2"],
        "ident": np.eye(P, dtype=np.float32),
        "phalf": np.full((P, 16), -0.5, np.float32),
        "desc": np.broadcast_to(np.arange(E, 0, -1, dtype=np.float32), (P, B, E)).copy(),
        "eid": np.broadcast_to(np.arange(E, dtype=np.float32), (P, B, E)).copy(),
        "tokv": np.arange(-NTOK, 0, dtype=np.float32).reshape(B, T).T.copy(),
        "upper": np.triu(np.ones((P, P), np.float32), 1),
        "ones": np.ones((P, P), np.float32),
        "iota": np.broadcast_to(np.arange(P, dtype=np.float32), (P, P)).copy(),
    }
    nc = bacc.Bacc("TRN2", target_bir_lowering=False, num_devices=1)
    aps, feed = {}, {}
    for name, arr in arrays.items():
        feed[f"in_{name}"] = arr
        aps[name] = nc.dram_tensor(f"in_{name}", arr.shape, mybir.dt.from_np(arr.dtype), kind="ExternalInput").ap()
    out = nc.dram_tensor("out", (B, T, D), F32, kind="ExternalOutput").ap()
    build(nc, aps, out.rearrange("b t d -> (b t) d"))
    result = run_bass_kernel_spmd(nc, [feed], core_ids=[0])
    return result.results[0]["out"]
```

```python
from contextlib import ExitStack

import numpy as np

import concourse.bass as bass
from concourse import mybir
from concourse.alu_op_type import AluOpType as ALU

F32 = mybir.dt.float32
F32R = mybir.dt.float32r
I32 = mybir.dt.int32
ACT = mybir.ActivationFunctionType
AX = mybir.AxisListType.X

B, T, D = 8, 100, 512
MEDIA = 722
HEADS, DH = 8, 128
INNER = HEADS * DH
FFN, E = 2048, 8
P = 128
ND = D // P
NTOK = B * T
EPS = 1e-5

HALF = 4
HT = HALF * T

MC = -(-MEDIA // P)
KC = MC + 1
MLAST = MEDIA - (MC - 1) * P
KEYS = MEDIA + T
KPAD = KC * P
SH = [412, KEYS - 412]
ROWS = HEADS * T
RT = -(-ROWS // P)
RLAST = ROWS - (RT - 1) * P
GROUPS = [[0, 1], [2, 3], [4, 5, 6]]
GW = 2 * P + RLAST

TILE = 128
NOV = NTOK // TILE
NSLOT = E + NOV + 1
N_CA, N_WB, N_CC = 9, 2, 10
POOL_B, DVE_B = 4 + 2 * MC, 56
FC = 512
NF = FFN // FC
NREC = 2 + E


def rows_of(tile):
    return RLAST if tile == RT - 1 else P


def segments(group):
    lo = group[0] * P
    hi = min(ROWS, (group[-1] + 1) * P)
    out = []
    while lo < hi:
        end = min(hi, (lo // T + 1) * T)
        out.append((lo // T, lo, end))
        lo = end
    return out


class Chain:

    def __init__(self, eng, sem):
        self.eng, self.sem, self.n, self.turn, self.per = eng, sem, 0, None, 0

    def add(self, ins):
        ins.then_inc(self.sem, 1)
        self.n += 1
        return ins

    def join(self):
        v = self.n if self.turn is None else self.turn * self.per + self.n
        self.eng.wait_ge(self.sem, v)

    def enter(self, turn, per):
        self.turn, self.per, self.start = turn, per, self.n

    def leave(self, turns):
        assert self.n - self.start == self.per, (self.n - self.start, self.per)
        self.n = self.start + turns * self.per
        self.turn = None


class Ring:

    def __init__(self, banks, read, begin):
        self.banks, self.read, self.begin, self.n, self.turn, self.per = banks, read, begin, 0, 0, 0

    def at(self, turn, per, first):
        assert per % 2 == 0
        self.turn, self.per, self.n = turn, per, first

    def take(self):
        k = self.n % 2
        self.n += 1
        return self.banks[k], self.read[k], self.turn * self.per + self.n

    def free(self, eng):
        v = self.turn * (self.per // 2) + self.n // 2 + self.begin
        if not isinstance(v, int) or v > 0:
            eng.wait_ge(self.read[self.n % 2], v)

    def all_read(self, eng):
        for k in range(2):
            eng.wait_ge(self.read[k], self.turn * (self.per // 2) + (self.n + 1 - k) // 2 + self.begin)


class Memory:

    def __init__(self, nc):
        self.nc = nc
        self.at = -(-nc.sbuf_base // 64) * 64
        self.end = nc.sbuf_usable_end
        self.placed = []

    def __call__(self, name, shape, dtype=F32):
        size = int(np.prod(shape[1:])) * 4
        t = self.nc.alloc_sbuf_tensor_at(name, shape, dtype, offset=self.at)
        self.placed.append((t, self.at))
        self.at += -(-size // 64) * 64
        assert self.at <= self.end, (name, self.at, self.end)
        return t

    def over(self, other, name, shape, dtype=F32):
        at = [at for t, at in self.placed if t is other][0]
        return self.nc.alloc_sbuf_tensor_at(name, shape, dtype, offset=at)


def build(nc, a, out):
    mem = Memory(nc)
    ctx = ExitStack()

    def sem(name):
        return ctx.enter_context(nc.semaphore(name))

    bank = [ctx.enter_context(nc.psum_tensor(f"bank{k}", [P, 512], F32)) for k in range(8)]

    def dram(name, shape, dtype=F32):
        return nc.dram_tensor(name, shape, dtype, kind="Internal").ap()
    d_ln = dram("scr_latents", (B, T, D))
    d_x1 = dram("scr_x1", (B, T, D))
    d_q = dram("scr_q", (B, P, ROWS))
    d_c = dram("scr_c", (B, ROWS))
    d_tok = dram("scr_tokens", (NTOK + 1, D))

    ident = mem("ident", [P, P])
    phalf = mem("phalf", [P, 16])
    gm = mem("gm", [P, D])
    bm = mem("bm", [P, D])
    bv = mem("bv", [P, HEADS])
    bk = mem("bk", [P, HEADS])
    wr = mem("wr", [P, ND, E])
    raw = mem("raw", [P, KC, D])
    mvr = mem("mvr", [P, MC, 2])
    rsr = mem("rsr", [P, MC])
    brb = mem("brb", [P, E])
    rec = mem("rec", [P, B + 1, NREC])
    str_ = mem("str_", [P, MC, 6])
    desc = mem("desc", [P, B, E])
    eid = mem("eid", [P, B, E])
    ones8 = mem("ones8", [P, E])
    tokv = mem("tokv", [P, B])
    iota = mem("iota", [P, P])
    upper = mem("upper", [P, P])
    ones = mem("ones", [P, P])
    base = mem.at

    wk = mem("wk", [P, HEADS, D])
    wv = mem("wv", [P, ND, INNER])
    wo = mem("wo", [P, HEADS, D])
    base_b = mem.at
    xn_h = mem("xn_h", [P, KC, D], F32R)
    xn_l = mem("xn_l", [P, KC, D], F32R)
    xt_h = mem("xt_h", [P, ND, KEYS + 2], F32R)
    xt_l = mem("xt_l", [P, ND, KEYS + 2], F32R)
    qt_h = mem("qt_h", [P, ND, RT * P], F32R)
    qt_l = mem("qt_l", [P, ND, RT * P], F32R)
    pr = [mem(f"pr{k}", [P, KPAD]) for k in range(3)]
    pt_h = mem("pt_h", [P, KC, GW], F32R)
    pt_l = mem("pt_l", [P, KC, GW], F32R)
    zt = mem("zt", [P, ND, GW])
    qb = mem("qb", [P, ROWS])
    ot = mem("ot", [P, ROWS])
    x1b = mem("x1b", [P, D])
    x2b = mem("x2b", [P, D])
    x3b = mem("x3b", [P, D])
    x3t = mem("x3t", [P, ND, T])
    cqn = mem("cqn", [P, RT])
    cq = mem("cq", [P, RT])
    stx = mem("stx", [P, 6])
    rbuf = mem("rbuf", [P, NREC])
    mvx = mem("mvx", [P, 2])
    rsx = mem("rsx", [P, 2])
    smx = mem("smx", [P, 6])
    rsm = mem("rsm", [P, 8])

    mem.at = base
    w3 = [mem(f"w3_{k}", [P, ND, D]) for k in range(3)]
    w3_h = [mem(f"w3_h{k}", [P, ND, D], F32R) for k in range(3)]
    w3_l = [mem.over(w3[k], f"w3_l{k}", [P, ND, D], F32R) for k in range(3)]
    crow = mem.over(w3_h[1], "crow", [P, HEADS, HALF, T])
    mem.at = base_b
    xin = mem("xin", [P, B, D])
    xh = mem("xh", [P, B, D])
    hs = mem("hs", [P, ND, NTOK])
    hs_h = mem("hs_h", [P, ND, NTOK], F32R)
    hs_l = mem.over(hs, "hs_l", [P, ND, NTOK], F32R)
    boa = mem.over(hs_h, "boa", [P, D])
    wq = mem("wq", [P, ND, INNER])
    wq_h = mem("wq_h", [P, ND, INNER], F32R)
    wq_l = mem.over(wq, "wq_l", [P, ND, INNER], F32R)
    qa = mem("qa", [P, HEADS, HALF, T])
    mem.at -= HEADS * HALF * T * 4
    ug = [mem(f"ug{k}", [P, NTOK]) for k in range(2)]
    gg = [mem(f"gg{k}", [P, NTOK]) for k in range(2)]
    xa_h = mem("xa_h", [P, ND, NTOK], F32R)
    xa_l = mem("xa_l", [P, ND, NTOK], F32R)
    og = mem("og", [P, NTOK])
    gl = mem("gl", [P, D])
    bl = mem("bl", [P, D])
    box = mem("box", [P, D])
    ab = mem("ab", [P, 2, ND])
    bq = mem("bq", [P, HEADS])
    bqs = mem("bqs", [P, HEADS])
    sta = mem("sta", [P, B, 6])
    mva = mem("mva", [P, 3, B, 2])
    rsa = mem("rsa", [P, 3, B])

    mem.at = base
    stage = [mem(f"stage{k}", [P, 4, FC]) for k in range(4)]
    gat = mem("gat", [P, D])
    x3g = mem("x3g", [P, D])
    x2g = mem("x2g", [P, D])
    yo = mem("yo", [P, D])
    xg_h = mem("xg_h", [P, ND, TILE], F32R)
    xg_l = mem("xg_l", [P, ND, TILE], F32R)
    hid = [mem(f"hid{k}", [P, FC]) for k in range(2)]
    wsh = [mem(f"wsh{k}", [P, 4, FC], F32R) for k in range(4)]
    wsl = [mem(f"wsl{k}", [P, 4, FC], F32R) for k in range(4)]
    ht_h = [mem(f"ht_h{k}", [P, 4, TILE], F32R) for k in range(2)]
    ht_l = [mem(f"ht_l{k}", [P, 4, TILE], F32R) for k in range(2)]
    cur = mem("cur", [P, 4])
    pg = mem("pg", [P, 1])
    idx = mem("idx", [P, NSLOT], I32)
    sm = mem("sm", [P, NSLOT, 4])
    idc = mem("idc", [P, 2], I32)
    ctl = mem("ctl", [P, 8], I32)
    lmx = mem("lmx", [P, B])
    eq = mem("eq", [P, B, E])
    kmx = mem("kmx", [P, B])
    oh = mem("oh", [P, B, E])
    tmp = mem("tmp", [P, B, E])
    rank = mem("rank", [P, B])
    pin = mem("pin", [P, B])
    jt = mem("jt", [P, B])
    pa = mem("pa", [P, B])
    pb = mem("pb", [P, B])
    cnt = mem("cnt", [P, E])
    cmr = mem("cmr", [P, NOV, B])
    cmp_ = mem("cmp_", [P, NOV, E])
    ovc = mem("ovc", [P, E])
    ove = mem("ove", [P, E])
    ovb = mem("ovb", [P, E])
    ek = mem("ek", [P, 8])
    vals = mem("vals", [P, B, 4])
    ohp = mem("ohp", [P, B, P])
    ohs = mem("ohs", [P, B, NSLOT])
    ohv = mem("ohv", [P, B, 4, NSLOT])

    s_x = [sem(f"s_xin{b}") for b in range(B)]
    s_w3 = [sem(f"s_w3_{k}") for k in range(3)]
    s_id, s_wk = sem("s_id"), sem("s_wk")
    s_ca, s_wq, s_wb, s_cc, s_zero, s_zout = (
        sem("s_ca"), sem("s_wq"), sem("s_wb"), sem("s_cc"), sem("s_zero"), sem("s_zout"))
    s_dve, s_act, s_pool = sem("s_dve"), sem("s_act"), sem("s_pool")
    s_mva, s_rsa, s_xha, s_tpa, s_tea = sem("s_mva"), sem("s_rsa"), sem("s_xha"), sem("s_tpa"), sem("s_tea")
    s_wa, s_wah, s_wal, s_tha, s_hsh, s_hsl = (sem(n) for n in ("s_wa", "s_wah", "s_wal", "s_tha", "s_hsh", "s_hsl"))
    s_lnout, s_bqs, s_padq, s_padp = sem("s_lnout"), sem("s_bqs"), sem("s_padq"), sem("s_padp")
    s_ugp, s_ugs, s_hsc, s_xr = sem("s_ugp"), sem("s_ugs"), sem("s_hsc"), sem("s_xr")
    s_op, s_x1, s_lnr, s_x1r = sem("s_op"), sem("s_x1"), sem("s_lnr"), sem("s_x1r")
    s_tpl, s_tel, s_qp, s_qe, s_out_a = sem("s_tpl"), sem("s_tel"), sem("s_qp"), sem("s_qe"), sem("s_out_a")
    s_qout = [sem("s_qout0"), sem("s_qout1")]
    s_apart = sem("s_apart")
    s_padb, s_rawz, s_lat = sem("s_padb"), sem("s_rawz"), sem("s_lat")
    s_cp, s_ce, s_cout = sem("s_cp"), sem("s_ce"), sem("s_cout")
    s_raw, s_rawfree, s_mvr, s_rsr, s_apr, s_ln = (sem(n) for n in (
        "s_raw", "s_rawfree", "s_mvr", "s_rsr", "s_apr", "s_ln"))
    s_qb, s_qbfree, s_x1l, s_x1free, s_x2, s_x2out, s_cq, s_cqfree = (sem(n) for n in (
        "s_qb", "s_qbfree", "s_x1l", "s_x1free", "s_x2", "s_x2out", "s_cq", "s_cqfree"))
    s_tb, s_zb = sem("s_tb"), sem("s_zb")
    s_tread, s_zread = [sem("s_tread0"), sem("s_tread1")], [sem("s_zread0"), sem("s_zread1")]
    s_hi, s_xnh, s_xnl, s_s, s_nb, s_exp, s_p, s_qp2, s_qread = (sem(n) for n in (
        "s_hi", "s_xnh", "s_xnl", "s_s", "s_nb", "s_exp", "s_p", "s_qp2", "s_qread"))
    s_mvx, s_rsx, s_x3, s_x3t, s_lp = (sem(n) for n in ("s_mvx", "s_rsx", "s_x3", "s_x3t", "s_lp"))
    s_lm, s_gate, s_oh, s_rk, s_ohv, s_tp, s_idx, s_ctl = (sem(n) for n in (
        "s_lm", "s_gate", "s_oh", "s_rk", "s_ohv", "s_tp", "s_idx", "s_ctl"))
    s_w = [sem(f"s_w{k}") for k in range(4)]
    s_wh, s_wl = sem("s_wh"), sem("s_wl")
    s_gat, s_gfree, s_x3g, s_xtp, s_xth, s_xtl = (sem(n) for n in (
        "s_gat", "s_gfree", "s_x3g", "s_xtp", "s_xth", "s_xtl"))
    s_hp, s_gelu, s_htp, s_hth, s_htl, s_yp, s_yo, s_out, s_yofree = (sem(n) for n in (
        "s_hp", "s_gelu", "s_htp", "s_hth", "s_htl", "s_yp", "s_yo", "s_out", "s_yofree"))

    def bc(vec, n, parts=P):
        return vec.rearrange("(o n) -> o n", o=1).broadcast_to([parts, n])

    plan = [("PT", 1), ("S", 2), ("R", 0), ("Z", (0, 0)), ("Z", (0, 1)), ("N", 2), ("L+", 0), ("S", 3), ("Z", (0, 2)),
            ("N", 3), ("Z", (0, 3)), ("PT", 2), ("V", 0), ("PT", 3), ("S", 4), ("R", 1), ("Z", (1, 0)), ("N", 4),
            ("Z", (1, 1)), ("L+", 1), ("R", 2), ("S", 5), ("R", 3), ("N", 5), ("S", 6), ("Z", (1, 2)), ("Z", (1, 3)),
            ("N", 6), ("PT", 4), ("V", 1), ("PT", 5), ("PT", 6), ("Q+", 0), ("Q+", 1), ("Q+", 2), ("Z", (2, 0)),
            ("T+", 0), ("T+", 1), ("Q+", 3), ("Z", (2, 1)), ("T+", 2), ("T+", 3), ("Z", (2, 2)), ("T+", 4), ("T+", 5),
            ("Q+", 4), ("T+", 6), ("Q+", 5), ("Q+", 6), ("Q+", 7), ("Z", (2, 3)), ("S+", 0), ("X+", 0), ("X+", 1),
            ("V", 2), ("N+", 0), ("S+", 1), ("X+", 2), ("X+", 3), ("PT+", 0), ("N+", 1), ("Y", 0),
            ("X+", 4), ("X+", 5), ("X+", 6)]
    first = [(what[:-1], k) for what, k in plan if what[-1] == "+" and what != "L+"]
    TB0, HI0 = KC + 2, KC + 2 * ND + 2
    TB_USES = KC + 2 * RT + 1
    ZB_USES = 3 * (ND + 1) + 1
    HI_USES = KC + 2 * ND + 2 * RT
    qbank = [bank[2], bank[3], bank[0], bank[1]]
    s_pair = [(bank[0], bank[1]), (bank[2], bank[3])]
    tbank, zbank = (bank[4], bank[5]), (bank[6], bank[7])

    def rings():
        return Ring(tbank, s_tread, 0), Ring(zbank, s_zread, 1)

    def batches(eng, body, chain=None, per=0):
        with eng.Fori(0, B - 1) as b:
            if chain:
                chain.enter(b, per)
            body(b, plan)
            if chain:
                chain.leave(B - 1)
        body(B - 1, [e for e in plan if e[0][-1] != "+"])

    def steps(run, b, events):
        for what, k in events:
            if what[-1] == "+":
                run(b + 1, [(what[:-1], k)])
            else:
                run(b, [(what, k)])

    def tcols(c):
        return (c * P, min(P, MEDIA - c * P)) if c < MC else (MEDIA, T)

    norms = [("A", 0), ("A", 1), ("B", 0), ("A", 2), ("B", 1), ("C", 0), ("C", 1), ("A", 3)]
    norms += [("H", b) for b in range(HALF)] + [("B", 2), ("B", 3), ("C", 2), ("C", 3)]
    norms += [("H", b) for b in range(HALF, B)]
    stds = [e for e in norms if e[0] in "AB"]

    slot_plan = [("M", 0), ("W", 0), ("M", 1), ("H", 0), ("W", 1), ("M", 2), ("H", 1), ("W", 2), ("O", 0), ("W", 3),
                 ("G", 1), ("M", 3), ("H", 2), ("W", 4), ("O", 1), ("X", 1), ("H", 3), ("W", 5), ("O", 2), ("W", 6),
                 ("O", 3), ("R", 0), ("K", 1), ("W", 7)]
    pieces = [(1, 0), (1, 1), (1, 2), (2, 0), (1, 3), (2, 1), (2, 2), (2, 3)]
    piece_of = {p: n for n, p in enumerate(pieces)}
    NW = len(pieces)

    def slots(eng, body, chain=None, per=0):
        with eng.Fori(0, E - 1) as n:
            if chain:
                chain.enter(n, per)
            body(n, None)
            if chain:
                chain.leave(E - 1)
        eng.wait_ge(s_ctl, 1)
        n_ov = eng.value_load(ctl[0:1, 7:8], min_val=0, max_val=NOV)
        body(E - 1, 0 < n_ov)
        with eng.Fori(0, NOV) as k:
            with eng.If(k < n_ov):
                if chain:
                    chain.enter(k, per)
                body(k + E, k + 1 < n_ov)
                if chain:
                    chain.leave(NOV)
        return n_ov

    def only_if(eng, cond):
        return ExitStack() if cond is None else eng.If(cond)

    def w_src(which, e, f):
        if which == 1:
            return a["W1"][e].rearrange("(k p) f -> p k f", p=P)[:, :, f * FC:(f + 1) * FC]
        return a["W2"][e, f * FC:(f + 1) * FC, :].rearrange("(k p) n -> p k n", p=P)

    def split_products(pe, dest, pairs, start, stop):
        n = len(pairs)
        for k, ((lh, ll), (rh, rl)) in enumerate(pairs):
            pe.matmul(dest, lh, rh, start=start and k == 0, stop=False)
            pe.matmul(dest, lh, rl, start=False, stop=False)
            last = pe.matmul(dest, ll, rh, start=False, stop=stop and k == n - 1)
        return last

    with ctx:
        block = ctx.enter_context(nc.Block())

        @block.sync
        def _(sp):
            def load_queries(b):
                sp.dma_start(qb[:], d_q[b]).then_inc(s_qb, 16)

            def load_bias_rows(b):
                m = (RT - 1) * P
                sp.dma_start(cqn[:, 0:RT - 1], d_c[b, 0:m].rearrange("(i p) -> p i", p=P),
                             allow_slow_non_contiguous=True).then_inc(s_cq, 16)
                sp.dma_start(cqn[0:RLAST, RT - 1:RT], d_c[b, m:ROWS].rearrange("(p o) -> p o", o=1)).then_inc(s_cq, 16)

            for b in range(B):
                sp.dma_start(xin[0:T, b, :], a["x"][b]).then_inc(s_x[b], 16)
            for k, name in enumerate(("WiT", "WgT", "WoT")):
                sp.dma_start(w3[k][:], a[name].rearrange("(c p) n -> p c n", p=P)).then_inc(s_w3[k], 16)
                if k == 0:
                    loads_a = [(ident[:], a["ident"]), (phalf[:], a["phalf"]), (boa[:], bc(a["bo_a"], D)),
                               (ab[:], a["ab"]), (bq[:], a["bq"]), (gl[:], bc(a["gl"], D)), (bl[:], bc(a["bl"], D)),
                               (box[:], bc(a["bo_x"], D)), (gm[:], bc(a["gm"], D)), (bm[:], bc(a["bm"], D)),
                               (bk[:], a["bk"])]
                    for dst, src in loads_a[:2]:
                        sp.dma_start(dst, src).then_inc(s_id, 16)
                if k == 1:
                    for dst, src in loads_a[2:]:
                        sp.dma_start(dst, src).then_inc(s_ca, 16)
                    assert len(loads_a) - 2 == N_CA

            def load_context(b, turn):
                sp.dma_start(raw[:, 0:MC - 1, :], a["ctx"][b, 0:(MC - 1) * P, :].rearrange("(c p) d -> p c d", p=P)
                             ).then_inc(s_raw, 16)
                sp.dma_start(raw[0:MLAST, MC - 1, :], a["ctx"][b, (MC - 1) * P:MEDIA, :]).then_inc(s_raw, 16)

            sp.wait_ge(s_rawz, 1)
            load_context(0, 0)
            sp.dma_start(wq[:], a["Wq"].rearrange("(c p) n -> p c n", p=P)).then_inc(s_wq, 16)
            loads_c = [(desc[:], a["desc"]), (eid[:], a["eid"]), (tokv[0:T, :], a["tokv"]),
                       (upper[:], a["upper"]), (ones[:], a["ones"]), (ones8[:], a["ones"][:, 0:E]),
                       (iota[:], a["iota"]), (brb[:], bc(a["br"], E)), (bv[:], a["bv"]),
                       (wr[:], a["Wr"].rearrange("(c p) e -> p c e", p=P))]
            for dst, src in loads_c:
                sp.dma_start(dst, src).then_inc(s_cc, 16)
            assert len(loads_c) == N_CC
            sp.wait_ge(s_op, B)
            sp.dma_start(wk[:], a["WkT"].rearrange("(h p) d -> p h d", p=P)).then_inc(s_wk, 16)
            for b in range(B):
                sp.wait_ge(s_lnr, b + 1)
                sp.dma_start(d_ln[b], xh[0:T, b, :]).then_inc(s_lnout, 16)
            sp.wait_ge(s_lnout, 16 * B)
            sp.dma_start(raw[0:T, MC, :], d_ln[0]).then_inc(s_lat, 16)
            for b in range(B):
                sp.wait_ge(s_x1r, b + 1)
                sp.dma_start(d_x1[b], xin[0:T, b, :]).then_inc(s_out_a, 16)
            for half in range(2):
                sp.wait_ge(s_qe, HEADS * (half + 1))
                if half:
                    load_queries(0)
                for bb in range(HALF):
                    sp.dma_start(d_q[half * HALF + bb].rearrange("p (h t) -> p h t", h=HEADS), qa[:, :, bb, :]
                                 ).then_inc(s_qout[half], 16)
                sp.wait_ge(s_ce, HEADS * (half + 1))
                for bb in range(HALF):
                    b = half * HALF + bb
                    sp.dma_start(d_c[b:b + 1, :].rearrange("o (h t) -> o h t", h=HEADS), crow[0:1, :, bb, :]
                                 ).then_inc(s_cout, 16)
            sp.wait_ge(s_cout, 16 * B)
            sp.wait_ge(s_padq, 1)
            load_bias_rows(0)
            sp.dma_start(wv[:], a["Wv"].rearrange("(c p) n -> p c n", p=P)).then_inc(s_wb, 16)
            sp.dma_start(wo[:], a["Wo_x"].rearrange("(h p) n -> p h n", p=P)).then_inc(s_wb, 16)
            sp.wait_ge(s_out_a, 16 * B)
            sp.dma_start(d_tok[NTOK:NTOK + 1, :], x2b[0:1, :]).then_inc(s_zout, 16)
            sp.dma_start(x1b[0:T, :], d_x1[0]).then_inc(s_x1l, 16)
            sp.wait_ge(s_zout, 16)
            sp.sem_inc(s_x2out, 16)

            def batch(b, events):
                more = ("T+", 0) in events
                if more:
                    sp.wait_ge(s_rawfree, b + 1)
                    load_context(b + 1, b + 1)
                    sp.dma_start(raw[0:T, MC, :], d_ln[b + 1]).then_inc(s_lat, 16)
                    sp.wait_ge(s_qbfree, b + 1)
                    load_queries(b + 1)
                    sp.wait_ge(s_cqfree, b + 1)
                    load_bias_rows(b + 1)
                else:
                    sp.wait_ge(s_qbfree, B)
                    load_weights(0, 0, range(2))
                sp.wait_ge(s_x2, b + 1)
                sp.dma_start(d_tok[bass.ds(b * T, T), :], x2b[0:T, :]).then_inc(s_x2out, 16)
                if more:
                    sp.dma_start(x1b[0:T, :], d_x1[b + 1]).then_inc(s_x1l, 16)
                else:
                    load_weights(0, 0, range(2, 4))

            def load_weights(e, turn, chunks):
                for j in chunks:
                    which, f = pieces[j]
                    if j >= 4 or not isinstance(turn, int) or turn > 0:
                        sp.wait_ge(s_wl, turn * NW + j - 3)
                    sp.dma_start(stage[j % 4][:], w_src(which, e, f)).then_inc(s_w[j % 4], 16)

            batches(sp, batch)

            with sp.Fori(0, E - 1) as n:
                load_weights(n, n, range(4, NW))
                load_weights(n + 1, n + 1, range(4))
            load_weights(E - 1, E - 1, range(4, NW))
            sp.wait_ge(s_ctl, 1)
            n_ov = sp.value_load(ctl[0:1, 7:8], min_val=0, max_val=NOV)
            with sp.Fori(0, NOV) as k:
                with sp.If(k < n_ov):
                    e = sp.value_load(ctl[0:1, bass.ds(k, 1)], min_val=0, max_val=E - 1)
                    load_weights(e, k + E, range(NW))

        @block.gpsimd
        def _(pool):
            ch = Chain(pool, s_pool)
            pool.memset(raw[:], 0.0).then_inc(s_rawz, 1)

            def inv_std(dst, var, n, parts, made, at, done):
                pool.wait_ge(made, at)
                apart()
                ch.add(pool.tensor_scalar(dst, var, EPS, 0.0, ALU.add, ALU.add))
                ch.join()
                ch.add(pool.tensor_tensor(dst, dst, phalf[0:parts, 0:n], ALU.pow))
                ch.join()
                pool.sem_inc(done, 1)

            def apart():
                pool.sem_inc(s_apart, 1)

            def norm_rows(turn):
                inv_std(rsr[:], mvr[:, :, 1], MC, P, s_mvr, turn + 1, s_rsr)
                for c in range(MC):
                    r = MLAST if c == MC - 1 else P
                    pool.wait_ge(s_apr, turn * MC + c + 1)
                    ch.add(pool.tensor_tensor(raw[0:r, c, :], raw[0:r, c, :], gm[0:r, :], ALU.mult))
                    ch.join()
                    ch.add(pool.tensor_tensor(raw[0:r, c, :], raw[0:r, c, :], bm[0:r, :], ALU.add))
                ch.join()
                pool.sem_inc(s_ln, 1)

            pool.wait_ge(s_id, 32)
            inv_std(rsa[0:T, 0, :], mva[0:T, 0, :, 1], B, T, s_mva, 1, s_rsa)
            pool.wait_ge(s_ca, 16 * N_CA)
            for b in range(B):
                pool.wait_ge(s_xha, b + 1)
                pool.tensor_tensor(xin[0:T, b, :], xin[0:T, b, :], boa[0:T, :], ALU.add).then_inc(s_xr, 1)
            norm_rows(0)
            for n, (what, g) in enumerate(stds):
                k, bs = 1 + "AB".index(what), slice(2 * g, 2 * g + 2)
                inv_std(rsa[0:T, k, bs], mva[0:T, k, bs, 1], 2, T, s_mva, n + 2, s_rsa)
            pool.wait_ge(s_lnr, B)
            for b in range(B):
                pool.tensor_tensor(xin[0:T, b, :], xin[0:T, b, :], box[0:T, :], ALU.add).then_inc(s_x1r, 1)

            def router_std(turn):
                pool.wait_ge(s_mvx, turn + 1)
                apart()
                ch.add(pool.tensor_scalar(rsx[0:T, 1:2], rsx[0:T, 0:1], EPS, 0.0, ALU.add, ALU.add))
                ch.join()
                ch.add(pool.tensor_tensor(rbuf[0:T, 1:2], rsx[0:T, 1:2], phalf[0:T, 0:1], ALU.pow))
                ch.join()
                pool.sem_inc(s_rsx, 1)

            def run(b, events):
                for what, k in events:
                    if what == "R" and k == 0:
                        router_std(b)
                    elif what == "X":
                        pool.wait_ge(s_xnh, b * KC + k + 1)
                        pool.tensor_tensor(xn_l[:, k, :], raw[:, k, :], xn_h[:, k, :].bitcast(F32), ALU.subtract
                                           ).then_inc(s_xnl, 1)
                        if k == KC - 1:
                            pool.wait_ge(s_xnl, b * KC + KC)
                            pool.sem_inc(s_rawfree, 1)
                    elif what == "L" and k == 0:
                        norm_rows(b)

            run(0, first)
            batches(pool, lambda b, events: steps(run, b, events), ch, POOL_B)
            router_std(B)

            pool.wait_ge(s_idx, 1)
            pool.wait_ge(s_x2out, 16 * (B + 1))
            pool.sem_inc(s_yofree, 1)

            def gather(n):
                if not isinstance(n, int) or n > 0:
                    pool.wait_ge(s_gfree, n)
                ch.add(pool.tensor_copy(idc[:, 0:1], idx[:, bass.ds(n, 1)]))
                ch.join()
                apart()
                pool.indirect_dma_start(
                    out=gat[:], out_offset=None, in_=d_tok,
                    in_offset=bass.IndirectOffsetOnAxis(ap=idc[:, 0:1], axis=0)).then_inc(s_gat, 16)

            def slot(n, more):
                gather(n + 1)
                ch.add(pool.tensor_copy(idc[:, 1:2], idx[:, bass.ds(n, 1)]))
                ch.join()
                pool.wait_ge(s_yo, n + 2)
                apart()
                pool.indirect_dma_start(
                    out=out, out_offset=bass.IndirectOffsetOnAxis(ap=idc[:, 1:2], axis=0),
                    in_=yo[:], in_offset=None, bounds_check=NTOK - 1, oob_is_err=False).then_inc(s_out, 16)
                pool.wait_ge(s_out, n * 16 + 16)
                pool.sem_inc(s_yofree, 1)

            gather(0)
            n_ov = slots(pool, slot, ch, 2)
            pool.wait_ge(s_gat, n_ov * 16 + 16 * (E + 1))

        @block.tensor
        def _(pe):
            pe.wait_ge(s_id, 32)
            for b in range(B):
                pe.wait_ge(s_xha, b + 1)
                if b >= 2:
                    pe.wait_ge(s_tea, b - 1)
                for c in range(ND):
                    last = pe.transpose(tbank[b % 2][:, c * T:(c + 1) * T], xh[0:T, b, c * P:(c + 1) * P],
                                        ident[0:T, 0:T])
                last.then_inc(s_tpa, 1)
            pe.wait_ge(s_tea, B)
            n = 0
            for e in range(ND):
                for w in range(2):
                    pe.wait_ge(s_wal, w + 1)
                    for half in range(2):
                        if n >= 4:
                            pe.wait_ge(s_ugs, n - 3)
                        cols = slice(half * HT, (half + 1) * HT)
                        split_products(
                            pe, bank[n % 4][:, 0:HT],
                            [((w3_h[w][:, c, e * P:(e + 1) * P], w3_l[w][:, c, e * P:(e + 1) * P]),
                              (xa_h[:, c, cols], xa_l[:, c, cols])) for c in range(ND)], True, True).then_inc(s_ugp, 1)
                        n += 1
            pe.wait_ge(s_wal, 3)
            pe.wait_ge(s_hsl, ND)
            for b in range(B):
                if b >= 2:
                    pe.wait_ge(s_x1, b - 1)
                cols = slice(b * T, (b + 1) * T)
                split_products(pe, zbank[b % 2][0:T, :],
                               [((hs_h[:, c, cols], hs_l[:, c, cols]), (w3_h[2][:, c, :], w3_l[2][:, c, :]))
                                for c in range(ND)], True, True).then_inc(s_op, 1)
            pe.wait_ge(s_wal, 4)
            for half in range(2):
                if half:
                    pe.wait_ge(s_ce, HEADS)
                for bb in range(HALF):
                    b = half * HALF + bb
                    pe.wait_ge(s_lnr, b + 1)
                    if b >= 2:
                        pe.wait_ge(s_tel, b - 1)
                    for c in range(ND):
                        last = pe.transpose(tbank[b % 2][:, c * T:(c + 1) * T], xh[0:T, b, c * P:(c + 1) * P],
                                            ident[0:T, 0:T])
                    last.then_inc(s_tpl, 1)
                pe.wait_ge(s_tel, HALF * (half + 1))
                for h in range(HEADS):
                    n = half * HEADS + h
                    if n >= 4:
                        pe.wait_ge(s_qe, n - 3)
                    cols = slice(half * HT, (half + 1) * HT)
                    split_products(
                        pe, bank[n % 4][:, 0:HT],
                        [((wq_h[:, c, h * P:(h + 1) * P], wq_l[:, c, h * P:(h + 1) * P]),
                          (xa_h[:, c, cols], xa_l[:, c, cols])) for c in range(ND)], True, True).then_inc(s_qp, 1)
                for h in range(HEADS):
                    n = half * HEADS + h
                    pe.wait_ge(s_qe, n + 1)
                    if n >= 4:
                        pe.wait_ge(s_ce, n - 3)
                    pe.matmul(bank[4 + n % 4][0:1, 0:HT], bk[:, h:h + 1], qa[:, h, :, :].rearrange("p b t -> p (b t)"),
                              start=True, stop=True).then_inc(s_cp, 1)
            pe.wait_ge(s_ce, 2 * HEADS)

            pe.wait_ge(s_wk, 16)
            tb, zb = rings()
            for s in s_zread:
                pe.sem_inc(s, 1)

            def run(b, events):
                for what, k in events:
                    if what == "T":
                        if k == 0:
                            pe.wait_ge(s_ln, b + 1)
                            pe.wait_ge(s_lat, b * 16 + 16)
                        tb.free(pe)
                        t, _, _ = tb.take()
                        for c in range(ND):
                            last = pe.transpose(t[:, c * P:(c + 1) * P], raw[:, k, c * P:(c + 1) * P], ident[:])
                        last.then_inc(s_tb, 1)
                    elif what == "Q":
                        dc, hg = k // 2, k % 2
                        if k == 0:
                            pe.wait_ge(s_qb, b * 16 + 16)
                        if k >= 4:
                            pe.wait_ge(s_qread, b * 2 * ND + k - 3)
                        elif not isinstance(b, int) or b > 0:
                            pe.wait_ge(s_exp, b * RT - (k < 2))
                        for hh in range(4):
                            h = hg * 4 + hh
                            last = pe.matmul(qbank[k % 4][:, hh * T:(hh + 1) * T], wk[:, h, dc * P:(dc + 1) * P],
                                             qb[:, h * T:(h + 1) * T], start=True, stop=True)
                        last.then_inc(s_qp2, 1)
                    elif what == "S":
                        if k == 0:
                            tb.all_read(pe)
                            pe.wait_ge(s_qread, (b + 1) * 2 * ND)
                        elif k >= 2:
                            pe.wait_ge(s_exp, b * RT + k - 1)
                        at = 0
                        for half in range(2):
                            last = split_products(
                                pe, s_pair[k % 2][half][:, 0:SH[half]],
                                [((qt_h[:, c, k * P:(k + 1) * P], qt_l[:, c, k * P:(k + 1) * P]),
                                  (xt_h[:, c, at:at + SH[half]], xt_l[:, c, at:at + SH[half]])) for c in range(ND)],
                                True, True)
                            at += SH[half]
                        last.then_inc(s_s, 1)
                    elif what == "PT":
                        pe.wait_ge(s_p, b * RT + k + 1)
                        for chunks in (range(0, 4), range(4, KC)):
                            tb.free(pe)
                            t, _, _ = tb.take()
                            for n, c in enumerate(chunks):
                                last = pe.transpose(t[:, n * P:(n + 1) * P], pr[k % 3][:, c * P:(c + 1) * P],
                                                    ident[:])
                            last.then_inc(s_tb, 1)
                    elif what == "Z":
                        g, dc = k
                        if k == (0, 0):
                            pe.wait_ge(s_xnl, b * KC + KC)
                        if dc == 0:
                            tb.all_read(pe)
                        w = sum(rows_of(i) for i in GROUPS[g])
                        zb.free(pe)
                        z, _, _ = zb.take()
                        split_products(
                            pe, z[:, 0:w],
                            [((xn_h[:, c, dc * P:(dc + 1) * P], xn_l[:, c, dc * P:(dc + 1) * P]),
                              (pt_h[:, c, 0:w], pt_l[:, c, 0:w])) for c in range(KC)],
                            True, True).then_inc(s_zb, 1)
                    elif what == "V":
                        lo = GROUPS[k][0] * P
                        zb.all_read(pe)
                        z, _, _ = zb.take()
                        for h, c0, c1 in segments(GROUPS[k]):
                            for dc in range(ND):
                                last = pe.matmul(z[:, c0 - lo:c1 - lo], wv[:, dc, h * P:(h + 1) * P],
                                                 zt[:, dc, c0 - lo:c1 - lo], start=dc == 0, stop=dc == ND - 1)
                        last.then_inc(s_zb, 1)
                    elif what == "Y":
                        zb.all_read(pe)
                        z, _, _ = zb.take()
                        for h in range(HEADS):
                            last = pe.matmul(z[0:T, :], ot[:, h * T:(h + 1) * T], wo[:, h, :],
                                             start=h == 0, stop=h == HEADS - 1)
                        last.then_inc(s_zb, 1)
                    elif what == "R" and k == 2:
                        pe.wait_ge(s_x3, b + 1)
                        tb.free(pe)
                        t, _, _ = tb.take()
                        for c in range(ND):
                            last = pe.transpose(t[:, c * T:(c + 1) * T], x3b[0:T, c * P:(c + 1) * P],
                                                ident[0:T, 0:T])
                        last.then_inc(s_tb, 1)
                    elif what == "R" and k == 3:
                        pe.wait_ge(s_x3t, b + 1)
                        t = tb.banks[(tb.n - 1) % 2]
                        for c in range(ND):
                            last = pe.matmul(t[0:T, ND * T:ND * T + E], x3t[:, c, :], wr[:, c, :],
                                             start=c == 0, stop=c == ND - 1)
                        last.then_inc(s_lp, 1)

            def batch(b, events):
                tb.at(b, TB_USES, TB0)
                zb.at(b, ZB_USES, 0)
                steps(run, b, events)

            run(0, first)
            pe.wait_ge(s_wb, 16 * N_WB)
            batches(pe, batch)
            run(B, [("R", 2), ("R", 3)])

            pe.wait_ge(s_cc, 16 * N_CC)
            pe.wait_ge(s_oh, 1)
            ohf = oh[0:T, :, :].rearrange("p b e -> p (b e)")
            pe.matmul(bank[0][0:T, 0:B * E], upper[0:T, 0:T], ohf, start=True, stop=False, skip_group_check=True)
            for k in range(1, B):
                last = pe.matmul(bank[0][0:T, k * E:B * E], ones[0:T, 0:T], ohf[:, 0:(B - k) * E],
                                 start=False, stop=k == B - 1, skip_group_check=True)
            for b in range(B):
                last = pe.matmul(bank[1][:, 0:E], ones[0:T, :], ohf[:, b * E:(b + 1) * E],
                                 start=b == 0, stop=b == B - 1)
            last.then_inc(s_rk, 1)
            pe.wait_ge(s_ohv, 1)
            for b in range(B):
                last = pe.matmul(bank[2][:, 0:4 * NSLOT], ohp[0:T, b, :], ohv[0:T, b, :, :].rearrange("p v s -> p (v s)"),
                                 start=b == 0, stop=b == B - 1)
            last.then_inc(s_tp, 1)

            def tokens(n):
                pe.wait_ge(s_x3g, n + 1)
                for c in range(ND):
                    last = pe.transpose(bank[4][:, c * P:(c + 1) * P], x3g[:, c * P:(c + 1) * P], ident[:])
                last.then_inc(s_xtp, 1)

            def slot(n, more):
                for what, k in slot_plan:
                    if what == "X":
                        tokens(n + 1)
                    elif what == "M":
                        q = piece_of[(1, k)]
                        if k == 0:
                            pe.wait_ge(s_xtl, n + 1)
                        pe.wait_ge(s_wl, n * NW + q + 1)
                        if k >= 2:
                            pe.wait_ge(s_gelu, n * NF + k - 1)
                        split_products(
                            pe, bank[k % 2][:],
                            [((xg_h[:, c, :], xg_l[:, c, :]), (wsh[q % 4][:, c, :], wsl[q % 4][:, c, :]))
                             for c in range(ND)], True, True).then_inc(s_hp, 1)
                    elif what == "H":
                        pe.wait_ge(s_gelu, n * NF + k + 1)
                        for c in range(4):
                            last = pe.transpose(bank[2 + k % 2][:, c * P:(c + 1) * P],
                                                hid[k % 2][:, c * P:(c + 1) * P], ident[:])
                        last.then_inc(s_htp, 1)
                    elif what == "O":
                        q = piece_of[(2, k)]
                        pe.wait_ge(s_htl, n * NF + k + 1)
                        pe.wait_ge(s_wl, n * NW + q + 1)
                        if k == 0:
                            pe.wait_ge(s_yo, n + 1)
                        last = split_products(
                            pe, bank[6][:],
                            [((ht_h[k % 2][:, c, :], ht_l[k % 2][:, c, :]),
                              (wsh[q % 4][:, c, :], wsl[q % 4][:, c, :])) for c in range(4)], k == 0, k == NF - 1)
                        last.then_inc(s_yp, 1)

            tokens(0)
            slots(pe, slot)

        @block.scalar
        def _(act):
            def high_weight(k):
                act.wait_ge((s_w3 + [s_wq])[k], 16)
                act.copy((w3_h + [wq_h])[k][:], (w3 + [wq])[k][:]).then_inc(s_wah, 1)

            high_weight(0)
            high_weight(1)
            for b in range(B):
                act.wait_ge(s_tpa, b + 1)
                act.copy(xa_h[:, :, b * T:(b + 1) * T], tbank[b % 2][:, 0:ND * T].rearrange("p (c t) -> p c t", c=ND)
                         ).then_inc(s_tha, 1)
            act.wait_ge(s_ca, 16 * N_CA)
            act.wait_ge(s_xr, B)
            n = 0
            for e in range(ND):
                if e >= 2:
                    act.wait_ge(s_hsc, e - 1)
                for w, dst in enumerate((ug, gg)):
                    for half in range(2):
                        act.wait_ge(s_ugp, n + 1)
                        act.activation(dst[e % 2][:, half * HT:(half + 1) * HT], bank[n % 4][:, 0:HT],
                                       (ACT.Identity, ACT.Sigmoid)[w], bias=ab[:, w, e:e + 1]).then_inc(s_ugs, 1)
                        n += 1
                act.wait_ge(s_hsc, e + 1)
                act.copy(hs_h[:, e, :], hs[:, e, :]).then_inc(s_hsh, 1)
                if e < 2:
                    high_weight(2 + e)
            act.wait_ge(s_bqs, 1)
            act.wait_ge(s_hsl, ND)
            for half in range(2):
                for b in range(half * HALF, (half + 1) * HALF):
                    act.wait_ge(s_tpl, b + 1)
                    act.copy(xa_h[:, :, b * T:(b + 1) * T], tbank[b % 2][:, 0:ND * T].rearrange("p (c t) -> p c t", c=ND)
                             ).then_inc(s_tha, 1)
                for h in range(HEADS):
                    n = half * HEADS + h
                    act.wait_ge(s_qp, n + 1)
                    if half and not h:
                        act.wait_ge(s_qout[0], 16 * HALF)
                        act.wait_ge(s_cout, 16 * HALF)
                    act.activation(qa[:, h, :, :].rearrange("p b t -> p (b t)"), bank[n % 4][:, 0:HT], ACT.Identity,
                                   bias=bqs[:, h:h + 1], scale=float(DH) ** -0.5).then_inc(s_qe, 1)
                for h in range(HEADS):
                    n = half * HEADS + h
                    act.wait_ge(s_cp, n + 1)
                    act.copy(crow[0:1, h, :, :].rearrange("p b t -> p (b t)"), bank[4 + n % 4][0:1, 0:HT]
                             ).then_inc(s_ce, 1)

            act.wait_ge(s_out_a, 16 * B)
            act.wait_ge(s_lnout, 16 * B)
            tb, zb = rings()

            def run(b, events):
                for what, k in events:
                    if what == "T":
                        t, _, n = tb.take()
                        act.wait_ge(s_tb, n)
                        c0, w = tcols(k)
                        act.copy(xt_h[:, :, c0:c0 + w], t[:].rearrange("p (c n) -> p c n", c=ND)[:, :, 0:w]
                                 ).then_inc(s_hi, 1)
                    elif what == "X":
                        act.copy(xn_h[:, k, :], raw[:, k, :]).then_inc(s_xnh, 1)
                    elif what == "Q":
                        dc, hg = k // 2, k % 2
                        act.wait_ge(s_qp2, b * 2 * ND + k + 1)
                        act.copy(qt_h[:, dc, hg * 4 * T:(hg + 1) * 4 * T], qbank[k % 4][:, 0:4 * T]).then_inc(s_hi, 1)
                    elif what == "S":
                        if k == 0:
                            act.wait_ge(s_padp, 1)
                        act.wait_ge(s_nb, b * RT + k + 1)
                        p, (s0, s1) = pr[k % 3], s_pair[k % 2]
                        nb = smx[:, 4 + k % 2:5 + k % 2]
                        cut = MEDIA - SH[0]
                        r = rsm[:, 4 * (k % 2):4 * (k % 2) + 3]
                        act.activation(p[:, 0:SH[0]], s0[:, 0:SH[0]], ACT.Exp, bias=nb, accum_out=r[:, 0:1])
                        act.activation(p[:, SH[0]:MEDIA], s1[:, 0:cut], ACT.Exp, bias=nb, accum_out=r[:, 1:2])
                        act.activation(p[:, MC * P:MC * P + T], s1[:, cut:SH[1]], ACT.Exp, bias=nb,
                                       accum_out=r[:, 2:3]).then_inc(s_exp, 1)
                    elif what == "PT":
                        r = rows_of(k)
                        g = [g for g in GROUPS if k in g][0]
                        col = (k - g[0]) * P
                        for chunks in (range(0, 4), range(4, KC)):
                            t, _, u = tb.take()
                            act.wait_ge(s_tb, u)
                            n = len(chunks)
                            act.copy(pt_h[:, chunks[0]:chunks[0] + n, col:col + r],
                                     t[:, 0:n * P].rearrange("p (c q) -> p c q", c=n)[:, :, 0:r]).then_inc(s_hi, 1)
                    elif what == "Z":
                        g, dc = k
                        w = sum(rows_of(i) for i in GROUPS[g])
                        z, read, n = zb.take()
                        act.wait_ge(s_zb, n)
                        act.copy(zt[:, dc, 0:w], z[:, 0:w]).then_inc(read, 1)
                    elif what in ("V", "Y"):
                        zb.take()
                    elif what == "R" and k == 2:
                        t, _, n = tb.take()
                        act.wait_ge(s_tb, n)
                        act.copy(x3t[:], t[:, 0:ND * T].rearrange("p (c t) -> p c t", c=ND)).then_inc(s_x3t, 1)

            def batch(b, events):
                tb.at(b, TB_USES, TB0)
                zb.at(b, ZB_USES, 0)
                steps(run, b, events)

            run(0, first)
            batches(act, batch)
            def high_weights(n, q):
                act.wait_ge(s_w[q % 4], n * 32 + 16 * (q // 4) + 16)
                act.copy(wsh[q % 4][:], stage[q % 4][:]).then_inc(s_wh, 1)

            def tokens(n):
                act.wait_ge(s_xtp, n + 1)
                act.copy(xg_h[:], bank[4][:].rearrange("p (c t) -> p c t", c=ND)).then_inc(s_xth, 1)

            def slot(n, more):
                for what, k in slot_plan:
                    if what == "W":
                        with only_if(act, more if k >= 4 else None):
                            which, f = pieces[k]
                            act.wait_ge((s_hp, s_yp)[which - 1], n * NF + f + 1)
                            high_weights(n, k + 4)
                    elif what == "X":
                        tokens(n + 1)
                    elif what == "M":
                        act.wait_ge(s_hp, n * NF + k + 1)
                        act.activation(hid[k % 2][:], bank[k % 2][:], ACT.Gelu).then_inc(s_gelu, 1)
                    elif what == "H":
                        act.wait_ge(s_htp, n * NF + k + 1)
                        act.copy(ht_h[k % 2][:], bank[2 + k % 2][:].rearrange("p (c t) -> p c t", c=4)
                                 ).then_inc(s_hth, 1)

            high_weights(0, 0)
            high_weights(0, 1)
            run(B, [("R", 2)])
            high_weights(0, 2)
            high_weights(0, 3)
            act.wait_ge(s_lm, 1)
            act.activation(vals[0:T, :, 3], lmx[0:T, :], ACT.Sigmoid).then_inc(s_gate, 1)
            tokens(0)
            slots(act, slot)

        @block.vector
        def _(dve):
            ch = Chain(dve, s_dve)

            def stats(st, mv, src):
                ch.add(dve.bn_stats(st, src))
                ch.join()
                return ch.add(dve.bn_aggr(mv, st))

            def tally(s):
                ch.join()
                dve.sem_inc(s, 1)

            def rows_stats(turn):
                dve.wait_ge(s_raw, turn * 32 + 32)
                for c in range(MC):
                    r = MLAST if c == MC - 1 else P
                    ch.add(dve.bn_stats(str_[0:r, c, :], raw[0:r, c, :]))
                ch.join()
                dve.sem_inc(s_apart, 1)
                for c in range(MC):
                    r = MLAST if c == MC - 1 else P
                    ch.add(dve.bn_aggr(mvr[0:r, c, :], str_[0:r, c, :]))
                tally(s_mvr)

            def rows_norm(turn):
                dve.wait_ge(s_rsr, turn + 1)
                for c in range(MC):
                    r = MLAST if c == MC - 1 else P
                    dve.tensor_scalar(raw[0:r, c, :], raw[0:r, c, :], mvr[0:r, c, 0:1], rsr[0:r, c:c + 1],
                                      ALU.subtract, ALU.mult).then_inc(s_apr, 1)

            def low(dst, src, high):
                return dve.tensor_tensor(dst, src, high.bitcast(F32), ALU.subtract)

            def low_weight(k):
                dve.wait_ge(s_wah, k + 1)
                low((w3_l + [wq_l])[k][:], (w3 + [wq])[k][:], (w3_h + [wq_h])[k][:]).then_inc(s_wal, 1)

            def low_rows(b, n, done):
                dve.wait_ge(s_tha, n + 1)
                part = (slice(None), slice(None), slice(b * T, (b + 1) * T))
                low(xa_l[part], tbank[b % 2][:, 0:ND * T].rearrange("p (c t) -> p c t", c=ND), xa_h[part]
                    ).then_inc(done, 1)

            ch.add(dve.memset(mvr[:], 0.0))
            ch.join()
            for b in range(B):
                dve.wait_ge(s_x[b], 16)
                ch.add(dve.bn_stats(sta[0:T, b, :], xin[0:T, b, :]))
            ch.join()
            for b in range(B):
                ch.add(dve.bn_aggr(mva[0:T, 0, b, :], sta[0:T, b, :]))
            tally(s_mva)
            low_weight(0)
            dve.wait_ge(s_rsa, 1)
            for b in range(B):
                dve.tensor_scalar(xh[0:T, b, :], xin[0:T, b, :], mva[0:T, 0, b, 0:1], rsa[0:T, 0, b:b + 1],
                                  ALU.subtract, ALU.mult).then_inc(s_xha, 1)
            for b in range(B):
                low_rows(b, b, s_tea)
            low_weight(1)
            dve.wait_ge(s_ca, 16 * N_CA)
            ch.add(dve.tensor_scalar(bqs[:], bq[:], float(DH) ** -0.5, None, ALU.mult))
            tally(s_bqs)
            for e in range(ND):
                g, u = gg[e % 2], ug[e % 2]
                dve.wait_ge(s_ugs, 4 * e + 4)
                ch.add(dve.tensor_scalar(og[:], g[:], -1.0, 1.0, ALU.mult, ALU.add))
                ch.join()
                ch.add(dve.tensor_tensor(u[:], u[:], og[:], ALU.mult))
                ch.add(dve.memset(g[:].rearrange("p (b t) -> p b t", b=B)[:, :, 0:1], 0.0))
                ch.join()
                dve.tensor_tensor_scan(hs[:, e, :], g[:], u[:], 0.0, ALU.mult, ALU.add).then_inc(s_hsc, 1)
                dve.wait_ge(s_hsh, e + 1)
                low(hs_l[:, e, :], hs[:, e, :], hs_h[:, e, :]).then_inc(s_hsl, 1)
                if e < 2:
                    (rows_stats, rows_norm)[e](0)
                    low_weight(2 + e)
            for what, g in norms:
                bs = range(2 * g, 2 * g + 2)
                if what == "A":
                    for b in bs:
                        dve.wait_ge(s_op, b + 1)
                        dve.wait_ge(s_xr, b + 1)
                        ch.add(dve.tensor_tensor(xin[0:T, b, :], zbank[b % 2][0:T, :], xin[0:T, b, :], ALU.add))
                        ch.join()
                        dve.sem_inc(s_x1, 1)
                        ch.add(dve.bn_stats(sta[0:T, b, :], xin[0:T, b, :]))
                    ch.join()
                    for b in bs:
                        ch.add(dve.bn_aggr(mva[0:T, 1, b, :], sta[0:T, b, :]))
                    tally(s_mva)
                elif what == "B":
                    dve.wait_ge(s_rsa, stds.index(("A", g)) + 2)
                    for b in bs:
                        ch.add(dve.tensor_scalar(xh[0:T, b, :], xin[0:T, b, :], mva[0:T, 1, b, 0:1],
                                                 rsa[0:T, 1, b:b + 1], ALU.subtract, ALU.mult))
                    ch.join()
                    for b in bs:
                        ch.add(dve.bn_stats(sta[0:T, b, :], xh[0:T, b, :]))
                    ch.join()
                    for b in bs:
                        ch.add(dve.bn_aggr(mva[0:T, 2, b, :], sta[0:T, b, :]))
                    tally(s_mva)
                elif what == "C":
                    dve.wait_ge(s_rsa, stds.index(("B", g)) + 2)
                    for b in bs:
                        ch.add(dve.scalar_tensor_tensor(xh[0:T, b, :], xh[0:T, b, :], mva[0:T, 2, b, 0:1], gl[0:T, :],
                                                        ALU.subtract, ALU.mult))
                    ch.join()
                    for b in bs:
                        dve.scalar_tensor_tensor(xh[0:T, b, :], xh[0:T, b, :], rsa[0:T, 2, b:b + 1], bl[0:T, :],
                                                 ALU.mult, ALU.add).then_inc(s_lnr, 1)
                elif what == "H":
                    low_rows(g, B + g, s_tel)

            dve.wait_ge(s_qe, 2 * HEADS)
            ch.add(dve.memset(x2b[:], 0.0))
            ch.add(dve.memset(cqn[:], 0.0))
            ch.add(dve.memset(qt_h[:, :, ROWS:RT * P].bitcast(F32), 0.0))
            ch.add(dve.memset(qt_l[:, :, ROWS:RT * P].bitcast(F32), 0.0))
            tally(s_padq)

            tb, zb = rings()
            hi = [0, 0]

            def high_part():
                hi[0] += 1
                dve.wait_ge(s_hi, hi[1] * HI_USES + hi[0])

            def run(b, events):
                for what, k in events:
                    if what == "T":
                        t, read, _ = tb.take()
                        high_part()
                        c0, w = tcols(k)
                        low(xt_l[:, :, c0:c0 + w], t[:].rearrange("p (c n) -> p c n", c=ND)[:, :, 0:w],
                            xt_h[:, :, c0:c0 + w]).then_inc(read, 1)
                    elif what == "Q":
                        dc, hg = k // 2, k % 2
                        high_part()
                        cols = slice(hg * 4 * T, (hg + 1) * 4 * T)
                        low(qt_l[:, dc, cols], qbank[k % 4][:, 0:4 * T], qt_h[:, dc, cols]).then_inc(s_qread, 1)
                        if k == 2 * ND - 1:
                            dve.sem_inc(s_qbfree, 1)
                            dve.wait_ge(s_cq, b * 32 + 32)
                            ch.add(dve.tensor_copy(cq[:], cqn[:]))
                            tally(s_cqfree)
                    elif what == "S":
                        dve.wait_ge(s_s, b * RT + k + 1)
                        s0, s1 = s_pair[k % 2]
                        ch.add(dve.reduce_max(smx[:, 0:1], s0[:, 0:SH[0]], AX))
                        ch.add(dve.reduce_max(smx[:, 1:2], s1[:, 0:SH[1]], AX))
                        ch.join()
                        c = cq[:, k:k + 1]
                        ch.add(dve.scalar_tensor_tensor(smx[:, 2:3], smx[:, 0:1], smx[:, 1:2], c, ALU.max, ALU.add))
                        ch.join()
                        dve.tensor_tensor(smx[:, 4 + k % 2:5 + k % 2], c, smx[:, 2:3], ALU.subtract
                                          ).then_inc(s_nb, 1)
                    elif what == "N":
                        dve.wait_ge(s_exp, b * RT + k + 1)
                        o = 4 * (k % 2)
                        ch.add(dve.reduce_sum(rsm[:, o + 3:o + 4], rsm[:, o:o + 3], AX))
                        ch.join()
                        ch.add(dve.reciprocal(rsm[:, o + 3:o + 4], rsm[:, o + 3:o + 4]))
                        ch.join()
                        dve.tensor_scalar(pr[k % 3][:], pr[k % 3][:], rsm[:, o + 3:o + 4], None, ALU.mult
                                          ).then_inc(s_p, 1)
                    elif what == "PT":
                        r = rows_of(k)
                        g = [g for g in GROUPS if k in g][0]
                        col = (k - g[0]) * P
                        for chunks in (range(0, 4), range(4, KC)):
                            t, read, _ = tb.take()
                            high_part()
                            n = len(chunks)
                            part = (slice(None), slice(chunks[0], chunks[0] + n), slice(col, col + r))
                            low(pt_l[part], t[:, 0:n * P].rearrange("p (c q) -> p c q", c=n)[:, :, 0:r],
                                pt_h[part]).then_inc(read, 1)
                    elif what == "Z":
                        zb.take()
                    elif what == "V":
                        lo = GROUPS[k][0] * P
                        z, read, n = zb.take()
                        dve.wait_ge(s_zb, n)
                        for h, c0, c1 in segments(GROUPS[k]):
                            last = dve.tensor_scalar(ot[:, c0:c1], z[:, c0 - lo:c1 - lo],
                                                     bv[:, h:h + 1], None, ALU.add)
                        last.then_inc(read, 1)
                    elif what == "Y":
                        z, read, n = zb.take()
                        dve.wait_ge(s_zb, n)
                        dve.wait_ge(s_x1l, b * 16 + 16)
                        dve.wait_ge(s_x2out, b * 16 + 16)
                        ch.add(dve.tensor_tensor(x2b[0:T, :], z[0:T, :], x1b[0:T, :], ALU.add))
                        ch.join()
                        dve.sem_inc(read, 1)
                        dve.sem_inc(s_x2, 1)
                    elif what == "L":
                        (rows_stats, rows_norm)[k](b)
                    elif what == "R" and k == 0:
                        ch.add(dve.bn_stats(stx[0:T, :], x2b[0:T, :]))
                        ch.join()
                        dve.sem_inc(s_apart, 1)
                        ch.add(dve.bn_aggr(mvx[0:T, :], stx[0:T, :]))
                        ch.join()
                        ch.add(dve.tensor_copy(rbuf[0:T, 0:1], mvx[0:T, 0:1]))
                        ch.add(dve.tensor_copy(rsx[0:T, 0:1], mvx[0:T, 1:2]))
                        tally(s_mvx)
                    elif what == "R" and k == 1:
                        dve.wait_ge(s_rsx, b + 1)
                        ch.add(dve.tensor_scalar(x3b[0:T, :], x2b[0:T, :], rbuf[0:T, 0:1], rbuf[0:T, 1:2],
                                                 ALU.subtract, ALU.mult))
                        tally(s_x3)
                    elif what == "R" and k == 2:
                        router_bank[0] = tb.take()
                    elif what == "R" and k == 3:
                        t, read, _ = router_bank[0]
                        dve.wait_ge(s_lp, b + 1)
                        ch.add(dve.tensor_tensor(rbuf[0:T, 2:NREC], t[0:T, ND * T:ND * T + E], brb[0:T, :], ALU.add))
                        ch.join()
                        dve.sem_inc(read, 1)
                        ch.add(dve.tensor_copy(rec[0:T, bass.ds(b, 1), :], rbuf[0:T, :].unsqueeze(1)))

            router_bank = [None]

            def batch(b, events):
                tb.at(b, TB_USES, TB0)
                zb.at(b, ZB_USES, 0)
                hi[0], hi[1] = HI0, b
                steps(run, b, events)

            split_at = first.index(("S", 0))
            run(0, first[:split_at])
            dve.wait_ge(s_qout[1], 16 * HALF)
            for k in range(3):
                ch.add(dve.memset(pr[k][:], 0.0))
            tally(s_padp)
            run(0, first[split_at:])
            batches(dve, batch, ch, DVE_B)

            def low_weights(n, q):
                dve.wait_ge(s_wh, n * NW + q + 1)
                low(wsl[q % 4][:], stage[q % 4][:], wsh[q % 4][:]).then_inc(s_wl, 1)

            run(B, [("R", 0)])
            low_weights(0, 0)
            run(B, [("R", 1)])
            low_weights(0, 1)
            run(B, [("R", 2), ("R", 3)])
            ch.join()

            dve.wait_ge(s_x2out, 16 * (B + 1))
            t = slice(0, T)
            be = "p b e -> p (b e)"
            lg = rec[t, 1:B + 1, 2:NREC]
            ch.add(dve.reduce_max(lmx[t, :], lg, AX))
            tally(s_lm)
            for b in range(B):
                ch.add(dve.tensor_scalar(eq[t, b, :], lg[:, b, :], lmx[t, b:b + 1], None, ALU.is_ge))
            ch.join()
            ch.add(dve.tensor_tensor(eq[t].rearrange(be), eq[t].rearrange(be), desc[t].rearrange(be), ALU.mult))
            ch.join()
            ch.add(dve.reduce_max(kmx[t, :], eq[t], AX))
            ch.join()
            for b in range(B):
                ch.add(dve.tensor_scalar(oh[t, b, :], desc[t, b, :], kmx[t, b:b + 1], None, ALU.is_equal))
            tally(s_oh)
            low_weights(0, 2)
            dve.wait_ge(s_rk, 1)
            ch.add(dve.tensor_tensor(tmp[t].rearrange(be), bank[0][t, 0:B * E], oh[t].rearrange(be), ALU.mult))
            ch.add(dve.tensor_copy(cnt[:], bank[1][:, 0:E]))
            ch.join()
            ch.add(dve.reduce_sum(rank[t, :], tmp[t], AX))
            for j in range(NOV):
                ch.add(dve.tensor_scalar(cmp_[:, j, :], cnt[:], float(TILE * (j + 1)), None, ALU.is_gt))
            ch.join()
            ch.add(dve.reduce_sum(ovc[:], cmp_[:].rearrange("p j e -> p e j"), AX))
            ch.add(dve.tensor_tensor(tmp[t].rearrange(be), eid[t].rearrange(be), oh[t].rearrange(be), ALU.mult))
            for j in range(NOV):
                ch.add(dve.tensor_scalar(cmr[t, j, :], rank[t, :], float(TILE * (j + 1)), None, ALU.is_ge))
            ch.join()
            ch.add(dve.reduce_sum(jt[t, :], cmr[t].rearrange("p j b -> p b j"), AX))
            ch.add(dve.reduce_sum(pa[t, :], tmp[t], AX))
            ch.add(dve.tensor_tensor_scan(ove[:], ones8[:], ovc[:], 0.0, ALU.mult, ALU.add))
            ch.join()
            ch.add(dve.tensor_tensor(ovb[:], ove[:], ovc[:], ALU.subtract))
            ch.add(dve.scalar_tensor_tensor(pin[t, :], jt[t, :], -float(TILE), rank[t, :], ALU.mult, ALU.add))
            ch.join()
            for b in range(B):
                ch.add(dve.tensor_tensor(tmp[t, b, :], oh[t, b, :], ovb[t, :], ALU.mult))
                ch.add(dve.tensor_scalar(ohp[t, b, :], iota[t, :], pin[t, b:b + 1], None, ALU.is_equal))
            ch.join()
            ch.add(dve.reduce_sum(pb[t, :], tmp[t], AX))
            ch.join()
            ch.add(dve.scalar_tensor_tensor(pb[t, :], pb[t, :], float(E - 1), jt[t, :], ALU.add, ALU.add))
            ch.join()
            ch.add(dve.tensor_tensor(pb[t, :], pb[t, :], pa[t, :], ALU.subtract))
            ch.join()
            ch.add(dve.tensor_tensor(pb[t, :], pb[t, :], cmr[t, 0, :], ALU.mult))
            ch.join()
            ch.add(dve.tensor_tensor(pb[t, :], pb[t, :], pa[t, :], ALU.add))
            ch.add(dve.tensor_copy(vals[t, :, 0], tokv[t, :]))
            ch.add(dve.tensor_copy(vals[t, :, 1:3], rec[t, 1:B + 1, 0:2]))
            ch.join()
            for b in range(B):
                ch.add(dve.tensor_scalar(ohs[t, b, :], iota[t, 0:NSLOT], pb[t, b:b + 1], None, ALU.is_equal))
            ch.join()
            dve.wait_ge(s_gate, 1)
            ch.add(dve.tensor_tensor(ohv[t], ohs[t].unsqueeze(2).broadcast_to([T, B, 4, NSLOT]),
                                     vals[t].unsqueeze(3).broadcast_to([T, B, 4, NSLOT]), ALU.mult))
            tally(s_ohv)
            for k in range(NOV):
                ch.add(dve.tensor_scalar(cmp_[:, k, :], ove[:], float(k), None, ALU.is_le))
            ch.join()
            ch.add(dve.reduce_sum(ek[:, 0:NOV], cmp_[:], AX))
            ch.join()
            ch.add(dve.tensor_scalar(ek[:, 0:NOV], ek[:, 0:NOV], float(E - 1), None, ALU.min))
            ch.add(dve.tensor_copy(ek[:, 7:8], ove[:, E - 1:E]))
            ch.add(dve.memset(ek[:, 6:7], 0.0))
            ch.join()
            ch.add(dve.tensor_copy(ctl[:], ek[:]))
            tally(s_ctl)
            low_weights(0, 3)
            dve.wait_ge(s_tp, 1)
            ch.add(dve.tensor_scalar(idx[:], bank[2][:, 0:NSLOT], float(NTOK), None, ALU.add))
            tally(s_idx)
            ch.add(dve.tensor_copy(sm[:].rearrange("p s v -> p v s"),
                                   bank[2][:, 0:4 * NSLOT].rearrange("p (v s) -> p v s", v=4)))
            ch.join()

            dve.sem_inc(s_yo, 1)

            def norm_tokens(n):
                ch.add(dve.tensor_copy(cur[:], sm[:, bass.ds(n, 1), :].rearrange("p o v -> p (o v)")))
                ch.join()
                dve.wait_ge(s_gat, n * 16 + 16)
                ch.add(dve.tensor_scalar(x3g[:], gat[:], cur[:, 1:2], cur[:, 2:3], ALU.subtract, ALU.mult))
                tally(s_x3g)

            def keep_tokens(n):
                ch.add(dve.tensor_copy(x2g[:], gat[:]))
                ch.add(dve.tensor_copy(pg[:], cur[:, 3:4]))
                tally(s_gfree)

            def split_tokens(n):
                dve.wait_ge(s_xth, n + 1)
                low(xg_l[:], bank[4][:].rearrange("p (c t) -> p c t", c=ND), xg_h[:]).then_inc(s_xtl, 1)

            def slot(n, more):
                for what, k in slot_plan:
                    if what == "G":
                        dve.wait_ge(s_xtp, n + 1)
                        norm_tokens(n + 1)
                    elif what == "K":
                        dve.wait_ge(s_yo, n + 2)
                        keep_tokens(n + 1)
                    elif what == "W":
                        with only_if(dve, more if k >= 4 else None):
                            low_weights(n, k + 4)
                    elif what == "X":
                        split_tokens(n + 1)
                    elif what == "H":
                        dve.wait_ge(s_hth, n * NF + k + 1)
                        low(ht_l[k % 2][:], bank[2 + k % 2][:].rearrange("p (c t) -> p c t", c=4), ht_h[k % 2][:]
                            ).then_inc(s_htl, 1)
                    elif what == "R":
                        dve.wait_ge(s_yp, n * NF + NF)
                        dve.wait_ge(s_yofree, n + 1)
                        dve.scalar_tensor_tensor(yo[:], bank[6][:], pg[:], x2g[:], ALU.mult, ALU.add
                                                 ).then_inc(s_yo, 1)

            norm_tokens(0)
            keep_tokens(0)
            split_tokens(0)
            slots(dve, slot, ch, 4)


def kernel(**inputs):
    from concourse import bacc
    from concourse.bass_utils import run_bass_kernel_spmd

    src = {k: np.ascontiguousarray(v) for k, v in inputs.items()}
    t = np.ascontiguousarray
    arrays = {
        "x": src["x"], "ctx": src["ctx_1024"],
        "WiT": t(src["L0_attn_Wi"].T), "WgT": t(src["L0_attn_Wg"].T), "WoT": t(src["L0_attn_Wo"].T),
        "ab": t(np.stack([src["L0_attn_bi"], src["L0_attn_bg"]]).reshape(2, ND, P).transpose(2, 0, 1)),
        "bo_a": src["L0_attn_bo"],
        "gm": src["L0_xattn_gamma_media"], "bm": src["L0_xattn_beta_media"],
        "gl": src["L0_xattn_gamma_lat"], "bl": src["L0_xattn_beta_lat"],
        "Wq": src["L0_xattn_Wq"], "bq": t(src["L0_xattn_bq"].reshape(HEADS, P).T),
        "WkT": t(src["L0_xattn_Wkv"][:, :INNER].T), "Wv": t(src["L0_xattn_Wkv"][:, INNER:]),
        "bk": t(src["L0_xattn_bkv"][:INNER].reshape(HEADS, P).T),
        "bv": t(src["L0_xattn_bkv"][INNER:].reshape(HEADS, P).T), "Wo_x": src["L0_xattn_Wo"], "bo_x": src["L0_xattn_bo"],
        "Wr": src["L0_ffn_Wr"], "br": src["L0_ffn_br"], "W1": src["L0_ffn_W1"], "W2": src["L0_ffn_W2"],
        "ident": np.eye(P, dtype=np.float32),
        "phalf": np.full((P, 16), -0.5, np.float32),
        "desc": np.broadcast_to(np.arange(E, 0, -1, dtype=np.float32), (P, B, E)).copy(),
        "eid": np.broadcast_to(np.arange(E, dtype=np.float32), (P, B, E)).copy(),
        "tokv": np.arange(-NTOK, 0, dtype=np.float32).reshape(B, T).T.copy(),
        "upper": np.triu(np.ones((P, P), np.float32), 1),
        "ones": np.ones((P, P), np.float32),
        "iota": np.broadcast_to(np.arange(P, dtype=np.float32), (P, P)).copy(),
    }
    nc = bacc.Bacc("TRN2", target_bir_lowering=False, num_devices=1)
    aps, feed = {}, {}
    for name, arr in arrays.items():
        feed[f"in_{name}"] = arr
        aps[name] = nc.dram_tensor(f"in_{name}", arr.shape, mybir.dt.from_np(arr.dtype), kind="ExternalInput").ap()
    out = nc.dram_tensor("out", (B, T, D), F32, kind="ExternalOutput").ap()
    build(nc, aps, out.rearrange("b t d -> (b t) d"))
    result = run_bass_kernel_spmd(nc, [feed], core_ids=[0])
    return result.results[0]["out"]
```

```python
from contextlib import ExitStack

import numpy as np

import concourse.bass as bass
from concourse import mybir
from concourse.alu_op_type import AluOpType as ALU

F32 = mybir.dt.float32
F32R = mybir.dt.float32r
I32 = mybir.dt.int32
ACT = mybir.ActivationFunctionType
AX = mybir.AxisListType.X

B, T, D = 8, 100, 512
MEDIA = 722
HEADS, DH = 8, 128
INNER = HEADS * DH
FFN, E = 2048, 8
P = 128
ND = D // P
NTOK = B * T
EPS = 1e-5

HALF = 4
HT = HALF * T

MC = -(-MEDIA // P)
KC = MC + 1
MLAST = MEDIA - (MC - 1) * P
KEYS = MEDIA + T
KPAD = KC * P
SH = [412, KEYS - 412]
ROWS = HEADS * T
RT = -(-ROWS // P)
RLAST = ROWS - (RT - 1) * P
GROUPS = [[0, 1], [2, 3], [4, 5, 6]]
GW = 2 * P + RLAST

TILE = 128
NOV = NTOK // TILE
NSLOT = E + NOV + 1
N_CA, N_WB, N_CC = 9, 2, 12
POOL_B, DVE_B = 4 + 2 * MC, 56
FC = 512
NF = FFN // FC
NREC = 2 + E


def rows_of(tile):
    return RLAST if tile == RT - 1 else P


def segments(group):
    lo = group[0] * P
    hi = min(ROWS, (group[-1] + 1) * P)
    out = []
    while lo < hi:
        end = min(hi, (lo // T + 1) * T)
        out.append((lo // T, lo, end))
        lo = end
    return out


class Chain:

    def __init__(self, eng, sem):
        self.eng, self.sem, self.n, self.turn, self.per = eng, sem, 0, None, 0

    def add(self, ins):
        ins.then_inc(self.sem, 1)
        self.n += 1
        return ins

    def join(self):
        v = self.n if self.turn is None else self.turn * self.per + self.n
        self.eng.wait_ge(self.sem, v)

    def enter(self, turn, per):
        self.turn, self.per, self.start = turn, per, self.n

    def leave(self, turns):
        self.again()
        self.n = self.start + turns * self.per

    def again(self):
        assert self.n - self.start == self.per, (self.n - self.start, self.per)
        self.n, self.turn = self.start, None


class Ring:

    def __init__(self, banks, read, begin):
        self.banks, self.read, self.begin, self.n, self.turn, self.per = banks, read, begin, 0, 0, 0

    def at(self, turn, per, first):
        assert per % 2 == 0
        self.turn, self.per, self.n = turn, per, first

    def take(self):
        k = self.n % 2
        self.n += 1
        return self.banks[k], self.read[k], self.turn * self.per + self.n

    def free(self, eng):
        v = self.turn * (self.per // 2) + self.n // 2 + self.begin
        if not isinstance(v, int) or v > 0:
            eng.wait_ge(self.read[self.n % 2], v)

    def all_read(self, eng):
        for k in range(2):
            eng.wait_ge(self.read[k], self.turn * (self.per // 2) + (self.n + 1 - k) // 2 + self.begin)


class Memory:

    def __init__(self, nc):
        self.nc = nc
        self.at = -(-nc.sbuf_base // 64) * 64
        self.end = nc.sbuf_usable_end
        self.placed = []

    def __call__(self, name, shape, dtype=F32):
        size = int(np.prod(shape[1:])) * 4
        t = self.nc.alloc_sbuf_tensor_at(name, shape, dtype, offset=self.at)
        self.placed.append((t, self.at))
        self.at += -(-size // 64) * 64
        assert self.at <= self.end, (name, self.at, self.end)
        return t

    def over(self, other, name, shape, dtype=F32):
        at = [at for t, at in self.placed if t is other][0]
        return self.nc.alloc_sbuf_tensor_at(name, shape, dtype, offset=at)


def build(nc, a, out):
    mem = Memory(nc)
    ctx = ExitStack()

    def sem(name):
        return ctx.enter_context(nc.semaphore(name))

    bank = [ctx.enter_context(nc.psum_tensor(f"bank{k}", [P, 512], F32)) for k in range(8)]

    def dram(name, shape, dtype=F32):
        return nc.dram_tensor(name, shape, dtype, kind="Internal").ap()

    d_ln = dram("scr_latents", (B, T, D))
    d_x1 = dram("scr_x1", (B, T, D))
    d_q = dram("scr_q", (B, P, ROWS))
    d_c = dram("scr_c", (B, ROWS))
    d_tok = dram("scr_tokens", (NTOK + 1, D))

    ident = mem("ident", [P, P])
    phalf = mem("phalf", [P, 16])
    gm = mem("gm", [P, D])
    bm = mem("bm", [P, D])
    bv = mem("bv", [P, HEADS])
    bk = mem("bk", [P, HEADS])
    wr = mem("wr", [P, ND, E])
    raw_at = mem.at
    raw = mem("raw", [P, KC, D])
    mvr = mem("mvr", [P, MC, 2])
    rsr = mem("rsr", [P, MC])
    brb = mem("brb", [P, E])
    rec = mem("rec", [P, B + 1, NREC])
    str_ = mem("str_", [P, MC, 6])
    desc = mem("desc", [P, B, E])
    eid = mem("eid", [P, B, E])
    ones8 = mem("ones8", [P, E])
    inner = mem("inner", [P, E, B])
    sizes = mem("sizes", [P, NOV])
    tokv = mem("tokv", [P, B])
    iota = mem("iota", [P, P])
    before = mem("before", [P, P])
    ones = mem("ones", [P, P])
    base = mem.at

    wk = mem("wk", [P, HEADS, D])
    wv = mem("wv", [P, ND, INNER])
    wo = mem("wo", [P, HEADS, D])
    base_b = mem.at
    xn_h = mem("xn_h", [P, KC, D], F32R)
    xn_l = mem("xn_l", [P, KC, D], F32R)
    xt_h = mem("xt_h", [P, ND, KEYS + 2], F32R)
    xt_l = mem("xt_l", [P, ND, KEYS + 2], F32R)
    qt_h = mem("qt_h", [P, ND, RT * P], F32R)
    qt_l = mem("qt_l", [P, ND, RT * P], F32R)
    pr = [mem(f"pr{k}", [P, KPAD]) for k in range(3)]
    pt_h = mem("pt_h", [P, KC, GW], F32R)
    pt_l = mem("pt_l", [P, KC, GW], F32R)
    zt = mem("zt", [P, ND, GW])
    qb = mem("qb", [P, ROWS])
    ot = mem("ot", [P, ROWS])
    x1b = mem("x1b", [P, D])
    x2b = mem("x2b", [P, D])
    x3b = mem("x3b", [P, D])
    x3t = mem("x3t", [P, ND, T])
    cqn = mem("cqn", [P, RT])
    cq = mem("cq", [P, RT])
    stx = mem("stx", [P, 6])
    rbuf = mem("rbuf", [P, NREC])
    mvx = mem("mvx", [P, 2])
    rsx = mem("rsx", [P, 2])
    smx = mem("smx", [P, 6])
    rsm = mem("rsm", [P, 8])

    mem.at = base
    w3 = [mem(f"w3_{k}", [P, ND, D]) for k in range(3)]
    w3_h = [mem(f"w3_h{k}", [P, ND, D], F32R) for k in range(3)]
    w3_l = [mem.over(w3[k], f"w3_l{k}", [P, ND, D], F32R) for k in range(3)]
    crow = mem.over(w3_h[1], "crow", [P, HEADS, HALF, T])
    mem.at = base_b
    xin = mem("xin", [P, B, D])
    xh = mem("xh", [P, B, D])
    hs = mem("hs", [P, ND, NTOK])
    hs_h = mem("hs_h", [P, ND, NTOK], F32R)
    hs_l = mem.over(hs, "hs_l", [P, ND, NTOK], F32R)
    boa = mem.over(hs_h, "boa", [P, D])
    wq = mem("wq", [P, ND, INNER])
    wq_h = mem("wq_h", [P, ND, INNER], F32R)
    wq_l = mem.over(wq, "wq_l", [P, ND, INNER], F32R)
    qa = mem("qa", [P, HEADS, HALF, T])
    mem.at -= HEADS * HALF * T * 4
    ug = [mem(f"ug{k}", [P, NTOK]) for k in range(2)]
    gg = [mem(f"gg{k}", [P, NTOK]) for k in range(2)]
    xa_h = mem("xa_h", [P, ND, NTOK], F32R)
    xa_l = mem("xa_l", [P, ND, NTOK], F32R)
    og = mem("og", [P, NTOK])
    gl = mem("gl", [P, D])
    bl = mem("bl", [P, D])
    box = mem("box", [P, D])
    ab = mem("ab", [P, 2, ND])
    bq = mem("bq", [P, HEADS])
    bqs = mem("bqs", [P, HEADS])
    sta = mem("sta", [P, B, 6])
    mva = mem("mva", [P, 3, B, 2])
    rsa = mem("rsa", [P, 3, B])

    mem.at = base
    stage = [mem(f"stage{k}", [P, 4, FC]) for k in range(4)]
    xg_h = mem("xg_h", [P, ND, TILE], F32R)
    xg_l = mem("xg_l", [P, ND, TILE], F32R)
    ht_h = [mem(f"ht_h{k}", [P, 4, TILE], F32R) for k in range(2)]
    ht_l = [mem(f"ht_l{k}", [P, 4, TILE], F32R) for k in range(2)]
    ohp = mem("ohp", [P, B, P])
    wsh, wsl = [], []
    for k in range(8):
        wsh.append(mem(f"wsh{k}", [P, 4, FC], F32R))
        wsl.append(mem(f"wsl{k}", [P, 4, FC], F32R))
    after = mem.at
    mem.at = raw_at
    gat = mem("gat", [P, D])
    x3g = mem("x3g", [P, D])
    x2g = mem("x2g", [P, D])
    yo = mem("yo", [P, D])
    hid = [mem(f"hid{k}", [P, FC]) for k in range(2)]
    mem.at = after
    cur = mem("cur", [P, 4])
    pg = mem("pg", [P, 1])
    idx = mem("idx", [P, NSLOT], I32)
    sm = mem("sm", [P, NSLOT, 4])
    idc = mem("idc", [P, 2], I32)
    ctl = mem("ctl", [P, 2, E], I32)
    lmx = mem("lmx", [P, B])
    eq = mem("eq", [P, B, E])
    kmx = mem("kmx", [P, B])
    oh = mem("oh", [P, B, E])
    tmp = mem("tmp", [P, B, E])
    rank = mem("rank", [P, B])
    pin = mem("pin", [P, B])
    jt = mem("jt", [P, B])
    pb = mem("pb", [P, B])
    cmr = mem("cmr", [P, NOV, B])
    cmp_ = mem("cmp_", [P, NOV, E])
    ovc = mem("ovc", [P, E])
    upto = mem("upto", [P, E, B])
    ove = mem("ove", [P, E])
    ovb = mem("ovb", [P, E])
    slot_of = mem("slot_of", [P, 2, E])
    vals = mem("vals", [P, B, 4])
    ohs = mem("ohs", [P, B, NSLOT])
    ohv = mem("ohv", [P, B, 4, NSLOT])

    s_x = [sem(f"s_xin{b}") for b in range(B)]
    s_w3 = [sem(f"s_w3_{k}") for k in range(3)]
    s_id, s_wk = sem("s_id"), sem("s_wk")
    s_ca, s_wq, s_wb, s_cc, s_zout = sem("s_ca"), sem("s_wq"), sem("s_wb"), sem("s_cc"), sem("s_zout")
    s_dve, s_pool = sem("s_dve"), sem("s_pool")
    s_mva, s_rsa, s_xha, s_tpa, s_tea = sem("s_mva"), sem("s_rsa"), sem("s_xha"), sem("s_tpa"), sem("s_tea")
    s_wah, s_wal, s_wil, s_tha, s_hsh, s_hsl = (sem(n) for n in ("s_wah", "s_wal", "s_wil", "s_tha", "s_hsh", "s_hsl"))
    s_lnout, s_bqs, s_padq, s_padp = sem("s_lnout"), sem("s_bqs"), sem("s_padq"), sem("s_padp")
    s_ugp, s_ugs, s_hsc, s_xr = sem("s_ugp"), sem("s_ugs"), sem("s_hsc"), sem("s_xr")
    s_op, s_x1, s_lnr, s_x1r = sem("s_op"), sem("s_x1"), sem("s_lnr"), sem("s_x1r")
    s_tpl, s_tel, s_qp, s_qe, s_out_a = sem("s_tpl"), sem("s_tel"), sem("s_qp"), sem("s_qe"), sem("s_out_a")
    s_qout = [sem("s_qout0"), sem("s_qout1")]
    s_apart = sem("s_apart")
    s_rawz, s_lat = sem("s_rawz"), sem("s_lat")
    s_cp, s_ce, s_cout = sem("s_cp"), sem("s_ce"), sem("s_cout")
    s_raw, s_rawfree, s_mvr, s_rsr, s_apr, s_ln = (sem(n) for n in (
        "s_raw", "s_rawfree", "s_mvr", "s_rsr", "s_apr", "s_ln"))
    s_qb, s_qbfree, s_x1l, s_x2, s_x2out, s_cq, s_cqfree = (sem(n) for n in (
        "s_qb", "s_qbfree", "s_x1l", "s_x2", "s_x2out", "s_cq", "s_cqfree"))
    s_tb, s_zb = sem("s_tb"), sem("s_zb")
    s_tread, s_zread = [sem("s_tread0"), sem("s_tread1")], [sem("s_zread0"), sem("s_zread1")]
    s_hi, s_xnh, s_xnl, s_s, s_nb, s_exp, s_p, s_qk, s_qread = (sem(n) for n in (
        "s_hi", "s_xnh", "s_xnl", "s_s", "s_nb", "s_exp", "s_p", "s_qk", "s_qread"))
    s_mvx, s_rsx, s_x3, s_x3t, s_lp = (sem(n) for n in ("s_mvx", "s_rsx", "s_x3", "s_x3t", "s_lp"))
    s_lm, s_gate, s_oh, s_rk, s_ohv, s_tp, s_idx, s_ctl = (sem(n) for n in (
        "s_lm", "s_gate", "s_oh", "s_rk", "s_ohv", "s_tp", "s_idx", "s_ctl"))
    s_w = [sem(f"s_w{k}") for k in range(4)]
    s_wh, s_wl, s_wlp, s_vused = sem("s_wh"), sem("s_wl"), sem("s_wlp"), sem("s_vused")
    s_gat, s_gfree, s_x3g, s_xtp, s_xth, s_xtl = (sem(n) for n in (
        "s_gat", "s_gfree", "s_x3g", "s_xtp", "s_xth", "s_xtl"))
    s_hp, s_gelu, s_htp, s_hth, s_htl, s_yp, s_yo, s_out, s_yofree = (sem(n) for n in (
        "s_hp", "s_gelu", "s_htp", "s_hth", "s_htl", "s_yp", "s_yo", "s_out", "s_yofree"))

    def bc(vec, n, parts=P):
        return vec.rearrange("(o n) -> o n", o=1).broadcast_to([parts, n])

    plan = [("PT", 1), ("S", 2), ("R", 0), ("Z", (0, 0)), ("Z", (0, 1)), ("N", 2), ("L+", 0), ("S", 3), ("Z", (0, 2)),
            ("N", 3), ("Z", (0, 3)), ("PT", 2), ("V", 0), ("PT", 3), ("S", 4), ("R", 1), ("Z", (1, 0)), ("N", 4),
            ("Z", (1, 1)), ("L+", 1), ("R", 2), ("S", 5), ("R", 3), ("N", 5), ("S", 6), ("Z", (1, 2)), ("Z", (1, 3)),
            ("N", 6), ("PT", 4), ("V", 1), ("PT", 5), ("Q+", 0), ("Q+", 1), ("PT", 6), ("Q+", 2), ("Q+", 3),
            ("Z", (2, 0)), ("T+", 0), ("T+", 1), ("Z", (2, 1)), ("T+", 2), ("T+", 3), ("Q+", 4), ("Z", (2, 2)),
            ("T+", 4), ("T+", 5), ("Q+", 5), ("Q+", 6), ("T+", 6), ("Q+", 7), ("Z", (2, 3)), ("S+", 0), ("X+", 0),
            ("X+", 1), ("V", 2), ("N+", 0), ("S+", 1), ("X+", 2), ("X+", 3), ("N+", 1), ("PT+", 0), ("Y", 0),
            ("X+", 4), ("X+", 5), ("X+", 6)]
    first = []
    for what, k in plan:
        if what in ("T+", "Q+", "S+", "N+", "PT+"):
            first.append((what[:-1], k))
        if what == "T+":
            first.append(("X", k))
    TB0, HI0 = KC + 2, KC + 2 * ND + 2
    TB_USES = KC + 2 * RT + 1
    ZB_USES = 3 * (ND + 1) + 1
    HI_USES = KC + 2 * ND + 2 * RT
    qbank = [bank[2], bank[3], bank[0], bank[1]]
    s_pair = [(bank[0], bank[1]), (bank[2], bank[3])]
    tbank, zbank = (bank[4], bank[5]), (bank[6], bank[7])

    def rings():
        return Ring(tbank, s_tread, 0), Ring(zbank, s_zread, 1)

    def batches(eng, body, chain=None, per=0):
        with eng.Fori(0, B - 1) as b:
            if chain:
                chain.enter(b, per)
            body(b, plan)
            if chain:
                chain.leave(B - 1)
        body(B - 1, [e for e in plan if e[0][-1] != "+"])

    def steps(run, b, events):
        for what, k in events:
            if what[-1] == "+":
                run(b + 1, [(what[:-1], k)])
            else:
                run(b, [(what, k)])

    def tcols(c):
        return (c * P, min(P, MEDIA - c * P)) if c < MC else (MEDIA, T)

    def weights_a(k, three, q):
        return three[k][:] if k < 3 else q[:, (k - 3) * ND // 2:(k - 2) * ND // 2, :]

    norms = [("A", 0), ("A", 1), ("B", 0), ("B", 1), ("C", 0), ("C", 1)] + [("H", b) for b in range(HALF)]
    norms += [("A", 2), ("A", 3), ("B", 2), ("B", 3), ("C", 2), ("C", 3)]
    norms += [("H", b) for b in range(HALF, B)]
    obank = [bank[6], bank[7], bank[0], bank[1], bank[2], bank[3], bank[6], bank[7]]
    stds = [e for e in norms if e[0] in "AB"]

    slot_plan = [("M", 0), ("W", 0), ("M", 1), ("H", 0), ("W", 1), ("M", 2), ("H", 1), ("W", 2), ("O", 0), ("W", 3),
                 ("G", 1), ("M", 3), ("H", 2), ("W", 4), ("O", 1), ("X", 1), ("H", 3), ("W", 5), ("O", 2), ("W", 6),
                 ("O", 3), ("R", 0), ("K", 1), ("W", 7)]
    pieces = [(1, 0), (1, 1), (1, 2), (2, 0), (1, 3), (2, 1), (2, 2), (2, 3)]
    piece_of = {p: n for n, p in enumerate(pieces)}
    NW = len(pieces)
    last_expert = E - 1

    def slots(eng, body, chain=None, per=0):
        eng.wait_ge(s_ctl, 1)

        def run(n, e, last):
            if chain:
                chain.enter(n, per)
            body(n, e, last)
            if chain:
                chain.again()

        def expert(e):
            at = (lambda r: ctl[0:1, r, e:e + 1]) if isinstance(e, int) else (lambda r: ctl[0:1, r, bass.ds(e, 1)])
            n0 = eng.value_load(at(0), min_val=0, max_val=NSLOT - 2)
            n1 = eng.value_load(at(1), min_val=0, max_val=NSLOT - 2)
            with eng.If(n0 < n1):
                with eng.Fori(0, NOV) as k:
                    with eng.If(n0 + k < n1):
                        run(nc.s_assert_within(n0 + k, 0, NSLOT - 3, skip_runtime_bounds_check_because=
                                               "it is less than n1, an expert's last slot"), e, False)
            run(n1, e, True)
            return n1

        with eng.Fori(0, E - 1) as e:
            expert(e)
        return expert(E - 1)

    def w_src(which, e, f):
        if which == 1:
            return a["W1"][e].rearrange("(k p) f -> p k f", p=P)[:, :, f * FC:(f + 1) * FC]
        return a["W2"][e, f * FC:(f + 1) * FC, :].rearrange("(k p) n -> p k n", p=P)

    def split_products(pe, dest, pairs, start, stop):
        n = len(pairs)
        for k, ((lh, ll), (rh, rl)) in enumerate(pairs):
            pe.matmul(dest, lh, rh, start=start and k == 0, stop=False)
            pe.matmul(dest, lh, rl, start=False, stop=False)
            last = pe.matmul(dest, ll, rh, start=False, stop=stop and k == n - 1)
        return last

    with ctx:
        block = ctx.enter_context(nc.Block())

        @block.sync
        def _(sp):
            def load_queries(b):
                sp.dma_start(qb[:], d_q[b]).then_inc(s_qb, 16)

            def load_bias_rows(b):
                m = (RT - 1) * P
                sp.dma_start(cqn[:, 0:RT - 1], d_c[b, 0:m].rearrange("(i p) -> p i", p=P),
                             allow_slow_non_contiguous=True).then_inc(s_cq, 16)
                sp.dma_start(cqn[0:RLAST, RT - 1:RT], d_c[b, m:ROWS].rearrange("(p o) -> p o", o=1)).then_inc(s_cq, 16)

            for b in range(B):
                sp.dma_start(xin[0:T, b, :], a["x"][b]).then_inc(s_x[b], 16)
            loads_a = [(ident[:], a["ident"]), (phalf[:], a["phalf"]), (boa[:], bc(a["bo_a"], D)),
                       (ab[:], a["ab"]), (bq[:], a["bq"]), (gl[:], bc(a["gl"], D)), (bl[:], bc(a["bl"], D)),
                       (box[:], bc(a["bo_x"], D)), (gm[:], bc(a["gm"], D)), (bm[:], bc(a["bm"], D)), (bk[:], a["bk"])]
            assert len(loads_a) - 2 == N_CA
            for dst, src in loads_a[:2]:
                sp.dma_start(dst, src).then_inc(s_id, 16)
            for k, name in enumerate(("WiT", "WgT", "WoT")):
                sp.dma_start(w3[k][:], a[name].rearrange("(c p) n -> p c n", p=P)).then_inc(s_w3[k], 16)
                if k == 1:
                    for dst, src in loads_a[2:]:
                        sp.dma_start(dst, src).then_inc(s_ca, 16)

            def load_context(b, turn):
                sp.dma_start(raw[:, 0:MC - 1, :], a["ctx"][b, 0:(MC - 1) * P, :].rearrange("(c p) d -> p c d", p=P)
                             ).then_inc(s_raw, 16)
                sp.dma_start(raw[0:MLAST, MC - 1, :], a["ctx"][b, (MC - 1) * P:MEDIA, :]).then_inc(s_raw, 16)

            sp.wait_ge(s_rawz, 1)
            load_context(0, 0)
            sp.dma_start(wq[:], a["Wq"].rearrange("(c p) n -> p c n", p=P)).then_inc(s_wq, 16)
            loads_c = [(desc[:], a["desc"]), (eid[:], a["eid"]), (tokv[0:T, :], a["tokv"]),
                       (before[:], a["before"]), (ones[:], a["ones"]), (ones8[:], a["ones"][:, 0:E]),
                       (inner[:], a["inner"]), (sizes[:], a["sizes"]),
                       (iota[:], a["iota"]), (brb[:], bc(a["br"], E)), (bv[:], a["bv"]),
                       (wr[:], a["Wr"].rearrange("(c p) e -> p c e", p=P))]
            for dst, src in loads_c:
                sp.dma_start(dst, src).then_inc(s_cc, 16)
            assert len(loads_c) == N_CC
            sp.wait_ge(s_op, B)
            sp.dma_start(wk[:], a["WkT"].rearrange("(h p) d -> p h d", p=P)).then_inc(s_wk, 16)
            for b in range(B):
                sp.wait_ge(s_lnr, b + 1)
                sp.dma_start(d_ln[b], xh[0:T, b, :]).then_inc(s_lnout, 16)
            sp.wait_ge(s_lnout, 16 * B)
            sp.dma_start(raw[0:T, MC, :], d_ln[0]).then_inc(s_lat, 16)
            for half in range(2):
                sp.wait_ge(s_qe, HEADS * (half + 1))
                if half:
                    load_queries(0)
                for bb in range(HALF):
                    sp.dma_start(d_q[half * HALF + bb].rearrange("p (h t) -> p h t", h=HEADS), qa[:, :, bb, :]
                                 ).then_inc(s_qout[half], 16)
                sp.wait_ge(s_ce, HEADS * (half + 1))
                for bb in range(HALF):
                    b = half * HALF + bb
                    sp.dma_start(d_c[b:b + 1, :].rearrange("o (h t) -> o h t", h=HEADS), crow[0:1, :, bb, :]
                                 ).then_inc(s_cout, 16)
                if not half:
                    for b in range(B):
                        sp.wait_ge(s_x1r, b + 1)
                        sp.dma_start(d_x1[b], xin[0:T, b, :]).then_inc(s_out_a, 16)
            sp.wait_ge(s_cout, 16 * B)
            sp.wait_ge(s_padq, 1)
            load_bias_rows(0)
            sp.dma_start(wv[:], a["Wv"].rearrange("(c p) n -> p c n", p=P)).then_inc(s_wb, 16)
            sp.dma_start(wo[:], a["Wo_x"].rearrange("(h p) n -> p h n", p=P)).then_inc(s_wb, 16)
            sp.wait_ge(s_out_a, 16 * B)
            sp.dma_start(d_tok[NTOK:NTOK + 1, :], x2b[0:1, :]).then_inc(s_zout, 16)
            sp.dma_start(x1b[0:T, :], d_x1[0]).then_inc(s_x1l, 16)
            sp.wait_ge(s_zout, 16)
            sp.sem_inc(s_x2out, 16)

            def batch(b, events):
                more = ("T+", 0) in events
                if more:
                    sp.wait_ge(s_rawfree, b + 1)
                    load_context(b + 1, b + 1)
                    sp.dma_start(raw[0:T, MC, :], d_ln[b + 1]).then_inc(s_lat, 16)
                    sp.wait_ge(s_qbfree, b + 1)
                    load_queries(b + 1)
                    sp.wait_ge(s_cqfree, b + 1)
                    load_bias_rows(b + 1)
                else:
                    sp.wait_ge(s_qbfree, B)
                    load_weights(0, 0, range(2))
                    sp.wait_ge(s_vused, 1)
                    load_weights(0, 0, range(2, 4))
                sp.wait_ge(s_x2, b + 1)
                sp.dma_start(d_tok[bass.ds(b * T, T), :], x2b[0:T, :]).then_inc(s_x2out, 16)
                if more:
                    sp.dma_start(x1b[0:T, :], d_x1[b + 1]).then_inc(s_x1l, 16)

            def load_weights(e, turn, chunks):
                for j in chunks:
                    which, f = pieces[j]
                    if j >= 6 and isinstance(turn, int):
                        sp.wait_ge(s_wlp, j - 5)
                    elif j >= 4 or not isinstance(turn, int):
                        sp.wait_ge(s_wl, turn * NW + j - 3)
                    sp.dma_start(stage[j % 4][:], w_src(which, e, f)).then_inc(s_w[j % 4], 16)

            batches(sp, batch)

            load_weights(0, 0, range(4, NW))
            sp.wait_ge(s_gat, 16)
            with sp.Fori(0, E - 1) as e:
                load_weights(e + 1, e + 1, range(NW))

        @block.gpsimd
        def _(pool):
            ch = Chain(pool, s_pool)
            pool.memset(raw[:], 0.0).then_inc(s_rawz, 1)

            def inv_std(dst, var, n, parts, made, at, done):
                pool.wait_ge(made, at)
                apart()
                ch.add(pool.tensor_scalar(dst, var, EPS, 0.0, ALU.add, ALU.add))
                ch.join()
                ch.add(pool.tensor_tensor(dst, dst, phalf[0:parts, 0:n], ALU.pow))
                ch.join()
                pool.sem_inc(done, 1)

            def apart():
                pool.sem_inc(s_apart, 1)

            def rows_std(turn):
                inv_std(rsr[:], mvr[:, :, 1], MC, P, s_mvr, turn + 1, s_rsr)

            def norm_rows(turn):
                for c in range(MC):
                    r = MLAST if c == MC - 1 else P
                    pool.wait_ge(s_apr, turn * MC + c + 1)
                    ch.add(pool.tensor_tensor(raw[0:r, c, :], raw[0:r, c, :], gm[0:r, :], ALU.mult))
                    ch.join()
                    ch.add(pool.tensor_tensor(raw[0:r, c, :], raw[0:r, c, :], bm[0:r, :], ALU.add))
                ch.join()
                pool.sem_inc(s_ln, 1)

            pool.wait_ge(s_id, 32)
            inv_std(rsa[0:T, 0, :], mva[0:T, 0, :, 1], B, T, s_mva, 1, s_rsa)
            def low_weight(k):
                pool.wait_ge(s_wah, k + 1)
                pool.tensor_tensor(weights_a(k, w3_l, wq_l), weights_a(k, w3, wq),
                                   weights_a(k, w3_h, wq_h).bitcast(F32),
                                   ALU.subtract).then_inc(s_wil, 1)

            low_weight(0)
            pool.wait_ge(s_ca, 16 * N_CA)
            for b in range(B):
                pool.wait_ge(s_xha, b + 1)
                pool.tensor_tensor(xin[0:T, b, :], xin[0:T, b, :], boa[0:T, :], ALU.add).then_inc(s_xr, 1)
            low_weight(2)
            low_weight(3)
            rows_std(0)
            low_weight(4)
            norm_rows(0)
            for n, (what, g) in enumerate(stds):
                k, bs = 1 + "AB".index(what), slice(2 * g, 2 * g + 2)
                inv_std(rsa[0:T, k, bs], mva[0:T, k, bs, 1], 2, T, s_mva, n + 2, s_rsa)
            pool.wait_ge(s_lnr, B)
            for b in range(B):
                pool.tensor_tensor(xin[0:T, b, :], xin[0:T, b, :], box[0:T, :], ALU.add).then_inc(s_x1r, 1)

            def router_std(turn):
                pool.wait_ge(s_mvx, turn + 1)
                apart()
                ch.add(pool.tensor_scalar(rsx[0:T, 1:2], rsx[0:T, 0:1], EPS, 0.0, ALU.add, ALU.add))
                ch.join()
                ch.add(pool.tensor_tensor(rbuf[0:T, 1:2], rsx[0:T, 1:2], phalf[0:T, 0:1], ALU.pow))
                ch.join()
                pool.sem_inc(s_rsx, 1)

            def run(b, events):
                for what, k in events:
                    if what == "R" and k == 0:
                        router_std(b)
                    elif what == "X":
                        pool.wait_ge(s_xnh, b * KC + k + 1)
                        pool.tensor_tensor(xn_l[:, k, :], raw[:, k, :], xn_h[:, k, :].bitcast(F32), ALU.subtract
                                           ).then_inc(s_xnl, 1)
                        if k == KC - 1:
                            pool.wait_ge(s_xnl, b * KC + KC)
                            pool.sem_inc(s_rawfree, 1)
                    elif what == "L" and k == 0:
                        rows_std(b)
                        norm_rows(b)

            run(0, first)
            batches(pool, lambda b, events: steps(run, b, events), ch, POOL_B)
            router_std(B)

            for q in range(2, 4):
                pool.wait_ge(s_wh, q + 1)
                pool.tensor_tensor(wsl[q][:], stage[q][:], wsh[q][:].bitcast(F32), ALU.subtract).then_inc(s_wlp, 1)
            pool.wait_ge(s_idx, 1)
            pool.wait_ge(s_x2out, 16 * (B + 1))
            pool.sem_inc(s_yofree, 1)

            def gather(n):
                if not isinstance(n, int) or n > 0:
                    pool.wait_ge(s_gfree, n)
                ch.add(pool.tensor_copy(idc[:, 0:1], idx[:, bass.ds(n, 1)]))
                ch.join()
                apart()
                pool.indirect_dma_start(
                    out=gat[:], out_offset=None, in_=d_tok,
                    in_offset=bass.IndirectOffsetOnAxis(ap=idc[:, 0:1], axis=0)).then_inc(s_gat, 16)

            def slot(n, e, last):
                gather(n + 1)
                ch.add(pool.tensor_copy(idc[:, 1:2], idx[:, bass.ds(n, 1)]))
                ch.join()
                pool.wait_ge(s_yo, n + 2)
                apart()
                pool.indirect_dma_start(
                    out=out, out_offset=bass.IndirectOffsetOnAxis(ap=idc[:, 1:2], axis=0),
                    in_=yo[:], in_offset=None, bounds_check=NTOK - 1, oob_is_err=False).then_inc(s_out, 16)
                pool.wait_ge(s_out, n * 16 + 16)
                pool.sem_inc(s_yofree, 1)

            gather(0)
            last_slot = slots(pool, slot, ch, 2)
            pool.wait_ge(s_gat, last_slot * 16 + 32)

        @block.tensor
        def _(pe):
            pe.wait_ge(s_id, 32)
            for b in range(B):
                pe.wait_ge(s_xha, b + 1)
                for c in range(ND):
                    last = pe.transpose(bank[b][:, c * T:(c + 1) * T], xh[0:T, b, c * P:(c + 1) * P],
                                        ident[0:T, 0:T])
                last.then_inc(s_tpa, 1)
            n = 0
            for e in range(ND):
                for w in range(2):
                    pe.wait_ge((s_wil, s_wal)[w], 1)
                    for half in range(2):
                        if n < 2:
                            pe.wait_ge(s_tea, (n + 1) * HALF)
                        if n >= 4:
                            pe.wait_ge(s_ugs, n - 3)
                        cols = slice(half * HT, (half + 1) * HT)
                        split_products(
                            pe, bank[n % 4][:, 0:HT],
                            [((w3_h[w][:, c, e * P:(e + 1) * P], w3_l[w][:, c, e * P:(e + 1) * P]),
                              (xa_h[:, c, cols], xa_l[:, c, cols])) for c in range(ND)], True, True).then_inc(s_ugp, 1)
                        n += 1
            pe.wait_ge(s_wil, 2)
            for b, chunks in ([(0, [0, 1, 2]), (1, [0, 1, 2]), (0, [3]), (1, [3])]
                              + [(b, range(ND)) for b in range(2, B)]):
                pe.wait_ge(s_hsl, chunks[-1] + 1)
                if 2 <= b < 6:
                    pe.wait_ge(s_ugs, 4 * ND)
                elif b >= 6:
                    pe.wait_ge(s_x1, b - 5)
                cols = slice(b * T, (b + 1) * T)
                last = split_products(pe, obank[b][0:T, :],
                                      [((hs_h[:, c, cols], hs_l[:, c, cols]), (w3_h[2][:, c, :], w3_l[2][:, c, :]))
                                       for c in chunks], chunks[0] == 0, chunks[-1] == ND - 1)
                if chunks[-1] == ND - 1:
                    last.then_inc(s_op, 1)
            pe.wait_ge(s_wil, 4)

            def latents(half):
                for bb in range(HALF):
                    b = half * HALF + bb
                    pe.wait_ge(s_lnr, b + 1)
                    if b >= 2:
                        pe.wait_ge(s_tel, b - 1)
                    for c in range(ND):
                        last = pe.transpose(tbank[b % 2][:, c * T:(c + 1) * T], xh[0:T, b, c * P:(c + 1) * P],
                                            ident[0:T, 0:T])
                    last.then_inc(s_tpl, 1)

            latents(0)
            for half in range(2):
                pe.wait_ge(s_tel, HALF * (half + 1))
                for h in range(HEADS):
                    n = half * HEADS + h
                    if n < 4:
                        pe.wait_ge(s_x1, n + 3)
                    if n >= 4:
                        pe.wait_ge(s_qe, n - 3)
                    cols = slice(half * HT, (half + 1) * HT)
                    split_products(
                        pe, bank[n % 4][:, 0:HT],
                        [((wq_h[:, c, h * P:(h + 1) * P], wq_l[:, c, h * P:(h + 1) * P]),
                          (xa_h[:, c, cols], xa_l[:, c, cols])) for c in range(ND)], True, True).then_inc(s_qp, 1)
                if not half:
                    latents(1)
                for h in range(HEADS):
                    n = half * HEADS + h
                    pe.wait_ge(s_qe, n + 1)
                    if n == 0:
                        pe.wait_ge(s_x1, B)
                    if n >= 2:
                        pe.wait_ge(s_ce, n - 1)
                    pe.matmul(zbank[n % 2][0:1, 0:HT], bk[:, h:h + 1], qa[:, h, :, :].rearrange("p b t -> p (b t)"),
                              start=True, stop=True).then_inc(s_cp, 1)
            pe.wait_ge(s_ce, 2 * HEADS)

            pe.wait_ge(s_wk, 16)
            tb, zb = rings()
            for s in s_zread:
                pe.sem_inc(s, 1)

            def apart():
                pe.sem_inc(s_apart, 1)

            def run(b, events):
                for what, k in events:
                    if what == "T":
                        if k == 0:
                            pe.wait_ge(s_ln, b + 1)
                            pe.wait_ge(s_lat, b * 16 + 16)
                        tb.free(pe)
                        t, _, _ = tb.take()
                        r = tcols(k)[1]
                        if r < P:
                            apart()
                        for c in range(ND):
                            last = pe.transpose(t[:, c * P:c * P + r], raw[0:r, k, c * P:(c + 1) * P], ident[0:r, 0:r])
                        last.then_inc(s_tb, 1)
                    elif what == "Q":
                        dc, hg = k // 2, k % 2
                        if k == 0:
                            pe.wait_ge(s_qb, b * 16 + 16)
                        if k >= 4:
                            pe.wait_ge(s_qread, b * 2 * ND + k - 3)
                        elif not isinstance(b, int) or b > 0:
                            pe.wait_ge(s_exp, b * RT - (k < 2))
                        for hh in range(4):
                            h = hg * 4 + hh
                            last = pe.matmul(qbank[k % 4][:, hh * T:(hh + 1) * T], wk[:, h, dc * P:(dc + 1) * P],
                                             qb[:, h * T:(h + 1) * T], start=True, stop=True)
                        last.then_inc(s_qk, 1)
                    elif what == "S":
                        if k == 0:
                            tb.all_read(pe)
                            pe.wait_ge(s_qread, (b + 1) * 2 * ND)
                        elif k >= 2:
                            pe.wait_ge(s_exp, b * RT + k - 1)
                        at = 0
                        for half in range(2):
                            last = split_products(
                                pe, s_pair[k % 2][half][:, 0:SH[half]],
                                [((qt_h[:, c, k * P:(k + 1) * P], qt_l[:, c, k * P:(k + 1) * P]),
                                  (xt_h[:, c, at:at + SH[half]], xt_l[:, c, at:at + SH[half]])) for c in range(ND)],
                                True, True)
                            at += SH[half]
                        last.then_inc(s_s, 1)
                    elif what == "PT":
                        pe.wait_ge(s_p, b * RT + k + 1)
                        r = rows_of(k)
                        for chunks in (range(0, 4), range(4, KC)):
                            tb.free(pe)
                            t, _, _ = tb.take()
                            if r < P:
                                apart()
                            for n, c in enumerate(chunks):
                                last = pe.transpose(t[:, n * P:n * P + r], pr[k % 3][0:r, c * P:(c + 1) * P],
                                                    ident[0:r, 0:r])
                            last.then_inc(s_tb, 1)
                    elif what == "Z":
                        g, dc = k
                        if k == (0, 0):
                            pe.wait_ge(s_xnl, b * KC + KC)
                        if dc == 0:
                            tb.all_read(pe)
                        w = sum(rows_of(i) for i in GROUPS[g])
                        zb.free(pe)
                        z, _, _ = zb.take()
                        split_products(
                            pe, z[:, 0:w],
                            [((xn_h[:, c, dc * P:(dc + 1) * P], xn_l[:, c, dc * P:(dc + 1) * P]),
                              (pt_h[:, c, 0:w], pt_l[:, c, 0:w])) for c in range(KC)],
                            True, True).then_inc(s_zb, 1)
                    elif what == "V":
                        lo = GROUPS[k][0] * P
                        zb.all_read(pe)
                        z, _, _ = zb.take()
                        for h, c0, c1 in segments(GROUPS[k]):
                            for dc in range(ND):
                                last = pe.matmul(z[:, c0 - lo:c1 - lo], wv[:, dc, h * P:(h + 1) * P],
                                                 zt[:, dc, c0 - lo:c1 - lo], start=dc == 0, stop=dc == ND - 1)
                        last.then_inc(s_zb, 1)
                    elif what == "Y":
                        zb.all_read(pe)
                        z, _, _ = zb.take()
                        for h in range(HEADS):
                            last = pe.matmul(z[0:T, :], ot[:, h * T:(h + 1) * T], wo[:, h, :],
                                             start=h == 0, stop=h == HEADS - 1)
                        last.then_inc(s_zb, 1)
                    elif what == "R" and k == 2:
                        pe.wait_ge(s_x3, b + 1)
                        tb.free(pe)
                        t, _, _ = tb.take()
                        for c in range(ND):
                            last = pe.transpose(t[:, c * T:(c + 1) * T], x3b[0:T, c * P:(c + 1) * P],
                                                ident[0:T, 0:T])
                        last.then_inc(s_tb, 1)
                    elif what == "R" and k == 3:
                        pe.wait_ge(s_x3t, b + 1)
                        t = tb.banks[(tb.n - 1) % 2]
                        for c in range(ND):
                            last = pe.matmul(t[0:T, ND * T:ND * T + E], x3t[:, c, :], wr[:, c, :],
                                             start=c == 0, stop=c == ND - 1)
                        last.then_inc(s_lp, 1)

            def batch(b, events):
                tb.at(b, TB_USES, TB0)
                zb.at(b, ZB_USES, 0)
                steps(run, b, events)

            run(0, first)
            pe.wait_ge(s_wb, 16 * N_WB)
            batches(pe, batch)
            run(B, [("R", 2), ("R", 3)])

            pe.wait_ge(s_cc, 16 * N_CC)
            pe.wait_ge(s_oh, 1)
            ohf = oh[0:T, :, :].rearrange("p b e -> p (b e)")
            pe.matmul(bank[0][0:T, 0:B * E], before[0:T, 0:T], ohf, start=True, stop=True)
            pe.matmul(bank[1][:, 0:B * E].rearrange("p (e b) -> p e b", e=E), ones[0:T, :],
                      oh[0:T, :, :].rearrange("p b e -> p e b"), start=True, stop=True).then_inc(s_rk, 1)
            pe.wait_ge(s_ohv, 1)
            for b in range(B):
                last = pe.matmul(bank[2][:, 0:4 * NSLOT], ohp[0:T, b, :],
                                 ohv[0:T, b, :, :].rearrange("p v s -> p (v s)"),
                                 start=b == 0, stop=b == B - 1)
            last.then_inc(s_tp, 1)

            def tokens(n):
                pe.wait_ge(s_x3g, n + 1)
                for c in range(ND):
                    last = pe.transpose(bank[4][:, c * P:(c + 1) * P], x3g[:, c * P:(c + 1) * P], ident[:])
                last.then_inc(s_xtp, 1)

            def slot(n, e, last):
                for what, k in slot_plan:
                    if what == "X":
                        tokens(n + 1)
                    elif what == "M":
                        q = piece_of[(1, k)]
                        if k == 0:
                            pe.wait_ge(s_xtl, n + 1)
                        pe.wait_ge(s_wl, e * NW + q + 1)
                        if k >= 2:
                            pe.wait_ge(s_gelu, n * NF + k - 1)
                        split_products(
                            pe, bank[k % 2][:],
                            [((xg_h[:, c, :], xg_l[:, c, :]), (wsh[q][:, c, :], wsl[q][:, c, :]))
                             for c in range(ND)], True, True).then_inc(s_hp, 1)
                    elif what == "H":
                        pe.wait_ge(s_gelu, n * NF + k + 1)
                        for c in range(4):
                            last = pe.transpose(bank[2 + k % 2][:, c * P:(c + 1) * P],
                                                hid[k % 2][:, c * P:(c + 1) * P], ident[:])
                        last.then_inc(s_htp, 1)
                    elif what == "O":
                        q = piece_of[(2, k)]
                        pe.wait_ge(s_htl, n * NF + k + 1)
                        pe.wait_ge(s_wl, e * NW + q + 1)
                        if k == 0:
                            pe.wait_ge(s_yo, n + 1)
                        last = split_products(
                            pe, bank[6][:],
                            [((ht_h[k % 2][:, c, :], ht_l[k % 2][:, c, :]),
                              (wsh[q][:, c, :], wsl[q][:, c, :])) for c in range(4)], k == 0, k == NF - 1)
                        last.then_inc(s_yp, 1)

            tokens(0)
            slots(pe, slot)

        @block.scalar
        def _(act):
            def high_weight(k):
                act.wait_ge((s_w3 + [s_wq, s_wq])[k], 16)
                act.copy(weights_a(k, w3_h, wq_h), weights_a(k, w3, wq)).then_inc(s_wah, 1)

            high_weight(0)
            high_weight(1)
            for b in range(B):
                act.wait_ge(s_tpa, b + 1)
                act.copy(xa_h[:, :, b * T:(b + 1) * T], bank[b][:, 0:ND * T].rearrange("p (c t) -> p c t", c=ND)
                         ).then_inc(s_tha, 1)
            high_weight(2)
            act.wait_ge(s_ca, 16 * N_CA)
            n = 0
            for e in range(ND):
                if e >= 2:
                    act.wait_ge(s_hsc, e - 1)
                for w, dst in enumerate((ug, gg)):
                    for half in range(2):
                        act.wait_ge(s_ugp, n + 1)
                        act.activation(dst[e % 2][:, half * HT:(half + 1) * HT], bank[n % 4][:, 0:HT],
                                       (ACT.Identity, ACT.Sigmoid)[w], bias=ab[:, w, e:e + 1]).then_inc(s_ugs, 1)
                        n += 1
                act.wait_ge(s_hsc, e + 1)
                if e == 0:
                    act.wait_ge(s_xr, B)
                act.copy(hs_h[:, e, :], hs[:, e, :]).then_inc(s_hsh, 1)
                if e < 2:
                    high_weight(3 + e)
            act.wait_ge(s_bqs, 1)
            act.wait_ge(s_hsl, ND)

            def latents(half):
                for b in range(half * HALF, (half + 1) * HALF):
                    act.wait_ge(s_tpl, b + 1)
                    act.copy(xa_h[:, :, b * T:(b + 1) * T],
                             tbank[b % 2][:, 0:ND * T].rearrange("p (c t) -> p c t", c=ND)
                             ).then_inc(s_tha, 1)

            latents(0)
            for half in range(2):
                for h in range(HEADS):
                    n = half * HEADS + h
                    act.wait_ge(s_qp, n + 1)
                    if half and not h:
                        act.wait_ge(s_qout[0], 16 * HALF)
                        act.wait_ge(s_cout, 16 * HALF)
                    act.activation(qa[:, h, :, :].rearrange("p b t -> p (b t)"), bank[n % 4][:, 0:HT], ACT.Identity,
                                   bias=bqs[:, h:h + 1], scale=float(DH) ** -0.5).then_inc(s_qe, 1)
                if not half:
                    latents(1)
                for h in range(HEADS):
                    n = half * HEADS + h
                    act.wait_ge(s_cp, n + 1)
                    act.copy(crow[0:1, h, :, :].rearrange("p b t -> p (b t)"), zbank[n % 2][0:1, 0:HT]
                             ).then_inc(s_ce, 1)

            act.wait_ge(s_out_a, 16 * B)
            act.wait_ge(s_lnout, 16 * B)
            tb, zb = rings()

            def run(b, events):
                for what, k in events:
                    if what == "T":
                        t, _, n = tb.take()
                        act.wait_ge(s_tb, n)
                        c0, w = tcols(k)
                        act.copy(xt_h[:, :, c0:c0 + w], t[:].rearrange("p (c n) -> p c n", c=ND)[:, :, 0:w]
                                 ).then_inc(s_hi, 1)
                    elif what == "X":
                        act.copy(xn_h[:, k, :], raw[:, k, :]).then_inc(s_xnh, 1)
                    elif what == "Q":
                        dc, hg = k // 2, k % 2
                        act.wait_ge(s_qk, b * 2 * ND + k + 1)
                        act.copy(qt_h[:, dc, hg * 4 * T:(hg + 1) * 4 * T], qbank[k % 4][:, 0:4 * T]).then_inc(s_hi, 1)
                    elif what == "S":
                        if k == 0:
                            act.wait_ge(s_padp, 1)
                        act.wait_ge(s_nb, b * RT + k + 1)
                        p, (s0, s1) = pr[k % 3], s_pair[k % 2]
                        nb = smx[:, 4 + k % 2:5 + k % 2]
                        cut = MEDIA - SH[0]
                        r = rsm[:, 4 * (k % 2):4 * (k % 2) + 3]
                        act.activation(p[:, 0:SH[0]], s0[:, 0:SH[0]], ACT.Exp, bias=nb, accum_out=r[:, 0:1])
                        act.activation(p[:, SH[0]:MEDIA], s1[:, 0:cut], ACT.Exp, bias=nb, accum_out=r[:, 1:2])
                        act.activation(p[:, MC * P:MC * P + T], s1[:, cut:SH[1]], ACT.Exp, bias=nb,
                                       accum_out=r[:, 2:3]).then_inc(s_exp, 1)
                    elif what == "PT":
                        r = rows_of(k)
                        g = [g for g in GROUPS if k in g][0]
                        col = (k - g[0]) * P
                        for chunks in (range(0, 4), range(4, KC)):
                            t, _, u = tb.take()
                            act.wait_ge(s_tb, u)
                            n = len(chunks)
                            act.copy(pt_h[:, chunks[0]:chunks[0] + n, col:col + r],
                                     t[:, 0:n * P].rearrange("p (c q) -> p c q", c=n)[:, :, 0:r]).then_inc(s_hi, 1)
                    elif what == "Z":
                        g, dc = k
                        w = sum(rows_of(i) for i in GROUPS[g])
                        z, read, n = zb.take()
                        act.wait_ge(s_zb, n)
                        act.copy(zt[:, dc, 0:w], z[:, 0:w]).then_inc(read, 1)
                    elif what in ("V", "Y"):
                        zb.take()
                    elif what == "R" and k == 2:
                        t, _, n = tb.take()
                        act.wait_ge(s_tb, n)
                        act.copy(x3t[:], t[:, 0:ND * T].rearrange("p (c t) -> p c t", c=ND)).then_inc(s_x3t, 1)

            def batch(b, events):
                tb.at(b, TB_USES, TB0)
                zb.at(b, ZB_USES, 0)
                steps(run, b, events)

            run(0, first)
            batches(act, batch)
            def high_weights(e, q):
                act.wait_ge(s_w[q % 4], e * 32 + 16 * (q // 4) + 16)
                act.copy(wsh[q][:], stage[q % 4][:]).then_inc(s_wh, 1)

            def tokens(n):
                act.wait_ge(s_xtp, n + 1)
                act.copy(xg_h[:], bank[4][:].rearrange("p (c t) -> p c t", c=ND)).then_inc(s_xth, 1)

            def slot(n, e, last):
                for what, k in slot_plan:
                    if what == "W":
                        if last and e is not last_expert:
                            which, f = pieces[k]
                            act.wait_ge((s_hp, s_yp)[which - 1], n * NF + f + 1)
                            high_weights(e + 1, k)
                    elif what == "X":
                        tokens(n + 1)
                    elif what == "M":
                        act.wait_ge(s_hp, n * NF + k + 1)
                        act.activation(hid[k % 2][:], bank[k % 2][:], ACT.Gelu).then_inc(s_gelu, 1)
                    elif what == "H":
                        act.wait_ge(s_htp, n * NF + k + 1)
                        act.copy(ht_h[k % 2][:], bank[2 + k % 2][:].rearrange("p (c t) -> p c t", c=4)
                                 ).then_inc(s_hth, 1)

            for q in range(4):
                high_weights(0, q)
            run(B, [("R", 2)])
            act.wait_ge(s_lm, 1)
            act.activation(vals[0:T, :, 3], lmx[0:T, :], ACT.Sigmoid).then_inc(s_gate, 1)
            for q in range(4, NW):
                high_weights(0, q)
            tokens(0)
            slots(act, slot)

        @block.vector
        def _(dve):
            ch = Chain(dve, s_dve)

            def stats(st, mv, src):
                ch.add(dve.bn_stats(st, src))
                ch.join()
                return ch.add(dve.bn_aggr(mv, st))

            def tally(s):
                ch.join()
                dve.sem_inc(s, 1)

            def rows_stats(turn):
                dve.wait_ge(s_raw, turn * 32 + 32)
                for c in range(MC):
                    r = MLAST if c == MC - 1 else P
                    ch.add(dve.bn_stats(str_[0:r, c, :], raw[0:r, c, :]))
                ch.join()
                dve.sem_inc(s_apart, 1)
                for c in range(MC):
                    r = MLAST if c == MC - 1 else P
                    ch.add(dve.bn_aggr(mvr[0:r, c, :], str_[0:r, c, :]))
                tally(s_mvr)

            def rows_norm(turn):
                dve.wait_ge(s_rsr, turn + 1)
                for c in range(MC):
                    r = MLAST if c == MC - 1 else P
                    dve.tensor_scalar(raw[0:r, c, :], raw[0:r, c, :], mvr[0:r, c, 0:1], rsr[0:r, c:c + 1],
                                      ALU.subtract, ALU.mult).then_inc(s_apr, 1)

            def low(dst, src, high):
                return dve.tensor_tensor(dst, src, high.bitcast(F32), ALU.subtract)

            def low_weight(k):
                dve.wait_ge(s_wah, k + 1)
                low(w3_l[k][:], w3[k][:], w3_h[k][:]).then_inc(s_wal, 1)

            def low_rows(b, n, src, done):
                dve.wait_ge(s_tha, n + 1)
                part = (slice(None), slice(None), slice(b * T, (b + 1) * T))
                low(xa_l[part], src[:, 0:ND * T].rearrange("p (c t) -> p c t", c=ND), xa_h[part]
                    ).then_inc(done, 1)

            ch.add(dve.memset(mvr[:], 0.0))
            ch.join()
            for b in range(B):
                dve.wait_ge(s_x[b], 16)
                ch.add(dve.bn_stats(sta[0:T, b, :], xin[0:T, b, :]))
            ch.join()
            for b in range(B):
                ch.add(dve.bn_aggr(mva[0:T, 0, b, :], sta[0:T, b, :]))
            tally(s_mva)
            dve.wait_ge(s_rsa, 1)
            for b in range(B):
                dve.tensor_scalar(xh[0:T, b, :], xin[0:T, b, :], mva[0:T, 0, b, 0:1], rsa[0:T, 0, b:b + 1],
                                  ALU.subtract, ALU.mult).then_inc(s_xha, 1)
            for b in range(B):
                low_rows(b, b, bank[b], s_tea)
            low_weight(1)
            dve.wait_ge(s_ca, 16 * N_CA)
            ch.add(dve.tensor_scalar(bqs[:], bq[:], float(DH) ** -0.5, None, ALU.mult))
            tally(s_bqs)
            for e in range(ND):
                g, u = gg[e % 2], ug[e % 2]
                dve.wait_ge(s_ugs, 4 * e + 4)
                ch.add(dve.tensor_scalar(og[:], g[:], -1.0, 1.0, ALU.mult, ALU.add))
                ch.join()
                ch.add(dve.tensor_tensor(u[:], u[:], og[:], ALU.mult))
                ch.add(dve.memset(g[:].rearrange("p (b t) -> p b t", b=B)[:, :, 0:1], 0.0))
                ch.join()
                dve.tensor_tensor_scan(hs[:, e, :], g[:], u[:], 0.0, ALU.mult, ALU.add).then_inc(s_hsc, 1)
                dve.wait_ge(s_hsh, e + 1)
                low(hs_l[:, e, :], hs[:, e, :], hs_h[:, e, :]).then_inc(s_hsl, 1)
                if e < 2:
                    (rows_stats, rows_norm)[e](0)
            for what, g in norms:
                bs = range(2 * g, 2 * g + 2)
                if what == "A":
                    for b in bs:
                        dve.wait_ge(s_op, b + 1)
                        dve.wait_ge(s_xr, b + 1)
                        ch.add(dve.tensor_tensor(xin[0:T, b, :], obank[b][0:T, :], xin[0:T, b, :], ALU.add))
                        ch.join()
                        dve.sem_inc(s_x1, 1)
                        ch.add(dve.bn_stats(sta[0:T, b, :], xin[0:T, b, :]))
                    ch.join()
                    for b in bs:
                        ch.add(dve.bn_aggr(mva[0:T, 1, b, :], sta[0:T, b, :]))
                    tally(s_mva)
                elif what == "B":
                    dve.wait_ge(s_rsa, stds.index(("A", g)) + 2)
                    for b in bs:
                        ch.add(dve.tensor_scalar(xh[0:T, b, :], xin[0:T, b, :], mva[0:T, 1, b, 0:1],
                                                 rsa[0:T, 1, b:b + 1], ALU.subtract, ALU.mult))
                    ch.join()
                    for b in bs:
                        ch.add(dve.bn_stats(sta[0:T, b, :], xh[0:T, b, :]))
                    ch.join()
                    for b in bs:
                        ch.add(dve.bn_aggr(mva[0:T, 2, b, :], sta[0:T, b, :]))
                    tally(s_mva)
                elif what == "C":
                    dve.wait_ge(s_rsa, stds.index(("B", g)) + 2)
                    for b in bs:
                        ch.add(dve.scalar_tensor_tensor(xh[0:T, b, :], xh[0:T, b, :], mva[0:T, 2, b, 0:1], gl[0:T, :],
                                                        ALU.subtract, ALU.mult))
                    ch.join()
                    for b in bs:
                        dve.scalar_tensor_tensor(xh[0:T, b, :], xh[0:T, b, :], rsa[0:T, 2, b:b + 1], bl[0:T, :],
                                                 ALU.mult, ALU.add).then_inc(s_lnr, 1)
                elif what == "H":
                    low_rows(g, B + g, tbank[g % 2], s_tel)

            dve.wait_ge(s_qe, 2 * HEADS)
            ch.add(dve.memset(x2b[:], 0.0))
            ch.add(dve.memset(cqn[:], 0.0))
            ch.add(dve.memset(qt_h[:, :, ROWS:RT * P].bitcast(F32), 0.0))
            ch.add(dve.memset(qt_l[:, :, ROWS:RT * P].bitcast(F32), 0.0))
            tally(s_padq)

            tb, zb = rings()
            hi = [0, 0]

            def high_part():
                hi[0] += 1
                dve.wait_ge(s_hi, hi[1] * HI_USES + hi[0])

            def low_weights(e, q):
                dve.wait_ge(s_wh, e * NW + q + 1)
                low(wsl[q][:], stage[q % 4][:], wsh[q][:]).then_inc(s_wl, 1)

            def run(b, events):
                for what, k in events:
                    if what == "T":
                        t, read, _ = tb.take()
                        high_part()
                        c0, w = tcols(k)
                        low(xt_l[:, :, c0:c0 + w], t[:].rearrange("p (c n) -> p c n", c=ND)[:, :, 0:w],
                            xt_h[:, :, c0:c0 + w]).then_inc(read, 1)
                    elif what == "Q":
                        dc, hg = k // 2, k % 2
                        high_part()
                        cols = slice(hg * 4 * T, (hg + 1) * 4 * T)
                        low(qt_l[:, dc, cols], qbank[k % 4][:, 0:4 * T], qt_h[:, dc, cols]).then_inc(s_qread, 1)
                        if k == 2 * ND - 1:
                            dve.sem_inc(s_qbfree, 1)
                            dve.wait_ge(s_cq, b * 32 + 32)
                            ch.add(dve.tensor_copy(cq[:], cqn[:]))
                            tally(s_cqfree)
                    elif what == "S":
                        dve.wait_ge(s_s, b * RT + k + 1)
                        s0, s1 = s_pair[k % 2]
                        ch.add(dve.reduce_max(smx[:, 0:1], s0[:, 0:SH[0]], AX))
                        ch.add(dve.reduce_max(smx[:, 1:2], s1[:, 0:SH[1]], AX))
                        ch.join()
                        c = cq[:, k:k + 1]
                        ch.add(dve.scalar_tensor_tensor(smx[:, 2:3], smx[:, 0:1], smx[:, 1:2], c, ALU.max, ALU.add))
                        ch.join()
                        dve.tensor_tensor(smx[:, 4 + k % 2:5 + k % 2], c, smx[:, 2:3], ALU.subtract
                                          ).then_inc(s_nb, 1)
                    elif what == "N":
                        dve.wait_ge(s_exp, b * RT + k + 1)
                        o = 4 * (k % 2)
                        ch.add(dve.reduce_sum(rsm[:, o + 3:o + 4], rsm[:, o:o + 3], AX))
                        ch.join()
                        ch.add(dve.reciprocal(rsm[:, o + 3:o + 4], rsm[:, o + 3:o + 4]))
                        ch.join()
                        dve.tensor_scalar(pr[k % 3][:], pr[k % 3][:], rsm[:, o + 3:o + 4], None, ALU.mult
                                          ).then_inc(s_p, 1)
                    elif what == "PT":
                        r = rows_of(k)
                        g = [g for g in GROUPS if k in g][0]
                        col = (k - g[0]) * P
                        for chunks in (range(0, 4), range(4, KC)):
                            t, read, _ = tb.take()
                            high_part()
                            n = len(chunks)
                            part = (slice(None), slice(chunks[0], chunks[0] + n), slice(col, col + r))
                            low(pt_l[part], t[:, 0:n * P].rearrange("p (c q) -> p c q", c=n)[:, :, 0:r],
                                pt_h[part]).then_inc(read, 1)
                    elif what == "Z":
                        zb.take()
                    elif what == "V":
                        lo = GROUPS[k][0] * P
                        z, read, n = zb.take()
                        dve.wait_ge(s_zb, n)
                        for h, c0, c1 in segments(GROUPS[k]):
                            last = dve.tensor_scalar(ot[:, c0:c1], z[:, c0 - lo:c1 - lo],
                                                     bv[:, h:h + 1], None, ALU.add)
                        last.then_inc(read, 1)
                        if k == 2 and isinstance(b, int):
                            dve.sem_inc(s_vused, 1)
                    elif what == "Y":
                        z, read, n = zb.take()
                        if isinstance(b, int):
                            low_weights(0, 0)
                            low_weights(0, 1)
                        dve.wait_ge(s_zb, n)
                        dve.wait_ge(s_x1l, b * 16 + 16)
                        dve.wait_ge(s_x2out, b * 16 + 16)
                        ch.add(dve.tensor_tensor(x2b[0:T, :], z[0:T, :], x1b[0:T, :], ALU.add))
                        ch.join()
                        dve.sem_inc(read, 1)
                        dve.sem_inc(s_x2, 1)
                    elif what == "L":
                        (rows_stats, rows_norm)[k](b)
                    elif what == "R" and k == 0:
                        ch.add(dve.bn_stats(stx[0:T, :], x2b[0:T, :]))
                        ch.join()
                        dve.sem_inc(s_apart, 1)
                        ch.add(dve.bn_aggr(mvx[0:T, :], stx[0:T, :]))
                        ch.join()
                        ch.add(dve.tensor_copy(rbuf[0:T, 0:1], mvx[0:T, 0:1]))
                        ch.add(dve.tensor_copy(rsx[0:T, 0:1], mvx[0:T, 1:2]))
                        tally(s_mvx)
                    elif what == "R" and k == 1:
                        dve.wait_ge(s_rsx, b + 1)
                        ch.add(dve.tensor_scalar(x3b[0:T, :], x2b[0:T, :], rbuf[0:T, 0:1], rbuf[0:T, 1:2],
                                                 ALU.subtract, ALU.mult))
                        tally(s_x3)
                    elif what == "R" and k == 2:
                        router_bank[0] = tb.take()
                    elif what == "R" and k == 3:
                        t, read, _ = router_bank[0]
                        dve.wait_ge(s_lp, b + 1)
                        ch.add(dve.tensor_tensor(rbuf[0:T, 2:NREC], t[0:T, ND * T:ND * T + E], brb[0:T, :], ALU.add))
                        ch.join()
                        dve.sem_inc(read, 1)
                        ch.add(dve.tensor_copy(rec[0:T, bass.ds(b, 1), :], rbuf[0:T, :].unsqueeze(1)))

            router_bank = [None]

            def batch(b, events):
                tb.at(b, TB_USES, TB0)
                zb.at(b, ZB_USES, 0)
                hi[0], hi[1] = HI0, b
                steps(run, b, events)

            split_at = first.index(("S", 0))
            run(0, first[:split_at])
            dve.wait_ge(s_qout[1], 16 * HALF)
            for k in range(3):
                ch.add(dve.memset(pr[k][:], 0.0))
            tally(s_padp)
            run(0, first[split_at:])
            batches(dve, batch, ch, DVE_B)

            run(B, [("R", k) for k in range(4)])
            ch.join()

            dve.wait_ge(s_x2out, 16 * (B + 1))
            t = slice(0, T)
            be = "p b e -> p (b e)"
            lg = rec[t, 1:B + 1, 2:NREC]
            ch.add(dve.reduce_max(lmx[t, :], lg, AX))
            tally(s_lm)
            ch.add(dve.tensor_tensor(eq[t], lg, lmx[t].unsqueeze(2).broadcast_to([T, B, E]), ALU.is_ge))
            ch.join()
            ch.add(dve.tensor_tensor(eq[t].rearrange(be), eq[t].rearrange(be), desc[t].rearrange(be), ALU.mult))
            ch.join()
            ch.add(dve.reduce_max(kmx[t, :], eq[t], AX))
            ch.join()
            ch.add(dve.tensor_tensor(oh[t], desc[t], kmx[t].unsqueeze(2).broadcast_to([T, B, E]), ALU.is_equal))
            tally(s_oh)
            dve.wait_ge(s_rk, 1)
            ch.add(dve.tensor_tensor_scan(upto[:].rearrange("p e b -> p (e b)"), inner[:].rearrange("p e b -> p (e b)"),
                                          bank[1][:, 0:B * E], 0.0, ALU.mult, ALU.add))
            ch.join()
            ch.add(dve.tensor_tensor(tmp[t], bank[0][t, 0:B * E].rearrange("p (b e) -> p b e", e=E),
                                     upto[t].rearrange("p e b -> p b e"), ALU.add))
            ch.add(dve.tensor_tensor(cmp_[:], upto[:, :, B - 1].unsqueeze(1).broadcast_to([P, NOV, E]),
                                     sizes[:].unsqueeze(2).broadcast_to([P, NOV, E]), ALU.is_gt))
            ch.join()
            ch.add(dve.tensor_tensor(tmp[t], tmp[t], oh[t], ALU.mult))
            ch.add(dve.reduce_sum(ovc[:], cmp_[:].rearrange("p j e -> p e j"), AX))
            ch.join()
            ch.add(dve.reduce_sum(rank[t, :], tmp[t], AX))
            ch.join()
            ch.add(dve.tensor_tensor(cmr[t], rank[t].unsqueeze(1).broadcast_to([T, NOV, B]),
                                     sizes[t].unsqueeze(2).broadcast_to([T, NOV, B]), ALU.is_ge))
            ch.join()
            ch.add(dve.reduce_sum(jt[t, :], cmr[t].rearrange("p j b -> p b j"), AX))
            ch.add(dve.tensor_tensor_scan(ove[:], ones8[:], ovc[:], 0.0, ALU.mult, ALU.add))
            ch.join()
            ch.add(dve.tensor_tensor(ovb[:], ove[:], ovc[:], ALU.subtract))
            ch.add(dve.tensor_tensor(slot_of[:, 1, :], ove[:], eid[:, 0, :], ALU.add))
            ch.add(dve.scalar_tensor_tensor(pin[t, :], jt[t, :], -float(TILE), rank[t, :], ALU.mult, ALU.add))
            ch.join()
            ch.add(dve.tensor_tensor(slot_of[:, 0, :], ovb[:], eid[:, 0, :], ALU.add))
            ch.add(dve.tensor_tensor(ohp[t], iota[t].unsqueeze(1).broadcast_to([T, B, P]),
                                     pin[t].unsqueeze(2).broadcast_to([T, B, P]), ALU.is_equal))
            ch.join()
            ch.add(dve.tensor_tensor(tmp[t], oh[t], slot_of[t, 0:1, :].broadcast_to([T, B, E]), ALU.mult))
            ch.join()
            ch.add(dve.reduce_sum(pb[t, :], tmp[t], AX))
            ch.join()
            ch.add(dve.tensor_tensor(pb[t, :], pb[t, :], jt[t, :], ALU.add))
            ch.add(dve.tensor_copy(vals[t, :, 0], tokv[t, :]))
            ch.add(dve.tensor_copy(vals[t, :, 1:3], rec[t, 1:B + 1, 0:2]))
            ch.join()
            ch.add(dve.tensor_tensor(ohs[t], iota[t, 0:NSLOT].unsqueeze(1).broadcast_to([T, B, NSLOT]),
                                     pb[t].unsqueeze(2).broadcast_to([T, B, NSLOT]), ALU.is_equal))
            ch.join()
            dve.wait_ge(s_gate, 1)
            ch.add(dve.tensor_tensor(ohv[t], ohs[t].unsqueeze(2).broadcast_to([T, B, 4, NSLOT]),
                                     vals[t].unsqueeze(3).broadcast_to([T, B, 4, NSLOT]), ALU.mult))
            tally(s_ohv)
            ch.add(dve.tensor_copy(ctl[:], slot_of[:]))
            tally(s_ctl)
            dve.wait_ge(s_wlp, 2)
            dve.sem_inc(s_wl, 2)
            low_weights(0, 4)
            dve.wait_ge(s_tp, 1)
            ch.add(dve.tensor_scalar(idx[:], bank[2][:, 0:NSLOT], float(NTOK), None, ALU.add))
            tally(s_idx)
            ch.add(dve.tensor_copy(sm[:].rearrange("p s v -> p v s"),
                                   bank[2][:, 0:4 * NSLOT].rearrange("p (v s) -> p v s", v=4)))
            ch.join()

            dve.sem_inc(s_yo, 1)

            def norm_tokens(n):
                ch.add(dve.tensor_copy(cur[:], sm[:, bass.ds(n, 1), :].rearrange("p o v -> p (o v)")))
                ch.join()
                dve.wait_ge(s_gat, n * 16 + 16)
                ch.add(dve.tensor_scalar(x3g[:], gat[:], cur[:, 1:2], cur[:, 2:3], ALU.subtract, ALU.mult))
                tally(s_x3g)

            def keep_tokens(n):
                ch.add(dve.tensor_copy(x2g[:], gat[:]))
                ch.add(dve.tensor_copy(pg[:], cur[:, 3:4]))
                tally(s_gfree)

            def split_tokens(n):
                dve.wait_ge(s_xth, n + 1)
                low(xg_l[:], bank[4][:].rearrange("p (c t) -> p c t", c=ND), xg_h[:]).then_inc(s_xtl, 1)

            def slot(n, e, last):
                for what, k in slot_plan:
                    if what == "G":
                        dve.wait_ge(s_xtp, n + 1)
                        norm_tokens(n + 1)
                    elif what == "K":
                        dve.wait_ge(s_yo, n + 2)
                        keep_tokens(n + 1)
                    elif what == "W":
                        if last and e is not last_expert:
                            low_weights(e + 1, k)
                    elif what == "X":
                        split_tokens(n + 1)
                    elif what == "H":
                        dve.wait_ge(s_hth, n * NF + k + 1)
                        low(ht_l[k % 2][:], bank[2 + k % 2][:].rearrange("p (c t) -> p c t", c=4), ht_h[k % 2][:]
                            ).then_inc(s_htl, 1)
                    elif what == "R":
                        dve.wait_ge(s_yp, n * NF + NF)
                        dve.wait_ge(s_yofree, n + 1)
                        dve.scalar_tensor_tensor(yo[:], bank[6][:], pg[:], x2g[:], ALU.mult, ALU.add
                                                 ).then_inc(s_yo, 1)

            low_weights(0, 5)
            norm_tokens(0)
            keep_tokens(0)
            split_tokens(0)
            low_weights(0, 6)
            low_weights(0, 7)
            slots(dve, slot, ch, 4)


def kernel(**inputs):
    from concourse import bacc
    from concourse.bass_utils import run_bass_kernel_spmd

    src = {k: np.ascontiguousarray(v) for k, v in inputs.items()}
    t = np.ascontiguousarray
    arrays = {
        "x": src["x"], "ctx": src["ctx_1024"],
        "WiT": t(src["L0_attn_Wi"].T), "WgT": t(src["L0_attn_Wg"].T), "WoT": t(src["L0_attn_Wo"].T),
        "ab": t(np.stack([src["L0_attn_bi"], src["L0_attn_bg"]]).reshape(2, ND, P).transpose(2, 0, 1)),
        "bo_a": src["L0_attn_bo"],
        "gm": src["L0_xattn_gamma_media"], "bm": src["L0_xattn_beta_media"],
        "gl": src["L0_xattn_gamma_lat"], "bl": src["L0_xattn_beta_lat"],
        "Wq": src["L0_xattn_Wq"], "bq": t(src["L0_xattn_bq"].reshape(HEADS, P).T),
        "WkT": t(src["L0_xattn_Wkv"][:, :INNER].T), "Wv": t(src["L0_xattn_Wkv"][:, INNER:]),
        "bk": t(src["L0_xattn_bkv"][:INNER].reshape(HEADS, P).T),
        "bv": t(src["L0_xattn_bkv"][INNER:].reshape(HEADS, P).T), "Wo_x": src["L0_xattn_Wo"], "bo_x": src["L0_xattn_bo"],
        "Wr": src["L0_ffn_Wr"], "br": src["L0_ffn_br"], "W1": src["L0_ffn_W1"], "W2": src["L0_ffn_W2"],
        "ident": np.eye(P, dtype=np.float32),
        "phalf": np.full((P, 16), -0.5, np.float32),
        "desc": np.broadcast_to(np.arange(E, 0, -1, dtype=np.float32), (P, B, E)).copy(),
        "eid": np.broadcast_to(np.arange(E, dtype=np.float32), (P, B, E)).copy(),
        "tokv": np.arange(-NTOK, 0, dtype=np.float32).reshape(B, T).T.copy(),
        "before": np.triu(np.ones((P, P), np.float32), 1) - np.float32(1),
        "inner": np.broadcast_to((np.arange(B) > 0).astype(np.float32), (P, E, B)).copy(),
        "sizes": np.broadcast_to(TILE * np.arange(1, NOV + 1, dtype=np.float32), (P, NOV)).copy(),
        "ones": np.ones((P, P), np.float32),
        "iota": np.broadcast_to(np.arange(P, dtype=np.float32), (P, P)).copy(),
    }
    nc = bacc.Bacc("TRN2", target_bir_lowering=False, num_devices=1)
    aps, feed = {}, {}
    for name, arr in arrays.items():
        feed[f"in_{name}"] = arr
        aps[name] = nc.dram_tensor(f"in_{name}", arr.shape, mybir.dt.from_np(arr.dtype), kind="ExternalInput").ap()
    out = nc.dram_tensor("out", (B, T, D), F32, kind="ExternalOutput").ap()
    build(nc, aps, out.rearrange("b t d -> (b t) d"))
    result = run_bass_kernel_spmd(nc, [feed], core_ids=[0])
    return result.results[0]["out"]
```
